# Optimizing a Trainium2 kernel written in Bass

```python
import numpy as np
import jax
import jax.numpy as jnp

def _softmax(x, axis=-1):
    return jax.nn.softmax(x, axis=axis)

def _gelu(x):
    return jax.nn.gelu(x, approximate=True)

def _silu(x):
    return jax.nn.silu(x)

def _sigmoid(x):
    return jax.nn.sigmoid(x)

def _layernorm(x, axis=-1, eps=1e-05):
    m = jnp.mean(x, axis=axis, keepdims=True)
    v = jnp.var(x, axis=axis, keepdims=True)
    return (x - m) / jnp.sqrt(v + eps)

def _scatter_add(tgt, idx, src, axis=0):
    return tgt.at[idx].add(src)

def _segment_sum(src, seg, n):
    return jax.ops.segment_sum(src, seg, n)
kernel_name = 'mk_seq_preln_d2_jaxref_r8_51a267'

def setup_inputs(seed: int=0):
    np.random.seed(seed)
    _w = jnp.asarray

    def _L0_attn_setup():
        import math
        import jax, jax.numpy as jnp
        import numpy as np
        BLOCK = 64

        def build_slope_tensor(n_heads):

            def p2(n):
                start = 2.0 ** (-2.0 ** (-(math.log2(n) - 3)))
                return [start * start ** i for i in range(n)]
            if math.log2(n_heads).is_integer():
                s = p2(n_heads)
            else:
                closest = 2 ** math.floor(math.log2(n_heads))
                s = p2(closest) + p2(2 * closest)[0::2][:n_heads - closest]
            return jnp.asarray(np.array(s, dtype=np.float32))

        def lightning_attn(q, k, v, slopes, block=BLOCK):
            B, H, N, d = q.shape
            nc = N // block
            i = jnp.arange(block, dtype=q.dtype)
            diff = i[:, None] - i[None, :]
            intra_decay = jnp.where(diff >= 0, jnp.exp(-slopes[:, None, None] * diff), 0.0)
            q_decay = jnp.exp(-slopes[:, None] * i[None, :])
            k_decay = jnp.exp(-slopes[:, None] * (block - i[None, :]))
            blk_decay = jnp.exp(-slopes * block)

            def to_chunks(t):
                return t.reshape(B, H, nc, block, d).transpose(2, 0, 1, 3, 4)
            qc, kc, vc = (to_chunks(q), to_chunks(k), to_chunks(v))

            def body(S, xs):
                qb, kb, vb = xs
                scores = jnp.einsum('bhid,bhjd->bhij', qb, kb) * intra_decay[None]
                o_intra = jnp.einsum('bhij,bhjd->bhid', scores, vb)
                o_inter = jnp.einsum('bhid,bhde->bhie', qb * q_decay[None, :, :, None], S)
                S_new = blk_decay[None, :, None, None] * S + jnp.einsum('bhjd,bhje->bhde', kb * k_decay[None, :, :, None], vb)
                return (S_new, o_intra + o_inter)
            S0 = jnp.zeros((B, H, d, d), dtype=q.dtype)
            _, o = jax.lax.scan(body, S0, (qc, kc, vc))
            return o.transpose(1, 2, 0, 3, 4).reshape(B, H, N, d)
        key = jax.random.key(seed)
        k1, k2, k3 = jax.random.split(key, 3)
        dim, num_heads = (256, 16)
        B, N = (2, 512)
        x = jax.random.normal(k1, (B, N, dim), dtype=jnp.float32)
        Wqkv = jax.random.normal(k2, (dim, 3 * dim), dtype=jnp.float32) / math.sqrt(dim)
        bqkv = jnp.zeros((3 * dim,), dtype=jnp.float32)
        Wout = jax.random.normal(k3, (dim, dim), dtype=jnp.float32) / math.sqrt(dim)
        bout = jnp.zeros((dim,), dtype=jnp.float32)
        slopes = build_slope_tensor(num_heads)
        return {'x': x, 'Wqkv': Wqkv, 'bqkv': bqkv, 'Wout': Wout, 'bout': bout, 'slopes': slopes}
    _L0_attn_in = _L0_attn_setup()

    def _L0_ffn_setup():
        import jax, jax.numpy as jnp
        import numpy as np
        NUM_EXPERTS = 32
        TOP_K = 8
        THRESHOLD = 0.8
        HIDDEN = 256
        INTER = 96
        key = jax.random.key(seed)
        k1, k2, k3, k4 = jax.random.split(key, 4)
        hidden_states = jax.random.normal(k1, (2, 128, HIDDEN), jnp.float32)
        gate_weight = jax.random.normal(k2, (NUM_EXPERTS, HIDDEN), jnp.float32) * 0.02
        gate_up_proj = jax.random.normal(k3, (NUM_EXPERTS, 2 * INTER, HIDDEN), jnp.float32) * 0.02
        down_proj = jax.random.normal(k4, (NUM_EXPERTS, HIDDEN, INTER), jnp.float32) * 0.02
        return {'hidden_states': hidden_states, 'gate_weight': gate_weight, 'gate_up_proj': gate_up_proj, 'down_proj': down_proj}
    _L0_ffn_in = _L0_ffn_setup()

    def _L1_attn_setup():
        import jax, jax.numpy as jnp
        import numpy as np
        EPS = 1e-06
        ROPE_BASE = 10000.0

        def _rmsnorm(x, w):
            var = jnp.mean(x * x, axis=-1, keepdims=True)
            return x * jax.lax.rsqrt(var + EPS) * w

        def _rope(t):
            S, D = (t.shape[-2], t.shape[-1])
            inv_freq = 1.0 / ROPE_BASE ** (jnp.arange(0, D, 2, dtype=jnp.float32) / D)
            ang = jnp.arange(S, dtype=jnp.float32)[:, None] * inv_freq
            cos = jnp.concatenate([jnp.cos(ang), jnp.cos(ang)], axis=-1)
            sin = jnp.concatenate([jnp.sin(ang), jnp.sin(ang)], axis=-1)
            t1, t2 = jnp.split(t, 2, axis=-1)
            rot = jnp.concatenate([-t2, t1], axis=-1)
            return t * cos + rot * sin
        key = jax.random.key(seed)
        ks = jax.random.split(key, 9)
        B, S, H = (2, 256, 256)
        Hq, Hkv, D = (16, 4, 128)
        s = 0.02
        return {'x': jax.random.normal(ks[0], (B, S, H), jnp.float32), 'q_project': jax.random.normal(ks[1], (Hq * D, H), jnp.float32) * s, 'k_project': jax.random.normal(ks[2], (Hkv * D, H), jnp.float32) * s, 'v_project': jax.random.normal(ks[3], (Hkv * D, H), jnp.float32) * s, 'q_bias': jax.random.normal(ks[4], (Hq * D,), jnp.float32) * s, 'k_bias': jax.random.normal(ks[5], (Hkv * D,), jnp.float32) * s, 'v_bias': jax.random.normal(ks[6], (Hkv * D,), jnp.float32) * s, 'o_project': jax.random.normal(ks[7], (H, Hq * D), jnp.float32) * s, 'ln_weight': jnp.ones((H,), jnp.float32)}
    _L1_attn_in = _L1_attn_setup()

    def _L1_ffn_setup():
        import jax, jax.numpy as jnp
        import numpy as np
        H = 256
        I = 176
        E = 16
        K = 2
        SI = I * 2

        def _swiglu(gu, inter):
            g, u = (gu[..., :inter], gu[..., inter:])
            return jax.nn.silu(g) * u
        key = jax.random.key(seed)
        ks = jax.random.split(key, 6)
        s = 0.02
        hidden_states = jax.random.normal(ks[0], (1, 128, H), dtype=jnp.float32)
        gate_w = jax.random.normal(ks[1], (E, H), dtype=jnp.float32) * s
        w_gate_up = jax.random.normal(ks[2], (E, H, 2 * I), dtype=jnp.float32) * s
        w_down = jax.random.normal(ks[3], (E, I, H), dtype=jnp.float32) * s
        shared_gate_up = jax.random.normal(ks[4], (H, 2 * SI), dtype=jnp.float32) * s
        shared_down = jax.random.normal(ks[5], (SI, H), dtype=jnp.float32) * s
        return {'hidden_states': hidden_states, 'gate_w': gate_w, 'w_gate_up': w_gate_up, 'w_down': w_down, 'shared_gate_up': shared_gate_up, 'shared_down': shared_down}
    _L1_ffn_in = _L1_ffn_setup()
    _d = {'L0_attn_x': _L0_attn_in['x'], 'L0_attn_Wqkv': _L0_attn_in['Wqkv'], 'L0_attn_bqkv': _L0_attn_in['bqkv'], 'L0_attn_Wout': _L0_attn_in['Wout'], 'L0_attn_bout': _L0_attn_in['bout'], 'L0_attn_slopes': _L0_attn_in['slopes'], 'L0_ffn_gate_weight': _L0_ffn_in['gate_weight'], 'L0_ffn_gate_up_proj': _L0_ffn_in['gate_up_proj'], 'L0_ffn_down_proj': _L0_ffn_in['down_proj'], 'L1_attn_q_project': _L1_attn_in['q_project'], 'L1_attn_k_project': _L1_attn_in['k_project'], 'L1_attn_v_project': _L1_attn_in['v_project'], 'L1_attn_q_bias': _L1_attn_in['q_bias'], 'L1_attn_k_bias': _L1_attn_in['k_bias'], 'L1_attn_v_bias': _L1_attn_in['v_bias'], 'L1_attn_o_project': _L1_attn_in['o_project'], 'L1_attn_ln_weight': _L1_attn_in['ln_weight'], 'L1_ffn_gate_w': _L1_ffn_in['gate_w'], 'L1_ffn_w_gate_up': _L1_ffn_in['w_gate_up'], 'L1_ffn_w_down': _L1_ffn_in['w_down'], 'L1_ffn_shared_gate_up': _L1_ffn_in['shared_gate_up'], 'L1_ffn_shared_down': _L1_ffn_in['shared_down']}
    _x0 = _d['L0_attn_x']
    _d['L0_attn_x'] = jax.random.normal(jax.random.fold_in(jax.random.key(seed), 1), (16, 256, 256), dtype=_x0.dtype)
    del _x0
    return _d

def reference(L0_attn_x, L0_attn_Wqkv, L0_attn_bqkv, L0_attn_Wout, L0_attn_bout, L0_attn_slopes, L0_ffn_gate_weight, L0_ffn_gate_up_proj, L0_ffn_down_proj, L1_attn_q_project, L1_attn_k_project, L1_attn_v_project, L1_attn_q_bias, L1_attn_k_bias, L1_attn_v_bias, L1_attn_o_project, L1_attn_ln_weight, L1_ffn_gate_w, L1_ffn_w_gate_up, L1_ffn_w_down, L1_ffn_shared_gate_up, L1_ffn_shared_down):

    def _L0_attn_ref(x, Wqkv, bqkv, Wout, bout, slopes):
        import math
        import jax, jax.numpy as jnp
        import numpy as np
        BLOCK = 64

        def build_slope_tensor(n_heads):

            def p2(n):
                start = 2.0 ** (-2.0 ** (-(math.log2(n) - 3)))
                return [start * start ** i for i in range(n)]
            if math.log2(n_heads).is_integer():
                s = p2(n_heads)
            else:
                closest = 2 ** math.floor(math.log2(n_heads))
                s = p2(closest) + p2(2 * closest)[0::2][:n_heads - closest]
            return jnp.asarray(np.array(s, dtype=np.float32))

        def lightning_attn(q, k, v, slopes, block=BLOCK):
            B, H, N, d = q.shape
            nc = N // block
            i = jnp.arange(block, dtype=q.dtype)
            diff = i[:, None] - i[None, :]
            intra_decay = jnp.where(diff >= 0, jnp.exp(-slopes[:, None, None] * diff), 0.0)
            q_decay = jnp.exp(-slopes[:, None] * i[None, :])
            k_decay = jnp.exp(-slopes[:, None] * (block - i[None, :]))
            blk_decay = jnp.exp(-slopes * block)

            def to_chunks(t):
                return t.reshape(B, H, nc, block, d).transpose(2, 0, 1, 3, 4)
            qc, kc, vc = (to_chunks(q), to_chunks(k), to_chunks(v))

            def body(S, xs):
                qb, kb, vb = xs
                scores = jnp.einsum('bhid,bhjd->bhij', qb, kb) * intra_decay[None]
                o_intra = jnp.einsum('bhij,bhjd->bhid', scores, vb)
                o_inter = jnp.einsum('bhid,bhde->bhie', qb * q_decay[None, :, :, None], S)
                S_new = blk_decay[None, :, None, None] * S + jnp.einsum('bhjd,bhje->bhde', kb * k_decay[None, :, :, None], vb)
                return (S_new, o_intra + o_inter)
            S0 = jnp.zeros((B, H, d, d), dtype=q.dtype)
            _, o = jax.lax.scan(body, S0, (qc, kc, vc))
            return o.transpose(1, 2, 0, 3, 4).reshape(B, H, N, d)
        B, N, C = x.shape
        H = slopes.shape[0]
        hd = C // H
        qkv = (x @ Wqkv + bqkv).reshape(B, N, 3, H, hd)
        qkv = qkv.transpose(2, 0, 3, 1, 4)
        q, k, v = (qkv[0], qkv[1], qkv[2])
        attn = lightning_attn(q, k, v, slopes)
        out = attn.transpose(0, 2, 1, 3).reshape(B, N, C)
        return out @ Wout + bout

    def _L0_ffn_ref(hidden_states, gate_weight, gate_up_proj, down_proj):
        import jax, jax.numpy as jnp
        import numpy as np
        NUM_EXPERTS = 32
        TOP_K = 8
        THRESHOLD = 0.8
        HIDDEN = 256
        INTER = 96
        B, S, H = hidden_states.shape
        x = hidden_states.reshape(-1, H)
        logits = x @ gate_weight.T
        probs = jax.nn.softmax(logits.astype(jnp.float32), axis=-1).astype(logits.dtype)
        top_vals, top_idx = jax.lax.top_k(probs, TOP_K)
        renorm = top_vals / jnp.clip(jnp.sum(top_vals, axis=-1, keepdims=True), 1e-12)
        cum = jnp.cumsum(renorm, axis=-1)
        num_keep = jnp.minimum(jnp.sum((cum < THRESHOLD).astype(jnp.int32), axis=-1) + 1, TOP_K)
        active = jnp.arange(TOP_K)[None, :] < num_keep[:, None]
        rw = top_vals * active.astype(top_vals.dtype)
        rw = rw / jnp.clip(jnp.sum(rw, axis=-1, keepdims=True), 1e-12)
        combine = jnp.sum(jax.nn.one_hot(top_idx, NUM_EXPERTS, dtype=rw.dtype) * rw[..., None], axis=1)

        def body(acc, params):
            w_gu, w_d, ce = params
            gu = x @ w_gu.T
            g, u = jnp.split(gu, 2, axis=-1)
            h = jax.nn.silu(g) * u
            return (acc + h @ w_d.T * ce[:, None], None)
        out, _ = jax.lax.scan(body, jnp.zeros_like(x), (gate_up_proj, down_proj, combine.T))
        return out.reshape(B, S, H)

    def _L1_attn_ref(x, q_project, k_project, v_project, q_bias, k_bias, v_bias, o_project, ln_weight):
        import jax, jax.numpy as jnp
        import numpy as np
        EPS = 1e-06
        ROPE_BASE = 10000.0

        def _rmsnorm(x, w):
            var = jnp.mean(x * x, axis=-1, keepdims=True)
            return x * jax.lax.rsqrt(var + EPS) * w

        def _rope(t):
            S, D = (t.shape[-2], t.shape[-1])
            inv_freq = 1.0 / ROPE_BASE ** (jnp.arange(0, D, 2, dtype=jnp.float32) / D)
            ang = jnp.arange(S, dtype=jnp.float32)[:, None] * inv_freq
            cos = jnp.concatenate([jnp.cos(ang), jnp.cos(ang)], axis=-1)
            sin = jnp.concatenate([jnp.sin(ang), jnp.sin(ang)], axis=-1)
            t1, t2 = jnp.split(t, 2, axis=-1)
            rot = jnp.concatenate([-t2, t1], axis=-1)
            return t * cos + rot * sin
        B, S, _ = x.shape
        Hq, Hkv, D = (16, 4, 128)
        rep = Hq // Hkv
        h = _rmsnorm(x, ln_weight)
        q = h @ q_project.T + q_bias
        k = h @ k_project.T + k_bias
        v = h @ v_project.T + v_bias
        q = q.reshape(B, S, Hq, D).transpose(0, 2, 1, 3)
        k = k.reshape(B, S, Hkv, D).transpose(0, 2, 1, 3)
        v = v.reshape(B, S, Hkv, D).transpose(0, 2, 1, 3)
        q = _rope(q)
        k = _rope(k)
        qg = q.reshape(B, Hkv, rep, S, D)
        scale = jnp.float32(1.0) / jnp.sqrt(jnp.float32(D))
        scores = jnp.einsum('bgrqd,bgkd->bgrqk', qg, k) * scale
        mask = jnp.where(jnp.tril(jnp.ones((S, S), bool)), 0.0, -jnp.inf).astype(scores.dtype)
        attn = jax.nn.softmax(scores + mask, axis=-1)
        out = jnp.einsum('bgrqk,bgkd->bgrqd', attn, v)
        out = out.reshape(B, Hq, S, D).transpose(0, 2, 1, 3).reshape(B, S, Hq * D)
        return out @ o_project.T

    def _L1_ffn_ref(hidden_states, gate_w, w_gate_up, w_down, shared_gate_up, shared_down):
        import jax, jax.numpy as jnp
        import numpy as np
        H = 256
        I = 176
        E = 16
        K = 2
        SI = I * 2

        def _swiglu(gu, inter):
            g, u = (gu[..., :inter], gu[..., inter:])
            return jax.nn.silu(g) * u
        orig_shape = hidden_states.shape
        x = hidden_states.reshape(-1, H)
        logits = jnp.einsum('th,eh->te', x, gate_w)
        scores = jax.nn.softmax(logits, axis=-1)
        topk_w, topk_idx = jax.lax.top_k(scores, K)
        combine = jnp.sum(jax.nn.one_hot(topk_idx, E, dtype=x.dtype) * topk_w[..., None], axis=1)
        gu = jnp.einsum('th,ehj->etj', x, w_gate_up)
        h = _swiglu(gu, I)
        y = jnp.einsum('eti,eih,te->th', h, w_down, combine)
        gu_s = x @ shared_gate_up
        y = y + _swiglu(gu_s, SI) @ shared_down
        return y.reshape(orig_shape)
    x = L0_attn_x
    x = x + _L0_attn_ref(_layernorm(x, axis=-1), L0_attn_Wqkv, L0_attn_bqkv, L0_attn_Wout, L0_attn_bout, L0_attn_slopes)
    x = x + _L0_ffn_ref(_layernorm(x, axis=-1), L0_ffn_gate_weight, L0_ffn_gate_up_proj, L0_ffn_down_proj)
    x = x + _L1_attn_ref(_layernorm(x, axis=-1), L1_attn_q_project, L1_attn_k_project, L1_attn_v_project, L1_attn_q_bias, L1_attn_k_bias, L1_attn_v_bias, L1_attn_o_project, L1_attn_ln_weight)
    x = x + _L1_ffn_ref(_layernorm(x, axis=-1), L1_ffn_gate_w, L1_ffn_w_gate_up, L1_ffn_w_down, L1_ffn_shared_gate_up, L1_ffn_shared_down)
    return x

_drawn_inputs = setup_inputs


def setup_inputs(seed=0):
    import zlib

    import numpy as np

    out = dict(_drawn_inputs(seed))
    spreads = {'L0_attn_bqkv': (0.0, 0.1), 'L0_attn_bout': (0.0, 0.8), 'L1_attn_ln_weight': (1.0, 0.6)}
    factors = {'L0_ffn_gate_weight': 8.0,
     'L0_ffn_gate_up_proj': 8.0,
     'L0_ffn_down_proj': 8.0,
     'L1_attn_q_project': 8.0,
     'L1_attn_k_project': 8.0,
     'L1_attn_v_project': 8.0,
     'L1_attn_q_bias': 8.0,
     'L1_attn_k_bias': 8.0,
     'L1_attn_v_bias': 8.0,
     'L1_attn_o_project': 8.0,
     'L1_ffn_gate_w': 8.0,
     'L1_ffn_w_gate_up': 8.0,
     'L1_ffn_w_down': 8.0,
     'L1_ffn_shared_gate_up': 8.0,
     'L1_ffn_shared_down': 8.0}
    for name, (base, spread) in spreads.items():
        noise = np.random.default_rng([zlib.crc32(name.encode()), seed]).standard_normal(out[name].shape)
        drawn = base * np.exp(spread * noise) if base else spread * noise
        out[name] = jnp.asarray(drawn.astype(out[name].dtype))
    for name, factor in factors.items():
        out[name] = (out[name] * factor).astype(out[name].dtype)
    return out
```

```python
import concourse.bass as bass
from concourse import mybir
from contextlib import ExitStack

F32 = mybir.dt.float32
BF16 = mybir.dt.bfloat16
ALU = mybir.AluOpType
ACT = mybir.ActivationFunctionType
AX = mybir.AxisListType

P = 128
C = 256
KT = C // P
NT = 32
LN_EPS = 1e-5
RMS_EPS = 1e-6
BANK = 512

LA_HEADS, LA_HD = 16, 16
HQ, HKV, HD = 16, 4, 128
E0, I0, K0 = 32, 96, 8
E1, I1, K1, S1 = 16, 176, 2, 352
THRESHOLD = 0.8
NOT_KEPT = -5.0
MASKED = -1e30


class Chain:

    def __init__(self, eng, sem, per):
        self.eng, self.sem, self.per = eng, sem, per

    def start(self, step):
        self.base, self.n = step * self.per, 0

    def add(self, instruction):
        instruction.then_inc(self.sem, 1)
        self.n += 1

    def wait(self):
        self.eng.wait_ge(self.sem, self.base + self.n)

    def done(self):
        assert self.n == self.per, (self.n, self.per)


def move_x(sp, steps, tiles, src, dst, xin, xout, loaded, result_ready, results, stored):

    def load(step, buf):
        sp.dma_start(xin[:, buf], src[:, bass.ds(step * tiles, tiles), :]).then_inc(loaded[buf], 16)

    def store(step, buf):
        sp.wait_ge(result_ready, results * (step + 1) + 1)
        sp.dma_start(dst[:, bass.ds(step * tiles, tiles), :], xout[:, buf]).then_inc(stored, 16)

    sp.sem_inc(result_ready, 1)
    sp.sem_inc(stored, 16)
    load(0, 0)
    load(1, 1)
    with sp.Fori(0, steps // 2 - 1) as i:
        for u in range(2):
            store(2 * i + u, u)
            load(2 * i + u + 2, u)
    store(steps - 2, 0)
    load(0, 0)
    store(steps - 1, 1)
    sp.wait_ge(stored, 16 * (steps + 1))
    sp.wait_ge(loaded[0], 16 * (steps // 2 + 1))


def ffn_phase(nc, tag, banks, w, weights_loaded, weights_value, src, dst, experts, hidden, keep):
    T = 4
    TOK = T * P
    STEPS = NT // T
    NCH = -(-hidden // P)
    CR = 3 * experts + 1
    STATS, NORM, TR0, TR1, LOGITS = 0, 5, 7, 9, 11
    SHIFT, EXPS, PROBS, COMB, COMB_T = 12, 13, 14, 16, 20
    COPY0, COPY1, COPY_COMB = 8, 10, 21

    with ExitStack() as ctx:
        def sb(name, shape, dt=F32):
            return ctx.enter_context(nc.sbuf_tensor(f"{tag}_{name}", shape, dt))

        def sem(name):
            return ctx.enter_context(nc.semaphore(f"{tag}_{name}"))

        xin = sb("xin", [P, 2, T, C])
        xout = sb("xout", [P, 2, T, C])
        stats = sb("stats", [P, T, 6])
        mv = sb("mv", [P, T, 2])
        veps = sb("veps", [P, T])
        rstd = sb("rstd", [P, T])
        hn = sb("hn", [P, T, C])
        hT = sb("hT", [P, 2, KT, TOK])
        combT = sb("combT", [CR, 2, TOK], BF16)
        silu = sb("silu", [P, 2, TOK])
        gated = sb("gated", [P, 2, TOK])
        h = sb("h", [P, 2, TOK])
        mx = sb("mx", [P, T])
        shifted = sb("shifted", [P, T, experts])
        expd = sb("expd", [P, T, experts])
        rsum = sb("rsum", [P, T])
        probs = sb("probs", [P, T, experts + 8])
        top = sb("top", [P, T, 8])
        cum = sb("cum", [P, 2, T, 8])
        active = sb("active", [P, T, 8])
        kept = sb("kept", [P, T, 8])
        found = sb("found", [P, T, 8])
        tsum = sb("tsum", [P, T])
        replaced = sb("replaced", [P, T, experts + 8])
        chosen = sb("chosen", [P, T, experts])
        comb = sb("comb", [P, T, experts])
        rest = sb("rest", [P, T, experts])
        parts = sb("parts", [P, T, CR], BF16)

        gate_banks, up_banks, comb_bank, y_banks, misc = banks[0:2], banks[2:4], banks[4], banks[5:7], banks[7]

        loaded = [sem("x_loaded_0"), sem("x_loaded_1")]
        stored = sem("x_stored")
        var_ready = sem("var_ready")
        pool_chain = sem("pool_chain")
        rstd_ready = sem("rstd_ready")
        look = sem("lookahead_chain")
        hn_ready = sem("hn_ready")
        misc_ready = sem("misc_ready")
        misc_copied = sem("misc_copied")
        shifted_ready = sem("shifted_ready")
        exp_ready = sem("exp_ready")
        parts_ready = sem("parts_ready")
        gate_ready = sem("gate_ready")
        silu_ready = sem("silu_ready")
        up_ready = sem("up_ready")
        gated_ready = sem("gated_ready")
        comb_ready = sem("comb_ready")
        h_ready = sem("h_ready")
        h_used = sem("h_used")
        result_ready = sem("result_ready")
        const_ready = sem("const_ready")

        apart = sem("apart")

        block = ctx.enter_context(nc.Block())

        @block.sync
        def _(sp):
            move_x(sp, STEPS, T, src, dst, xin, xout, loaded, result_ready, 2, stored)

        @block.gpsimd
        def _(pool):
            def inverse_deviation(n):
                pool.wait_ge(var_ready, n + 1)
                pool.sem_inc(apart, 1)
                nc.gpsimd.tensor_scalar(veps[:], mv[:, :, 1], LN_EPS, None, ALU.add).then_inc(pool_chain, 1)
                pool.wait_ge(pool_chain, n + 1)
                nc.gpsimd.tensor_tensor(rstd[:], veps[:], w["minus_half"][:, 0:T], ALU.pow).then_inc(rstd_ready, 1)

            inverse_deviation(0)
            with pool.Fori(0, STEPS // 2) as i:
                for u in range(2):
                    inverse_deviation(2 * i + u + 1)

        @block.tensor
        def _(pe):
            def transposes(n, half):
                pe.wait_ge(hn_ready, T * n + 2 * half + 2)
                pe.wait_ge(misc_copied, 3 * n + half)
                out = misc[:].rearrange("p (k t) -> p k t", k=KT)
                for k in range(KT):
                    for j in range(2):
                        last = nc.tensor.transpose(out[:, k, j * P:(j + 1) * P], hn[:, 2 * half + j, k * P:(k + 1) * P],
                                                   w["ident"][:])
                last.then_inc(misc_ready, 1)

            def logits(n, b):
                pe.wait_ge(misc_copied, 3 * n + 2)
                for j in range(T):
                    for k in range(KT):
                        last = nc.tensor.matmul(misc[:, j * experts:(j + 1) * experts], hT[:, b, k, j * P:(j + 1) * P],
                                                w["router"][:, k, :], start=(k == 0), stop=(k == KT - 1))
                last.then_inc(misc_ready, 1)

            def transpose_parts(n):
                pe.wait_ge(shifted_ready, n + 1)
                pe.wait_ge(parts_ready, n + 1)
                pe.sem_inc(apart, 1)
                for j in range(T):
                    last = nc.tensor.transpose(misc[:].bitcast(BF16)[0:CR, j * P:(j + 1) * P], parts[:, j, :],
                                               w["ident_bf"][:])
                last.then_inc(misc_ready, 1)

            def gate_up(f, b, r, j):
                m = min(P, hidden - j * P)
                for banks_of, free, ready, wt in ((gate_banks, silu_ready, gate_ready, w["gate"]),
                                                  (up_banks, gated_ready, up_ready, w["up"])):
                    pe.wait_ge(free, f + 1)
                    for k in range(KT):
                        last = nc.tensor.matmul(banks_of[r][0:m], wt[:, k, j * P:j * P + m], hT[:, b, k, :],
                                                start=(k == 0), stop=(k == KT - 1))
                    last.then_inc(ready, 1)

            pe.sem_inc(silu_ready, 2)
            pe.sem_inc(gated_ready, 2)
            pe.sem_inc(h_used, 2)
            pe.sem_inc(h_ready, 1)
            pe.wait_ge(weights_loaded, weights_value)
            transposes(0, 0)
            transposes(0, 1)
            logits(0, 0)
            transpose_parts(0)
            gate_up(0, 0, 0, 0)
            with pe.Fori(0, STEPS // 2) as i:
                for u in range(2):
                    t = 2 * i + u
                    for j in range(NCH):
                        f, r = t * NCH + j, (u * NCH + j) % 2
                        m = min(P, hidden - j * P)
                        if j == 0:
                            pe.wait_ge(misc_copied, 3 * t + 3)
                        pe.wait_ge(h_ready, f + 1)
                        nc.tensor.matmul(comb_bank[0:m], w["spread"][0:CR, j * P:j * P + m], combT[:, u, :],
                                         start=True, stop=True).then_inc(comb_ready, 1)
                        if j < NCH - 1:
                            gate_up(f + 1, u, (r + 1) % 2, j + 1)
                        else:
                            gate_up(f + 1, 1 - u, (r + 1) % 2, 0)
                        if j == TR0:
                            transposes(t + 1, 0)
                        if j == TR1:
                            transposes(t + 1, 1)
                        if j == LOGITS:
                            logits(t + 1, 1 - u)
                        if j == COMB_T:
                            transpose_parts(t + 1)
                        pe.wait_ge(h_ready, f + 2)
                        if j == 0:
                            pe.wait_ge(result_ready, 2 * t + 1)
                        for k in range(T):
                            last = nc.tensor.matmul(y_banks[k // 2][:, (k % 2) * C:(k % 2 + 1) * C],
                                                    h[0:m, r, k * P:(k + 1) * P], w["down"][0:m, j, :],
                                                    start=(j == 0 and k % 2 == 0), stop=(j == NCH - 1),
                                                    skip_group_check=True)
                        last.then_inc(h_used, 1)

        @block.scalar
        def _(act):
            def copy_hT(n, b, half):
                act.wait_ge(misc_ready, 4 * n + half + 1)
                nc.scalar.copy(hT[:, b, :, half * 2 * P:(half + 1) * 2 * P],
                               misc[:].rearrange("p (k t) -> p k t", k=KT)).then_inc(misc_copied, 1)

            def exps(n):
                act.wait_ge(shifted_ready, n + 1)
                nc.scalar.activation(expd[:], shifted[:], ACT.Exp).then_inc(exp_ready, 1)

            def copy_combT(n, b):
                act.wait_ge(misc_ready, 4 * n + 4)
                nc.scalar.copy(combT[:, b], misc[:].bitcast(BF16)[0:CR, 0:TOK]).then_inc(misc_copied, 1)

            copy_hT(0, 0, 0)
            copy_hT(0, 0, 1)
            exps(0)
            copy_combT(0, 0)
            with act.Fori(0, STEPS // 2) as i:
                for u in range(2):
                    t, nb = 2 * i + u, 1 - u
                    for j in range(NCH):
                        f, r = t * NCH + j, (u * NCH + j) % 2
                        m = min(P, hidden - j * P)
                        act.wait_ge(gate_ready, f + 1)
                        act.wait_ge(gated_ready, f + 1)
                        nc.scalar.activation(silu[0:m, r], gate_banks[r][0:m], ACT.Silu).then_inc(silu_ready, 1)
                        if j == COPY0:
                            copy_hT(t + 1, nb, 0)
                        if j == COPY1:
                            copy_hT(t + 1, nb, 1)
                        if j == EXPS:
                            exps(t + 1)
                        if j == COPY_COMB:
                            copy_combT(t + 1, nb)

        @block.vector
        def _(dve):
            chain = Chain(dve, look, 4 * T + 8 + (18 if keep == 8 else 1))

            def statistics(n, b, before):
                dve.wait_ge(loaded[b], 16 * (before + 1))
                chain.start(n)
                for k in range(T):
                    chain.add(nc.vector.bn_stats(stats[:, k], xin[:, b, k]))
                chain.wait()
                dve.sem_inc(apart, 1)
                for k in range(T - 1):
                    chain.add(nc.vector.bn_aggr(mv[:, k], stats[:, k]))
                nc.vector.bn_aggr(mv[:, T - 1], stats[:, T - 1]).then_inc(var_ready, 1)

            def normalise(n, b):
                dve.wait_ge(rstd_ready, n + 1)
                for k in range(T):
                    nc.vector.tensor_scalar(hn[:, k], xin[:, b, k], mv[:, k, 0:1], rstd[:, k:k + 1],
                                            ALU.subtract, ALU.mult).then_inc(hn_ready, 1)

            def per_token(a, width):
                return a.unsqueeze(2).to_broadcast([P, T, width])

            def shift(n):
                logits = misc[:, 0:T * experts].rearrange("p (t e) -> p t e", t=T)
                dve.wait_ge(misc_ready, 4 * n + 3)
                chain.add(nc.vector.reduce_max(mx[:], logits, AX.X))
                chain.wait()
                nc.vector.tensor_tensor(shifted[:], logits, per_token(mx[:], experts), ALU.subtract).then_inc(shifted_ready, 1)

            def probabilities(n):
                dve.wait_ge(exp_ready, n + 1)
                chain.add(nc.vector.reduce_sum(rsum[:], expd[:], AX.X))
                chain.wait()
                chain.add(nc.vector.reciprocal(tsum[:], rsum[:]))
                chain.wait()
                chain.add(nc.vector.tensor_tensor(probs[:, :, 0:experts], expd[:], per_token(tsum[:], experts), ALU.mult))
                chain.wait()
                dve.sem_inc(apart, 1)
                for k in range(T):
                    chain.add(nc.vector.max(top[:, k], probs[:, k, 0:experts]))
                chain.wait()

            def keep_by_share():
                chain.add(nc.vector.reduce_sum(tsum[:], top[:], AX.X))
                chain.wait()
                chain.add(nc.vector.tensor_scalar(tsum[:], tsum[:], 1e-12, None, ALU.max))
                chain.wait()
                chain.add(nc.vector.reciprocal(rsum[:], tsum[:]))
                chain.wait()
                chain.add(nc.vector.tensor_tensor(cum[:, 0], top[:], per_token(rsum[:], 8), ALU.mult))
                chain.wait()
                a = 0
                for d in (1, 2, 4):
                    chain.add(nc.vector.tensor_copy(cum[:, 1 - a, :, 0:d], cum[:, a, :, 0:d]))
                    chain.add(nc.vector.tensor_tensor(cum[:, 1 - a, :, d:8], cum[:, a, :, d:8], cum[:, a, :, 0:8 - d], ALU.add))
                    chain.wait()
                    a = 1 - a
                chain.add(nc.vector.tensor_scalar(active[:, :, 1:8], cum[:, a, :, 0:7], THRESHOLD, None, ALU.is_lt))
                chain.wait()
                chain.add(nc.vector.tensor_tensor(kept[:], top[:], active[:], ALU.mult))
                chain.add(nc.vector.tensor_scalar(found[:], active[:], -NOT_KEPT, NOT_KEPT, ALU.mult, ALU.add))
                chain.wait()
                chain.add(nc.vector.tensor_tensor(found[:], found[:], kept[:], ALU.add))
                chain.add(nc.vector.reduce_sum(tsum[:], kept[:], AX.X))
                chain.wait()
                chain.add(nc.vector.tensor_scalar(tsum[:], tsum[:], 1e-12, None, ALU.max))
                chain.wait()
                chain.add(nc.vector.reciprocal(rsum[:], tsum[:]))

            def combine(n):
                if keep == 8:
                    keep_by_share()
                else:
                    chain.add(nc.vector.tensor_copy(found[:, :, 0:keep], top[:, :, 0:keep]))
                chain.wait()
                dve.sem_inc(apart, 1)
                for k in range(T):
                    chain.add(nc.vector.match_replace(replaced[:, k], found[:, k], probs[:, k], -9.0))
                chain.wait()
                chain.add(nc.vector.tensor_tensor(chosen[:], replaced[:, :, 0:experts], probs[:, :, 0:experts], ALU.not_equal))
                chain.wait()
                chain.add(nc.vector.tensor_tensor(comb[:], chosen[:], probs[:, :, 0:experts], ALU.mult))
                chain.wait()
                if keep == 8:
                    chain.add(nc.vector.tensor_tensor(comb[:], comb[:], per_token(rsum[:], experts), ALU.mult))
                    chain.wait()
                chain.add(nc.vector.tensor_copy(parts[:, :, 0:experts], comb[:]))
                chain.wait()
                chain.add(nc.vector.tensor_tensor(rest[:], comb[:], parts[:, :, 0:experts], ALU.subtract))
                chain.wait()
                chain.add(nc.vector.tensor_copy(parts[:, :, experts:2 * experts], rest[:]))
                chain.wait()
                nc.vector.tensor_tensor(parts[:, :, 2 * experts:3 * experts], rest[:], parts[:, :, experts:2 * experts],
                                        ALU.subtract).then_inc(parts_ready, 1)
                chain.done()

            nc.vector.memset(probs[:, :, experts:], NOT_KEPT).then_inc(const_ready, 1)
            nc.vector.memset(active[:], 1.0).then_inc(const_ready, 1)
            nc.vector.memset(found[:], NOT_KEPT).then_inc(const_ready, 1)
            nc.vector.memset(parts[:], 1.0).then_inc(const_ready, 1)
            dve.wait_ge(const_ready, 4)
            statistics(0, 0, 0)
            normalise(0, 0)
            shift(0)
            probabilities(0)
            combine(0)
            with dve.Fori(0, STEPS // 2) as i:
                for u in range(2):
                    t, nb = 2 * i + u, 1 - u
                    for j in range(NCH):
                        f, r = t * NCH + j, (u * NCH + j) % 2
                        m = min(P, hidden - j * P)
                        dve.wait_ge(silu_ready, f + 3)
                        dve.wait_ge(up_ready, f + 1)
                        nc.vector.tensor_tensor(gated[0:m, r], silu[0:m, r], up_banks[r][0:m], ALU.mult).then_inc(gated_ready, 1)
                        dve.wait_ge(gated_ready, f + 3)
                        dve.wait_ge(comb_ready, f + 1)
                        dve.wait_ge(h_used, f + 1)
                        nc.vector.tensor_tensor(h[0:m, r], gated[0:m, r], comb_bank[0:m], ALU.mult).then_inc(h_ready, 1)
                        if j == STATS:
                            statistics(t + 1, nb, i + u)
                        if j == NORM:
                            normalise(t + 1, nb)
                        if j == SHIFT:
                            shift(t + 1)
                        if j == PROBS:
                            probabilities(t + 1)
                        if j == COMB:
                            combine(t + 1)
                    dve.wait_ge(h_used, (t + 1) * NCH + 2)
                    dve.wait_ge(stored, 16 * t + 16)
                    for half in range(2):
                        s = slice(2 * half, 2 * half + 2)
                        nc.vector.tensor_tensor(xout[:, u, s], y_banks[half][:].rearrange("p (t c) -> p t c", t=2),
                                                xin[:, u, s], ALU.add).then_inc(result_ready, 1)


def lightning_phase(nc, banks, w, weights_loaded, weights_value, src, dst):
    T = 2
    TOK = T * P
    STEPS = NT // T
    QC = LA_HEADS // 4
    TRI = 3 * P
    RING = 4
    PROLOGUE, FILLS = 5, 6
    STATS, NORM, TR = 0, 3, 6

    with ExitStack() as ctx:
        def sb(name, shape, dt=F32):
            return ctx.enter_context(nc.sbuf_tensor(f"la_{name}", shape, dt))

        def sem(name):
            return ctx.enter_context(nc.semaphore(f"la_{name}"))

        decay = sb("decay", [P, LA_HEADS, TRI])
        neg_slopes = sb("neg_slopes", [P, LA_HEADS])
        xin = sb("xin", [P, 2, T, C])
        xout = sb("xout", [P, 2, T, C])
        xb = sb("xb", [P, 2, T, C])
        stats = sb("stats", [P, T, 6])
        mv = sb("mv", [P, T, 2])
        veps = sb("veps", [P, T])
        rstd = sb("rstd", [P, T])
        hn = sb("hn", [P, T, C])
        hT = sb("hT", [P, KT, TOK])
        qkT = sb("qkT", [P, 2 * QC, TOK])
        v = sb("v", [P, T, C])
        weighted = sb("weighted", [P, RING, TRI])
        o = sb("o", [P, T, C])
        oT = sb("oT", [P, KT, TOK])

        tr_bank, proj_banks, score_banks, o_bank = banks[0], banks[1:3], banks[3:7], banks[7]

        loaded = [sem("x_loaded_0"), sem("x_loaded_1")]
        stored = sem("x_stored")
        slopes_ready = sem("slopes_ready")
        exp_ready = sem("exp_ready")
        decay_ready = sem("decay_ready")
        stats_chain = sem("stats_chain")
        var_ready = sem("var_ready")
        pool_chain = sem("pool_chain")
        rstd_ready = sem("rstd_ready")
        xb_ready = sem("xb_ready")
        hn_ready = sem("hn_ready")
        tr_ready = sem("transposes_ready")
        tr_copied = sem("transposes_copied")
        proj_ready = sem("proj_ready")
        proj_read = [sem("proj_read_0"), sem("proj_read_1")]
        scores_ready = sem("scores_ready")
        weighted_ready = sem("weighted_ready")
        head_done = sem("head_done")
        o_copied = sem("o_copied")
        result_ready = sem("result_ready")

        apart = sem("apart")

        block = ctx.enter_context(nc.Block())

        @block.sync
        def _(sp):
            move_x(sp, STEPS, T, src, dst, xin, xout, loaded, result_ready, 1, stored)

        @block.gpsimd
        def _(pool):
            def inverse_deviation(n):
                pool.wait_ge(var_ready, n + 1)
                pool.sem_inc(apart, 1)
                nc.gpsimd.tensor_scalar(veps[:], mv[:, :, 1], LN_EPS, None, ALU.add).then_inc(pool_chain, 1)
                pool.wait_ge(pool_chain, n + 1)
                nc.gpsimd.tensor_tensor(rstd[:], veps[:], w["minus_half"][:, 0:T], ALU.pow).then_inc(rstd_ready, 1)

            def add_bias(b, before):
                pool.wait_ge(loaded[b], 16 * (before + 1))
                nc.gpsimd.tensor_tensor(xb[:, b], xin[:, b], w["bout"][:].unsqueeze(1).to_broadcast([P, T, C]),
                                        ALU.add).then_inc(xb_ready, 1)

            pool.wait_ge(weights_loaded, weights_value)
            inverse_deviation(0)
            add_bias(0, 0)
            for hd in range(LA_HEADS):
                pool.wait_ge(exp_ready, hd + 1)
                nc.gpsimd.tensor_tensor(decay[:, hd], decay[:, hd], w["causal"][:], ALU.mult).then_inc(decay_ready, 1)
            with pool.Fori(0, STEPS // 2) as i:
                for u in range(2):
                    inverse_deviation(2 * i + u + 1)
                    pool.wait_ge(result_ready, 2 * i + u + 1)
                    add_bias(1 - u, i + u)

        @block.tensor
        def _(pe):
            def transposes(dst_bank, a):
                out = dst_bank[:].rearrange("p (k t) -> p k t", k=KT)
                for k in range(KT):
                    for j in range(T):
                        last = nc.tensor.transpose(out[:, k, j * P:(j + 1) * P], a[:, j, k * P:(k + 1) * P], w["ident"][:])
                last.then_inc(tr_ready, 1)

            def transpose_hn(n, fills):
                pe.wait_ge(hn_ready, T * (n + 1))
                if fills is not None:
                    pe.wait_ge(tr_copied, fills)
                transposes(tr_bank, hn)

            def bank_free(loops, f):
                k = f - PROLOGUE
                if loops is None:
                    if f >= 2:
                        pe.wait_ge(proj_read[f % 2], f // 2)
                elif k % 2 == 0:
                    pe.wait_ge(proj_read[1], PROLOGUE // 2 + (FILLS // 2) * loops + k // 2)
                elif k == 1:
                    pe.wait_ge(result_ready, loops + 1)
                else:
                    pe.wait_ge(proj_read[0], (PROLOGUE + 1) // 2 + (FILLS // 2 - 1) * loops + k // 2)

            def project_qk(loops, fill):
                for c2 in range(QC):
                    f = fill + c2
                    bank_free(loops, f)
                    for c in range(2):
                        ch = 2 * c2 + c
                        for k in range(KT):
                            last = nc.tensor.matmul(proj_banks[f % 2][:, c * TOK:(c + 1) * TOK],
                                                    w["wqk"][:, k, ch * P:(ch + 1) * P], hT[:, k, :],
                                                    start=(k == 0), stop=(k == KT - 1))
                    last.then_inc(proj_ready, 1)

            def project_tokens(loops, f, a, wt):
                bank_free(loops, f)
                for j in range(T):
                    for k in range(KT):
                        last = nc.tensor.matmul(proj_banks[f % 2][:, j * C:(j + 1) * C], a[:, k, j * P:(j + 1) * P],
                                                wt[:, k, :], start=(k == 0), stop=(k == KT - 1))
                last.then_inc(proj_ready, 1)

            def scores(g, hd):
                r, c, s = 32 * (hd % 4), hd // 4, score_banks[hd % RING]
                pe.wait_ge(weighted_ready, g + 1)
                q, k = qkT[r:r + LA_HD, c], qkT[r:r + LA_HD, QC + c]
                nc.tensor.matmul(s[:, 0:TOK], k[:, 0:P], q[:, 0:TOK], start=True, stop=True)
                nc.tensor.matmul(s[:, TOK:TRI], k[:, P:TOK], q[:, P:TOK], start=True, stop=True).then_inc(scores_ready, 1)

            def outputs(g, hd):
                a, cols = weighted[:, hd % RING], slice(hd * LA_HD, (hd + 1) * LA_HD)
                pe.wait_ge(weighted_ready, g + 1 + RING)
                nc.tensor.matmul(o_bank[:, cols], a[:, 0:P], v[:, 0, cols], start=True, stop=True)
                out = o_bank[:, C + hd * LA_HD:C + (hd + 1) * LA_HD]
                nc.tensor.matmul(out, a[:, P:TOK], v[:, 0, cols], start=True, stop=False)
                nc.tensor.matmul(out, a[:, TOK:TRI], v[:, 1, cols], start=False, stop=True).then_inc(head_done, 1)

            pe.sem_inc(weighted_ready, RING)
            pe.sem_inc(o_copied, 1)
            pe.sem_inc(head_done, RING)
            pe.wait_ge(weights_loaded, weights_value)
            transpose_hn(0, None)
            pe.wait_ge(tr_copied, 1)
            project_qk(None, 0)
            project_tokens(None, QC, hT, w["wv"])
            with pe.Fori(0, STEPS // 2) as i:
                for u in range(2):
                    t = 2 * i + u
                    pe.wait_ge(proj_read[0], (PROLOGUE + 1) // 2 + (FILLS // 2 - 1) * t)
                    pe.wait_ge(proj_read[1], PROLOGUE // 2 + (FILLS // 2) * t)
                    pe.wait_ge(o_copied, t + 1)
                    for s in range(LA_HEADS + 3):
                        if s < LA_HEADS:
                            scores(t * LA_HEADS + s, s)
                        if s == TR:
                            transpose_hn(t + 1, 2 * t + 1)
                        if s >= 3:
                            outputs(t * LA_HEADS + s - 3, s - 3)
                    pe.wait_ge(tr_copied, 2 * t + 2)
                    project_qk(t, PROLOGUE)
                    pe.wait_ge(o_copied, t + 2)
                    transposes(tr_bank, o)
                    project_tokens(t, PROLOGUE + QC, hT, w["wv"])
                    pe.wait_ge(tr_copied, 2 * t + 3)
                    project_tokens(t, PROLOGUE + QC + 1, oT, w["wo"])

        @block.scalar
        def _(act):
            def copy_transposed(n, to):
                act.wait_ge(tr_ready, n + 1)
                nc.scalar.copy(to[:], tr_bank[:].rearrange("p (k t) -> p k t", k=KT)).then_inc(tr_copied, 1)

            def copy_qk(loops, fill):
                for c2 in range(QC):
                    f = fill + c2
                    act.wait_ge(proj_ready, loops * FILLS + f + 1)
                    for c in range(2):
                        ch = 2 * c2 + c
                        last = nc.scalar.activation(qkT[:, ch], proj_banks[f % 2][:, c * TOK:(c + 1) * TOK],
                                                    ACT.Identity, bias=w["bqk"][:, ch:ch + 1])
                    last.then_inc(proj_read[f % 2], 1)

            act.wait_ge(weights_loaded, weights_value)
            nc.scalar.mul(neg_slopes[:], w["slopes"][:], -1.0).then_inc(slopes_ready, 1)
            act.wait_ge(slopes_ready, 1)
            for hd in range(LA_HEADS):
                nc.scalar.activation(decay[:, hd], w["distance"][:], ACT.Exp, scale=neg_slopes[:, hd:hd + 1]).then_inc(exp_ready, 1)
            copy_transposed(0, hT)
            copy_qk(0, 0)
            with act.Fori(0, STEPS // 2) as i:
                for u in range(2):
                    t = 2 * i + u
                    copy_transposed(2 * t + 1, hT)
                    act.wait_ge(head_done, (t + 1) * LA_HEADS + RING)
                    nc.scalar.copy(o[:], o_bank[:].rearrange("p (j c) -> p j c", j=T)).then_inc(o_copied, 1)
                    copy_qk(t, PROLOGUE)
                    copy_transposed(2 * t + 2, oT)

        @block.vector
        def _(dve):
            chain = Chain(dve, stats_chain, 2 * T - 1)

            def statistics(n, b, before):
                dve.wait_ge(loaded[b], 16 * (before + 1))
                chain.start(n)
                for k in range(T):
                    chain.add(nc.vector.bn_stats(stats[:, k], xin[:, b, k]))
                chain.wait()
                dve.sem_inc(apart, 1)
                for k in range(T - 1):
                    chain.add(nc.vector.bn_aggr(mv[:, k], stats[:, k]))
                nc.vector.bn_aggr(mv[:, T - 1], stats[:, T - 1]).then_inc(var_ready, 1)
                chain.done()

            def normalise(n, b):
                dve.wait_ge(rstd_ready, n + 1)
                for k in range(T):
                    nc.vector.tensor_scalar(hn[:, k], xin[:, b, k], mv[:, k, 0:1], rstd[:, k:k + 1],
                                            ALU.subtract, ALU.mult).then_inc(hn_ready, 1)

            def copy_v(loops, f):
                dve.wait_ge(proj_ready, loops * FILLS + f + 1)
                nc.vector.tensor_tensor(v[:], proj_banks[f % 2][:].rearrange("p (j c) -> p j c", j=T),
                                        w["bv"][:].unsqueeze(1).to_broadcast([P, T, C]), ALU.add).then_inc(proj_read[f % 2], 1)

            dve.wait_ge(weights_loaded, weights_value)
            statistics(0, 0, 0)
            normalise(0, 0)
            copy_v(0, QC)
            with dve.Fori(0, STEPS // 2) as i:
                for u in range(2):
                    t = 2 * i + u
                    for s in range(LA_HEADS):
                        g = t * LA_HEADS + s
                        if u == 0:
                            dve.wait_ge(decay_ready, s + 1)
                        dve.wait_ge(scores_ready, g + 1)
                        dve.wait_ge(head_done, g + 1)
                        nc.vector.tensor_tensor(weighted[:, s % RING], score_banks[s % RING][:, 0:TRI], decay[:, s],
                                                ALU.mult).then_inc(weighted_ready, 1)
                        if s == STATS:
                            statistics(t + 1, 1 - u, i + u)
                        if s == NORM:
                            normalise(t + 1, 1 - u)
                    copy_v(t, PROLOGUE + QC)
                    f = PROLOGUE + QC + 1
                    dve.wait_ge(proj_ready, t * FILLS + f + 1)
                    dve.wait_ge(stored, 16 * t + 16)
                    dve.wait_ge(xb_ready, t + 1)
                    nc.vector.tensor_tensor(xout[:, u], proj_banks[f % 2][:].rearrange("p (j c) -> p j c", j=T),
                                            xb[:, u], ALU.add).then_inc(result_ready, 1)


def grouped_phase(nc, banks, w, weights_loaded, weights_value, next_weights, src, dst):
    T = 2
    TOK = T * P
    STEPS = NT // T
    GROUP = HQ // HKV
    PAIRS = HQ // 2
    TRI = 3 * P
    RING = 4
    SCALE = HD ** -0.5
    PROLOGUE = 3 + 2 + 2
    F_T, F_K, F_V, F_Q, F_OUT = 6, 7, 9, 11, 13
    FILLS = 14
    ROPE_PROLOGUE, ROPES = 4, 10
    STATS, NORM = 1, 5

    with ExitStack() as ctx:
        def sb(name, shape, dt=F32):
            return ctx.enter_context(nc.sbuf_tensor(f"ga_{name}", shape, dt))

        def sem(name):
            return ctx.enter_context(nc.semaphore(f"ga_{name}"))

        xin = sb("xin", [P, 2, T, C])
        xout = sb("xout", [P, 2, T, C])
        stats = sb("stats", [P, T, 6])
        mv = sb("mv", [P, T, 2])
        small = sb("small", [P, 6, T])
        rstd = sb("rstd", [P, T])
        hn = sb("hn", [P, T, C])
        hT = sb("hT", [P, KT, TOK])
        raw = sb("raw", [P, 2, 2, TOK])
        by_cos = sb("by_cos", [P, 2, 2, TOK])
        by_sin = sb("by_sin", [P, 2, TOK])
        q = sb("q", [P, 4, 2, TOK])
        kr = sb("kr", [P, HKV, TOK])
        v = sb("v", [P, T, HKV * HD])
        top = sb("top", [P, RING, 2])
        bias = sb("bias", [P, RING, 2])
        rsum = sb("rsum", [P, RING, 2])
        rinv = sb("rinv", [P, RING, 2])
        probs = sb("probs", [P, RING, TRI])
        probsT = sb("probsT", [P, 2, TRI])
        attn = sb("attn", [P, HQ, TOK])

        proj_banks, score_banks, pt_banks, attn_banks = banks[0:2], banks[2:4], banks[4:6], banks[6:8]

        loaded = [sem("x_loaded_0"), sem("x_loaded_1")]
        stored = sem("x_stored")
        stats_chain = sem("stats_chain")
        var_ready = sem("var_ready")
        pool_chain = sem("pool_chain")
        rstd_ready = sem("rstd_ready")
        hn_ready = sem("hn_ready")
        proj_ready = sem("proj_ready")
        hT_ready = sem("hT_ready")
        raw_ready = sem("raw_ready")
        v_ready = sem("v_ready")
        cos_ready = sem("cos_ready")
        sin_ready = sem("sin_ready")
        roped = sem("roped")
        scores_ready = sem("scores_ready")
        max_chain = sem("max_chain")
        bias_ready = sem("bias_ready")
        exp_ready = sem("exp_ready")
        rinv_ready = sem("rinv_ready")
        probs_ready = sem("probs_ready")
        pt_ready = sem("pt_ready")
        pt_copied = sem("pt_copied")
        attn_ready = sem("attn_ready")
        attn_copied = sem("attn_copied")
        result_ready = sem("result_ready")

        apart = sem("apart")

        block = ctx.enter_context(nc.Block())

        @block.sync
        def _(sp):
            next_weights(sp)
            move_x(sp, STEPS, T, src, dst, xin, xout, loaded, result_ready, 1, stored)

        @block.gpsimd
        def _(pool):
            steps = Chain(pool, pool_chain, 6)

            def inverse_deviation(n):
                pool.wait_ge(var_ready, n + 1)
                pool.sem_inc(apart, 1)
                var = mv[:, :, 1]
                steps.start(n)
                steps.add(nc.gpsimd.tensor_scalar(small[:, 0], var, LN_EPS, None, ALU.add))
                steps.wait()
                steps.add(nc.gpsimd.tensor_tensor(small[:, 1], small[:, 0], w["minus_half"][:, 0:T], ALU.pow))
                steps.wait()
                steps.add(nc.gpsimd.tensor_tensor(small[:, 2], small[:, 1], small[:, 1], ALU.mult))
                steps.wait()
                steps.add(nc.gpsimd.tensor_tensor(small[:, 3], small[:, 2], var, ALU.mult))
                steps.wait()
                pool.sem_inc(apart, 1)
                steps.add(nc.gpsimd.tensor_scalar(small[:, 4], small[:, 3], RMS_EPS, None, ALU.add))
                steps.wait()
                steps.add(nc.gpsimd.tensor_tensor(small[:, 5], small[:, 4], w["minus_half"][:, 0:T], ALU.pow))
                steps.wait()
                nc.gpsimd.tensor_tensor(rstd[:], small[:, 5], small[:, 1], ALU.mult).then_inc(rstd_ready, 1)
                steps.done()

            def cosine(loops, k):
                r = k % 2
                pool.wait_ge(raw_ready, loops * ROPES + k + 1)
                if isinstance(loops, int) and k < 2:
                    pass
                else:
                    pool.wait_ge(roped, loops * ROPES + k - 1)
                nc.gpsimd.tensor_tensor(by_cos[:, r], raw[:, r], w["cos"][:].unsqueeze(1).to_broadcast([P, 2, TOK]),
                                        ALU.mult).then_inc(cos_ready, 1)

            def normalise(g, hd):
                r = hd % RING
                pool.wait_ge(rinv_ready, g + 1)
                pool.sem_inc(apart, 1)
                nc.gpsimd.tensor_scalar(probs[:, r, 0:P], probs[:, r, 0:P], rinv[:, r, 0:1], None, ALU.mult)
                nc.gpsimd.tensor_scalar(probs[:, r, P:TRI], probs[:, r, P:TRI], rinv[:, r, 1:2], None,
                                        ALU.mult).then_inc(probs_ready, 1)

            pool.wait_ge(weights_loaded, weights_value)
            inverse_deviation(0)
            for k in range(ROPE_PROLOGUE):
                cosine(0, k)
            with pool.Fori(0, STEPS // 2) as i:
                for u in range(2):
                    t = 2 * i + u
                    for s in range(HQ + 1):
                        if s >= 1:
                            normalise(t * HQ + s - 1, s - 1)
                        if s % 2 == 0 and s // 2 < PAIRS - 2:
                            cosine(t, ROPE_PROLOGUE + s // 2)
                        if s == STATS:
                            inverse_deviation(t + 1)
                    for k in range(4):
                        cosine(t, ROPE_PROLOGUE + PAIRS - 2 + k)

        @block.tensor
        def _(pe):
            def bank_free(loops, f):
                if loops is None:
                    if f >= 2:
                        pe.wait_ge(*((hT_ready, 1), (raw_ready, 1), (raw_ready, 2), (v_ready, 1), (v_ready, 2))[f - 2])
                    return
                k = f - PROLOGUE - 2
                if k == -2:
                    pe.wait_ge(raw_ready, loops * ROPES + ROPE_PROLOGUE)
                elif k == -1:
                    pe.wait_ge(result_ready, loops + 1)
                elif k < F_T:
                    pe.wait_ge(raw_ready, loops * ROPES + ROPE_PROLOGUE + k + 1)
                elif k == F_T:
                    pe.wait_ge(hT_ready, loops + 2)
                elif k < F_V:
                    pe.wait_ge(raw_ready, loops * ROPES + ROPE_PROLOGUE + k)
                elif k < F_Q:
                    pe.wait_ge(v_ready, 2 * loops + 3 + k - F_V)
                else:
                    pe.wait_ge(raw_ready, loops * ROPES + ROPE_PROLOGUE + k - 2)

            def transpose_hn(loops, f, n):
                pe.wait_ge(hn_ready, T * (n + 1))
                bank_free(loops, f)
                out = proj_banks[f % 2][:].rearrange("p (k t) -> p k t", k=KT)
                for k in range(KT):
                    for j in range(T):
                        last = nc.tensor.transpose(out[:, k, j * P:(j + 1) * P], hn[:, j, k * P:(k + 1) * P], w["ident"][:])
                last.then_inc(proj_ready, 1)

            def project(loops, f, wt, pair):
                bank_free(loops, f)
                for c in range(2):
                    ch = 2 * pair + c
                    for k in range(KT):
                        last = nc.tensor.matmul(proj_banks[f % 2][:, c * TOK:(c + 1) * TOK], wt[:, k, ch * HD:(ch + 1) * HD],
                                                hT[:, k, :], start=(k == 0), stop=(k == KT - 1))
                last.then_inc(proj_ready, 1)

            def project_v(loops, f, j):
                bank_free(loops, f)
                for k in range(KT):
                    last = nc.tensor.matmul(proj_banks[f % 2][:], hT[:, k, j * P:(j + 1) * P], w["wv1"][:, k, :],
                                            start=(k == 0), stop=(k == KT - 1))
                last.then_inc(proj_ready, 1)

            def scores(g, hd):
                s, kv = score_banks[hd % 2], kr[:, hd // GROUP]
                qh = q[:, (hd // 2) % 4, hd % 2]
                pe.wait_ge(exp_ready, g + 1)
                for tile, c0, keys in ((0, 0, P), (1, P, TOK)):
                    nc.tensor.matmul(s[:, c0:c0 + keys], qh[:, tile * P:(tile + 1) * P], kv[:, 0:keys], start=True, stop=False)
                    last = nc.tensor.matmul(s[:, c0 + keys - P:c0 + keys], w["ident_bf"][:], w["masked"][:],
                                            start=False, stop=True)
                last.then_inc(scores_ready, 1)

            def transpose_probs(g, hd):
                pe.wait_ge(probs_ready, g + 1)
                pe.wait_ge(pt_copied, g + 1)
                for blk in range(3):
                    last = nc.tensor.transpose(pt_banks[hd % 2][:, blk * P:(blk + 1) * P],
                                               probs[:, hd % RING, blk * P:(blk + 1) * P], w["ident"][:])
                last.then_inc(pt_ready, 1)

            def attend(g, t, hd):
                out = attn_banks[(hd // 2) % 2][:, (hd % 2) * TOK:(hd % 2 + 1) * TOK]
                cols = slice((hd // GROUP) * HD, (hd // GROUP + 1) * HD)
                pe.wait_ge(pt_copied, g + 3)
                if hd == 0:
                    pe.wait_ge(v_ready, 2 * (t + 1))
                if hd % 2 == 0:
                    pe.wait_ge(attn_copied, t * PAIRS + hd // 2 + 1)
                nc.tensor.matmul(out, v[:, 0, cols], probsT[:, hd % 2, 0:TOK], start=True, stop=False)
                nc.tensor.matmul(out[:, P:TOK], v[:, 1, cols], probsT[:, hd % 2, TOK:TRI], start=False,
                                 stop=True).then_inc(attn_ready, 1)

            def project_out(t):
                f = PROLOGUE + F_OUT
                pe.wait_ge(attn_copied, (t + 1) * PAIRS + 2)
                bank_free(t, f)
                for j in range(T):
                    for hd in range(HQ):
                        last = nc.tensor.matmul(proj_banks[f % 2][:, j * C:(j + 1) * C], attn[:, hd, j * P:(j + 1) * P],
                                                w["wo1"][:, hd, :], start=(hd == 0), stop=(hd == HQ - 1))
                last.then_inc(proj_ready, 1)

            pe.sem_inc(exp_ready, 2)
            pe.sem_inc(pt_copied, 2)
            pe.sem_inc(attn_ready, 2)
            pe.sem_inc(attn_copied, 2)
            pe.wait_ge(weights_loaded, weights_value)
            transpose_hn(None, 0, 0)
            pe.wait_ge(hT_ready, 1)
            project(None, 1, w["wk"], 0)
            project(None, 2, w["wk"], 1)
            project_v(None, 3, 0)
            project_v(None, 4, 1)
            project(None, 5, w["wq"], 0)
            project(None, 6, w["wq"], 1)
            with pe.Fori(0, STEPS // 2) as i:
                for u in range(2):
                    t = 2 * i + u
                    for s in range(HQ + 3):
                        if s < HQ:
                            if s == 0:
                                pe.wait_ge(roped, t * ROPES + ROPE_PROLOGUE - 1)
                            elif s == 2:
                                pe.wait_ge(roped, t * ROPES + ROPE_PROLOGUE)
                            elif s % 2 == 0:
                                pe.wait_ge(roped, t * ROPES + ROPE_PROLOGUE + s // 2 - 1)
                            scores(t * HQ + s, s)
                        if s % 2 == 0 and s // 2 < PAIRS - 2:
                            project(t, PROLOGUE + s // 2, w["wq"], 2 + s // 2)
                        if s == HQ - 4:
                            transpose_hn(t, PROLOGUE + F_T, t + 1)
                        if s == HQ:
                            pe.wait_ge(hT_ready, t + 2)
                            project(t, PROLOGUE + F_K, w["wk"], 0)
                        if s == HQ + 1:
                            project(t, PROLOGUE + F_K + 1, w["wk"], 1)
                        if 2 <= s < HQ + 2:
                            transpose_probs(t * HQ + s - 2, s - 2)
                        if s >= 3:
                            attend(t * HQ + s - 3, t, s - 3)
                    project_v(t, PROLOGUE + F_V, 0)
                    project_v(t, PROLOGUE + F_V + 1, 1)
                    project(t, PROLOGUE + F_Q, w["wq"], 0)
                    project(t, PROLOGUE + F_Q + 1, w["wq"], 1)
                    project_out(t)

        @block.scalar
        def _(act):
            def copy_hT(loops, f):
                act.wait_ge(proj_ready, loops * FILLS + f + 1)
                for k in range(KT):
                    last = nc.scalar.activation(hT[:, k], proj_banks[f % 2][:, k * TOK:(k + 1) * TOK], ACT.Identity,
                                                scale=w["ln_weight"][:, k:k + 1])
                last.then_inc(hT_ready, 1)

            def copy_raw(loops, f, rope, biases, pair):
                act.wait_ge(proj_ready, loops * FILLS + f + 1)
                if not (isinstance(loops, int) and rope < 2):
                    act.wait_ge(roped, loops * ROPES + rope - 1)
                for c in range(2):
                    ch = 2 * pair + c
                    last = nc.scalar.activation(raw[:, rope % 2, c], proj_banks[f % 2][:, c * TOK:(c + 1) * TOK],
                                                ACT.Identity, bias=biases[:, ch:ch + 1])
                last.then_inc(raw_ready, 1)

            def exps(g, hd):
                r, s = hd % RING, score_banks[hd % 2]
                act.wait_ge(bias_ready, g + 1)
                for tile, c in ((0, slice(0, P)), (1, slice(P, TRI))):
                    last = nc.scalar.activation(probs[:, r, c], s[:, c], ACT.Exp, bias=bias[:, r, tile:tile + 1],
                                                scale=SCALE, accum_out=rsum[:, r, tile:tile + 1])
                last.then_inc(exp_ready, 1)

            def copy_attn(t, pair):
                act.wait_ge(attn_ready, t * HQ + 2 * pair + 4)
                nc.scalar.copy(attn[:, 2 * pair:2 * pair + 2], attn_banks[pair % 2][:].rearrange("p (h t) -> p h t", h=2)).then_inc(attn_copied, 1)

            act.wait_ge(weights_loaded, weights_value)
            copy_hT(0, 0)
            copy_raw(0, 1, 0, w["bk"], 0)
            copy_raw(0, 2, 1, w["bk"], 1)
            copy_raw(0, 5, 2, w["bq"], 0)
            copy_raw(0, 6, 3, w["bq"], 1)
            with act.Fori(0, STEPS // 2) as i:
                for u in range(2):
                    t = 2 * i + u
                    for s in range(HQ + 3):
                        if s < HQ:
                            exps(t * HQ + s, s)
                        if s % 2 == 0 and s // 2 < PAIRS - 2:
                            copy_raw(t, PROLOGUE + s // 2, ROPE_PROLOGUE + s // 2, w["bq"], 2 + s // 2)
                        if s == HQ - 4:
                            copy_hT(t, PROLOGUE + F_T)
                        if s == HQ:
                            copy_raw(t, PROLOGUE + F_K, ROPE_PROLOGUE + PAIRS - 2, w["bk"], 0)
                        if s == HQ + 1:
                            copy_raw(t, PROLOGUE + F_K + 1, ROPE_PROLOGUE + PAIRS - 1, w["bk"], 1)
                        if s >= 4 and s % 2 == 0:
                            copy_attn(t, (s - 4) // 2)
                    copy_raw(t, PROLOGUE + F_Q, ROPE_PROLOGUE + PAIRS, w["bq"], 0)
                    copy_raw(t, PROLOGUE + F_Q + 1, ROPE_PROLOGUE + PAIRS + 1, w["bq"], 1)

        @block.vector
        def _(dve):
            chain = Chain(dve, stats_chain, 2 * T - 1)

            def statistics(n, b, before):
                dve.wait_ge(loaded[b], 16 * (before + 1))
                chain.start(n)
                for k in range(T):
                    chain.add(nc.vector.bn_stats(stats[:, k], xin[:, b, k]))
                chain.wait()
                dve.sem_inc(apart, 1)
                for k in range(T - 1):
                    chain.add(nc.vector.bn_aggr(mv[:, k], stats[:, k]))
                nc.vector.bn_aggr(mv[:, T - 1], stats[:, T - 1]).then_inc(var_ready, 1)
                chain.done()

            def normalise(n, b):
                dve.wait_ge(rstd_ready, n + 1)
                for k in range(T):
                    nc.vector.tensor_scalar(hn[:, k], xin[:, b, k], mv[:, k, 0:1], rstd[:, k:k + 1],
                                            ALU.subtract, ALU.mult).then_inc(hn_ready, 1)

            def rope(loops, k, out):
                r, half = k % 2, HD // 2
                dve.wait_ge(raw_ready, loops * ROPES + k + 1)
                if not (isinstance(loops, int) and k == 0):
                    dve.wait_ge(roped, loops * ROPES + k)
                for d in range(2):
                    frm, to = slice((1 - d) * half, (2 - d) * half), slice(d * half, (d + 1) * half)
                    last = nc.vector.tensor_tensor(by_sin[to], raw[frm, r], w["sin"][frm].unsqueeze(1).to_broadcast([half, 2, TOK]),
                                                   ALU.mult)
                last.then_inc(sin_ready, 1)
                dve.wait_ge(sin_ready, loops * ROPES + k + 1)
                dve.wait_ge(cos_ready, loops * ROPES + k + 1)
                nc.vector.tensor_tensor(out, by_cos[:, r], by_sin[:], ALU.add).then_inc(roped, 1)

            def copy_v(loops, f, j):
                dve.wait_ge(proj_ready, loops * FILLS + f + 1)
                nc.vector.tensor_tensor(v[:, j], proj_banks[f % 2][:], w["bv1"][:], ALU.add).then_inc(v_ready, 1)

            def maximum(g, hd):
                r, s = hd % RING, score_banks[hd % 2]
                dve.wait_ge(scores_ready, g + 1)
                nc.vector.reduce_max(top[:, r, 0:1], s[:, 0:P], AX.X)
                nc.vector.reduce_max(top[:, r, 1:2], s[:, P:TRI], AX.X).then_inc(max_chain, 1)
                dve.wait_ge(max_chain, g + 1)
                nc.vector.tensor_scalar(bias[:, r], top[:, r], -SCALE, None, ALU.mult).then_inc(bias_ready, 1)

            def inverse_sum(g, hd):
                r = hd % RING
                dve.wait_ge(exp_ready, g + 3)
                nc.vector.reciprocal(rinv[:, r], rsum[:, r]).then_inc(rinv_ready, 1)

            def copy_probsT(g, hd):
                dve.wait_ge(pt_ready, g + 1)
                dve.wait_ge(attn_ready, g + 1)
                nc.vector.tensor_copy(probsT[:, hd % 2], pt_banks[hd % 2][:, 0:TRI]).then_inc(pt_copied, 1)

            dve.wait_ge(weights_loaded, weights_value)
            statistics(0, 0, 0)
            normalise(0, 0)
            rope(0, 0, kr[:, 0:2])
            rope(0, 1, kr[:, 2:4])
            copy_v(0, 3, 0)
            copy_v(0, 4, 1)
            rope(0, 2, q[:, 0])
            rope(0, 3, q[:, 1])
            with dve.Fori(0, STEPS // 2) as i:
                for u in range(2):
                    t = 2 * i + u
                    for s in range(HQ + 2):
                        if s < HQ:
                            maximum(t * HQ + s, s)
                        if 1 <= s <= HQ:
                            inverse_sum(t * HQ + s - 1, s - 1)
                        if s >= 2:
                            copy_probsT(t * HQ + s - 2, s - 2)
                        if s % 2 == 0 and s // 2 < PAIRS - 2:
                            rope(t, ROPE_PROLOGUE + s // 2, q[:, (2 + s // 2) % 4])
                        if s == STATS:
                            statistics(t + 1, 1 - u, i + u)
                        if s == NORM:
                            normalise(t + 1, 1 - u)
                    rope(t, ROPE_PROLOGUE + PAIRS - 2, kr[:, 0:2])
                    rope(t, ROPE_PROLOGUE + PAIRS - 1, kr[:, 2:4])
                    copy_v(t, PROLOGUE + F_V, 0)
                    copy_v(t, PROLOGUE + F_V + 1, 1)
                    rope(t, ROPE_PROLOGUE + PAIRS, q[:, 0])
                    rope(t, ROPE_PROLOGUE + PAIRS + 1, q[:, 1])
                    f = PROLOGUE + F_OUT
                    dve.wait_ge(proj_ready, t * FILLS + f + 1)
                    dve.wait_ge(stored, 16 * t + 16)
                    nc.vector.tensor_tensor(xout[:, u], proj_banks[f % 2][:].rearrange("p (j c) -> p j c", j=T),
                                            xin[:, u], ALU.add).then_inc(result_ready, 1)


def program(nc, a, out):
    with ExitStack() as ctx:
        def sb(name, shape, dt=F32):
            return ctx.enter_context(nc.sbuf_tensor(name, shape, dt))

        banks = [ctx.enter_context(nc.psum_tensor(f"bank{i}", [P, BANK], F32)) for i in range(8)]
        between = [nc.dram_tensor(f"x_after_{i}", (P, NT, C), F32, kind="Internal").ap() for i in range(3)]
        H0, H1 = E0 * I0, E1 * I1 + S1
        CH0, CH1 = -(-H0 // P), -(-H1 // P)
        wa = {"wqk": [P, KT, 8 * P], "wv": [P, KT, C], "wo": [P, KT, C], "bqk": [P, 8], "bv": [P, C], "bout": [P, C],
              "slopes": [P, LA_HEADS]}
        wc = {"wq": [P, KT, HQ * HD], "wk": [P, KT, HKV * HD], "wv1": [P, KT, HKV * HD], "wo1": [P, HQ, C],
              "bq": [P, HQ], "bk": [P, HKV], "bv1": [P, HKV * HD], "ln_weight": [P, KT]}
        ca = {"distance": [P, 3 * P], "causal": [P, 3 * P], "ident": [P, P], "minus_half": [P, 8]}
        cc = {"cos": [P, 2 * P], "sin": [P, 2 * P]}
        w = {name: sb(name, shape) for group in (wa, wc, ca, cc) for name, shape in group.items()}
        w["ident_bf"] = sb("ident_bf", [P, P], BF16)
        w["masked"] = sb("masked", [P, P], BF16)
        gate, up = sb("gate", [P, KT, H1]), sb("up", [P, KT, H1])
        down = sb("down", [P, CH1, C])
        router = sb("router", [P, KT, E0 + E1])
        spread = sb("spread", [3 * E0 + 1, H1], BF16)
        w0 = dict(w, gate=gate[:, :, 0:H0], up=up[:, :, 0:H0], down=down[:, 0:CH0], router=router[:, :, 0:E0], spread=spread)
        w1 = dict(w, gate=gate, up=up, down=down, router=router[:, :, E0:E0 + E1], spread=spread)

        loads_a = ctx.enter_context(nc.semaphore("weights_a"))
        loads_b = ctx.enter_context(nc.semaphore("weights_b"))
        loads_c = ctx.enter_context(nc.semaphore("weights_c"))
        loads_d = ctx.enter_context(nc.semaphore("weights_d"))

        def load_ffn(q, sem, n, h, chunks, rows):
            q.dma_start(gate[:, :, 0:h], a[f"gate{n}"]).then_inc(sem, 16)
            q.dma_start(up[:, :, 0:h], a[f"up{n}"]).then_inc(sem, 16)
            q.dma_start(down[:, 0:chunks], a[f"down{n}"]).then_inc(sem, 16)
            q.dma_start(router[:, :, n * E0:n * E0 + (E0, E1)[n]], a[f"router{n}"]).then_inc(sem, 16)
            q.dma_start(spread[0:rows, 0:h], a[f"spread{n}"]).then_inc(sem, 16)

        with nc.Block() as block:
            @block.sync
            def _(sp):
                for name in (*ca, *wa):
                    sp.dma_start(w[name][:], a[name]).then_inc(loads_a, 16)

            @block.scalar
            def _(act):
                act.dma_start(w["ident_bf"][:], a["ident_bf"]).then_inc(loads_b, 16)
                load_ffn(act, loads_b, 0, H0, CH0, 3 * E0 + 1)
                for name in (*wc, *cc):
                    act.dma_start(w[name][:], a[name]).then_inc(loads_c, 16)
                act.dma_start(w["masked"][:], a["masked"]).then_inc(loads_c, 16)

        def load_last_ffn(sp):
            load_ffn(sp, loads_d, 1, H1, CH1, 3 * E1 + 1)

        lightning_phase(nc, banks, w, loads_a, 16 * len((*ca, *wa)), a["x"], between[0])
        ffn_phase(nc, "f0", banks, w0, loads_b, 16 * 6, between[0], between[1], E0, H0, K0)
        grouped_phase(nc, banks, w, loads_c, 16 * (len((*wc, *cc)) + 1), load_last_ffn, between[1], between[2])
        ffn_phase(nc, "f1", banks, w1, loads_d, 16 * 5, between[2], out, E1, H1, K1)


def kernel(**inputs):
    import ml_dtypes
    import numpy as np
    import concourse.bacc as bacc
    from concourse.bass_utils import run_bass_kernel_spmd

    x = {k: np.asarray(v) for k, v in inputs.items()}
    f32, bf16 = np.float32, ml_dtypes.bfloat16

    def by_partition(m):
        return m.reshape(m.shape[0] // P, P, -1).transpose(1, 0, 2)

    def to_all(v):
        return np.broadcast_to(v, (P, v.shape[0]))

    def heads_apart(m):
        out = np.zeros((m.shape[0], LA_HEADS, 2 * LA_HD), m.dtype)
        out[:, :, 0:LA_HD] = m.reshape(m.shape[0], LA_HEADS, LA_HD)
        return out.reshape(m.shape[0], -1)

    def spread(experts, unit, hidden):
        s = np.zeros((3 * experts + 1, hidden), bf16)
        for e in range(experts):
            for part in range(3):
                s[part * experts + e, e * unit:(e + 1) * unit] = 1
        s[3 * experts, experts * unit:] = 1
        return s

    w, b = x["L0_attn_Wqkv"], x["L0_attn_bqkv"].reshape(1, -1)
    a = {"x": x["L0_attn_x"].reshape(NT, P, C).transpose(1, 0, 2)}
    a["wqk"] = by_partition(np.concatenate([heads_apart(w[:, 0:C]), heads_apart(w[:, C:2 * C])], 1))
    a["bqk"] = np.concatenate([heads_apart(b[:, 0:C]), heads_apart(b[:, C:2 * C])], 1).reshape(-1, P).T
    a["wv"], a["bv"] = by_partition(w[:, 2 * C:]), to_all(b[0, 2 * C:])
    a["wo"], a["bout"] = by_partition(x["L0_attn_Wout"]), to_all(x["L0_attn_bout"])
    a["slopes"] = to_all(x["L0_attn_slopes"])

    gu, down = x["L0_ffn_gate_up_proj"], x["L0_ffn_down_proj"]
    a["gate0"] = by_partition(gu[:, 0:I0].reshape(E0 * I0, C).T)
    a["up0"] = by_partition(gu[:, I0:].reshape(E0 * I0, C).T)
    a["down0"] = by_partition(down.transpose(0, 2, 1).reshape(E0 * I0, C))
    a["router0"] = by_partition(x["L0_ffn_gate_weight"].T)

    a["wq"], a["bq"] = by_partition(x["L1_attn_q_project"].T), x["L1_attn_q_bias"].reshape(HQ, HD).T
    a["wk"], a["bk"] = by_partition(x["L1_attn_k_project"].T), x["L1_attn_k_bias"].reshape(HKV, HD).T
    a["wv1"], a["bv1"] = by_partition(x["L1_attn_v_project"].T), to_all(x["L1_attn_v_bias"])
    a["wo1"] = by_partition(x["L1_attn_o_project"].T)
    a["ln_weight"] = x["L1_attn_ln_weight"].reshape(KT, P).T

    gu, shared = x["L1_ffn_w_gate_up"], x["L1_ffn_shared_gate_up"]
    a["gate1"] = by_partition(np.concatenate([gu[:, :, 0:I1].transpose(1, 0, 2).reshape(C, -1), shared[:, 0:S1]], 1))
    a["up1"] = by_partition(np.concatenate([gu[:, :, I1:].transpose(1, 0, 2).reshape(C, -1), shared[:, S1:]], 1))
    rows = E1 * I1 + S1
    down = np.zeros((-(-rows // P) * P, C), f32)
    down[0:E1 * I1] = x["L1_ffn_w_down"].reshape(-1, C)
    down[E1 * I1:rows] = x["L1_ffn_shared_down"]
    a["down1"] = by_partition(down)
    a["router1"] = by_partition(x["L1_ffn_gate_w"].T)

    key, query = np.arange(P)[:, None], np.arange(2 * P)[None, :]
    distance = np.maximum(query - key, 0).astype(f32)
    causal = (query >= key).astype(f32)
    a["distance"] = np.concatenate([distance, distance[:, 0:P]], 1)
    a["causal"] = np.concatenate([causal, causal[:, 0:P]], 1)
    a["minus_half"] = np.full((P, 8), -0.5, f32)
    a["ident"], a["ident_bf"] = np.eye(P, dtype=f32), np.eye(P, dtype=f32).astype(bf16)
    a["masked"] = np.where(np.arange(P)[:, None] >= np.arange(P)[None, :], 0.0, MASKED).astype(bf16)
    inv_freq = (f32(1.0) / f32(10000.0) ** (np.arange(0, HD, 2, dtype=f32) / f32(HD))).astype(f32)
    angle = (np.arange(2 * P, dtype=f32)[:, None] * inv_freq).astype(f32).T
    a["cos"] = np.concatenate([np.cos(angle), np.cos(angle)], 0)
    a["sin"] = np.concatenate([np.sin(angle), -np.sin(angle)], 0)
    a["spread0"], a["spread1"] = spread(E0, I0, E0 * I0), spread(E1, I1, E1 * I1 + S1)

    nc = bacc.Bacc("TRN2", target_bir_lowering=False, num_devices=1)
    arrays = {f"in_{k}": np.ascontiguousarray(v) for k, v in a.items()}
    aps = {k: nc.dram_tensor(f"in_{k}", v.shape, mybir.dt.from_np(v.dtype), kind="ExternalInput").ap()
           for k, v in ((k, arrays[f"in_{k}"]) for k in a)}
    out = nc.dram_tensor("out_x", (P, NT, C), F32, kind="ExternalOutput").ap()
    program(nc, aps, out)
    r = run_bass_kernel_spmd(nc, [arrays], core_ids=[0])
    y = r.results[0]["out_x"]
    return y.transpose(1, 0, 2).reshape(x["L0_attn_x"].shape)
```

```python
import concourse.bass as bass
from concourse import mybir
from contextlib import ExitStack

F32 = mybir.dt.float32
F32R = mybir.dt.float32r
BF16 = mybir.dt.bfloat16
ALU = mybir.AluOpType
ACT = mybir.ActivationFunctionType
AX = mybir.AxisListType

P = 128
C = 256
KT = C // P
NT = 32
LN_EPS = 1e-5
RMS_EPS = 1e-6
BANK = 512

LA_HEADS, LA_HD = 16, 16
HQ, HKV, HD = 16, 4, 128
E0, I0, K0 = 32, 96, 8
E1, I1, K1, S1 = 16, 176, 2, 352
THRESHOLD = 0.8
NOT_KEPT = -5.0
MASKED = -1e30


HALVES = ((0, 1), (1, 0), (0, 0))


class Chain:

    def __init__(self, eng, sem, per):
        self.eng, self.sem, self.per = eng, sem, per

    def start(self, step):
        self.base, self.n = step * self.per, 0

    def add(self, instruction):
        instruction.then_inc(self.sem, 1)
        self.n += 1

    def wait(self):
        self.eng.wait_ge(self.sem, self.base + self.n)

    def done(self):
        assert self.n == self.per, (self.n, self.per)


def move_x(sp, steps, tiles, src, dst, xin, xout, loaded, result_ready, results, stored, behind=None):

    def load(step, buf):
        sp.dma_start(xin[:, buf], src[:, bass.ds(step * tiles, tiles), :]).then_inc(loaded[buf], 16)

    def store(step, buf):
        sp.wait_ge(result_ready, results * (step + 1) + 1)
        sp.dma_start(dst[:, bass.ds(step * tiles, tiles), :], xout[:, buf]).then_inc(stored, 16)

    sp.sem_inc(result_ready, 1)
    sp.sem_inc(stored, 16)
    load(0, 0)
    load(1, 1)
    if behind is not None:
        behind(sp)
    with sp.Fori(0, steps // 2 - 1) as i:
        for u in range(2):
            store(2 * i + u, u)
            load(2 * i + u + 2, u)
    store(steps - 2, 0)
    load(0, 0)
    store(steps - 1, 1)
    sp.wait_ge(stored, 16 * (steps + 1))
    sp.wait_ge(loaded[0], 16 * (steps // 2 + 1))


def ffn_phase(nc, tag, banks, w, weights_loaded, weights_value, src, dst, experts, hidden, keep):
    T = 4
    TOK = T * P
    STEPS = NT // T
    NCH = -(-hidden // P)
    CR = 3 * experts + 1
    STATS, NORM, TR0, TR1, LOGITS = 0, 5, 7, 9, 11
    SHIFT, EXPS, PROBS, COMB, COMB_T = 12, 13, 14, 16, 20
    COPY0, COPY1, COPY_COMB = 8, 10, 21

    with ExitStack() as ctx:
        def sb(name, shape, dt=F32):
            return ctx.enter_context(nc.sbuf_tensor(f"{tag}_{name}", shape, dt))

        def sem(name):
            return ctx.enter_context(nc.semaphore(f"{tag}_{name}"))

        xin = sb("xin", [P, 2, T, C])
        xout = sb("xout", [P, 2, T, C])
        stats = sb("stats", [P, T, 6])
        mv = sb("mv", [P, T, 2])
        veps = sb("veps", [P, T])
        rstd = sb("rstd", [P, T])
        hn = sb("hn", [P, T, C])
        hT = [sb("hT_high", [P, 2, KT, TOK], F32R), sb("hT_low", [P, 2, KT, TOK], F32R)]
        raw = [w["router"], w["gate"], w["up"]]
        low = [w["router_low"], w["gate_low"], w["up_low"]]
        high = [sb("router_high", [P, KT, experts], F32R), sb("gate_high", [P, KT, hidden], F32R),
                sb("up_high", [P, KT, hidden], F32R)]
        router, gate, up = zip(high, low)
        combT = sb("combT", [CR, 2, TOK], BF16)
        silu = sb("silu", [P, 2, TOK])
        gated = sb("gated", [P, 2, TOK])
        h = sb("h", [P, 2, TOK])
        mx = sb("mx", [P, T])
        shifted = sb("shifted", [P, T, experts])
        expd = sb("expd", [P, T, experts])
        rsum = sb("rsum", [P, T])
        probs = sb("probs", [P, T, experts + 8])
        top = sb("top", [P, T, 8])
        cum = sb("cum", [P, 2, T, 8])
        active = sb("active", [P, T, 8])
        kept = sb("kept", [P, T, 8])
        found = sb("found", [P, T, 8])
        tsum = sb("tsum", [P, T])
        replaced = sb("replaced", [P, T, experts + 8])
        chosen = sb("chosen", [P, T, experts])
        comb = sb("comb", [P, T, experts])
        rest = sb("rest", [P, T, experts])
        parts = sb("parts", [P, T, CR], BF16)

        gate_banks, up_banks, comb_bank, y_banks, misc = banks[0:2], banks[2:4], banks[4], banks[5:7], banks[7]

        loaded = [sem("x_loaded_0"), sem("x_loaded_1")]
        stored = sem("x_stored")
        var_ready = sem("var_ready")
        pool_chain = sem("pool_chain")
        rstd_ready = sem("rstd_ready")
        look = sem("lookahead_chain")
        hn_ready = sem("hn_ready")
        misc_ready = sem("misc_ready")
        misc_copied = sem("misc_copied")
        shifted_ready = sem("shifted_ready")
        exp_ready = sem("exp_ready")
        parts_ready = sem("parts_ready")
        gate_ready = sem("gate_ready")
        silu_ready = sem("silu_ready")
        up_ready = sem("up_ready")
        gated_ready = sem("gated_ready")
        comb_ready = sem("comb_ready")
        h_ready = sem("h_ready")
        h_used = sem("h_used")
        result_ready = sem("result_ready")
        const_ready = sem("const_ready")
        high_ready = sem("high_ready")
        split_ready = sem("split_ready")
        hT_ready = sem("hT_ready")

        apart = sem("apart")

        block = ctx.enter_context(nc.Block())

        @block.sync
        def _(sp):
            move_x(sp, STEPS, T, src, dst, xin, xout, loaded, result_ready, 2, stored)

        @block.gpsimd
        def _(pool):
            def inverse_deviation(n):
                pool.wait_ge(var_ready, n + 1)
                pool.sem_inc(apart, 1)
                nc.gpsimd.tensor_scalar(veps[:], mv[:, :, 1], LN_EPS, None, ALU.add).then_inc(pool_chain, 1)
                pool.wait_ge(pool_chain, n + 1)
                nc.gpsimd.tensor_tensor(rstd[:], veps[:], w["minus_half"][:, 0:T], ALU.pow).then_inc(rstd_ready, 1)

            inverse_deviation(0)
            with pool.Fori(0, STEPS // 2) as i:
                for u in range(2):
                    inverse_deviation(2 * i + u + 1)

        @block.tensor
        def _(pe):
            def transposes(n, half):
                pe.wait_ge(hn_ready, T * n + 2 * half + 2)
                if half:
                    pe.wait_ge(hT_ready, 2 * n + 1)
                elif not (isinstance(n, int) and n == 0):
                    pe.wait_ge(misc_copied, 3 * n)
                out = misc[:].rearrange("p (k t) -> p k t", k=KT)
                for k in range(KT):
                    for j in range(2):
                        last = nc.tensor.transpose(out[:, k, j * P:(j + 1) * P], hn[:, 2 * half + j, k * P:(k + 1) * P],
                                                   w["ident"][:])
                last.then_inc(misc_ready, 1)

            def logits(n, b):
                pe.wait_ge(hT_ready, 2 * n + 2)
                for j in range(T):
                    products = [(k, a, c) for k in range(KT) for a, c in HALVES]
                    for k, a, c in products:
                        last = nc.tensor.matmul(misc[:, j * experts:(j + 1) * experts], hT[a][:, b, k, j * P:(j + 1) * P],
                                                router[c][:, k, :], start=((k, a, c) == products[0]),
                                                stop=((k, a, c) == products[-1]))
                last.then_inc(misc_ready, 1)

            def transpose_parts(n):
                pe.wait_ge(shifted_ready, n + 1)
                pe.wait_ge(parts_ready, n + 1)
                pe.sem_inc(apart, 1)
                for j in range(T):
                    last = nc.tensor.transpose(misc[:].bitcast(BF16)[0:CR, j * P:(j + 1) * P], parts[:, j, :],
                                               w["ident_bf"][:])
                last.then_inc(misc_ready, 1)

            def gate_up(f, b, r, j):
                m = min(P, hidden - j * P)
                for banks_of, free, ready, wt in ((gate_banks, silu_ready, gate_ready, gate),
                                                  (up_banks, gated_ready, up_ready, up)):
                    pe.wait_ge(free, f + 1)
                    products = [(k, a, c) for k in range(KT) for a, c in HALVES]
                    for k, a, c in products:
                        last = nc.tensor.matmul(banks_of[r][0:m], wt[a][:, k, j * P:j * P + m], hT[c][:, b, k, :],
                                                start=((k, a, c) == products[0]), stop=((k, a, c) == products[-1]))
                    last.then_inc(ready, 1)

            pe.sem_inc(silu_ready, 2)
            pe.sem_inc(gated_ready, 2)
            pe.sem_inc(h_used, 2)
            pe.sem_inc(h_ready, 1)
            transposes(0, 0)
            transposes(0, 1)
            pe.wait_ge(split_ready, len(raw))
            logits(0, 0)
            transpose_parts(0)
            gate_up(0, 0, 0, 0)
            with pe.Fori(0, STEPS // 2) as i:
                for u in range(2):
                    t = 2 * i + u
                    for j in range(NCH):
                        f, r = t * NCH + j, (u * NCH + j) % 2
                        m = min(P, hidden - j * P)
                        if j == 0:
                            pe.wait_ge(misc_copied, 3 * t + 3)
                        pe.wait_ge(h_ready, f + 1)
                        nc.tensor.matmul(comb_bank[0:m], w["spread"][0:CR, j * P:j * P + m], combT[:, u, :],
                                         start=True, stop=True).then_inc(comb_ready, 1)
                        if j < NCH - 1:
                            gate_up(f + 1, u, (r + 1) % 2, j + 1)
                        else:
                            gate_up(f + 1, 1 - u, (r + 1) % 2, 0)
                        if j == TR0:
                            transposes(t + 1, 0)
                        if j == TR1:
                            transposes(t + 1, 1)
                        if j == LOGITS:
                            logits(t + 1, 1 - u)
                        if j == COMB_T:
                            transpose_parts(t + 1)
                        pe.wait_ge(h_ready, f + 2)
                        if j == 0:
                            pe.wait_ge(result_ready, 2 * t + 1)
                        for k in range(T):
                            last = nc.tensor.matmul(y_banks[k // 2][:, (k % 2) * C:(k % 2 + 1) * C],
                                                    h[0:m, r, k * P:(k + 1) * P], w["down"][0:m, j, :],
                                                    start=(j == 0 and k % 2 == 0), stop=(j == NCH - 1),
                                                    skip_group_check=True)
                        last.then_inc(h_used, 1)

        @block.scalar
        def _(act):
            def copy_hT(n, b, half):
                act.wait_ge(misc_ready, 4 * n + half + 1)
                nc.scalar.copy(hT[0][:, b, :, half * 2 * P:(half + 1) * 2 * P],
                               misc[:].rearrange("p (k t) -> p k t", k=KT)).then_inc(misc_copied, 1)

            def exps(n):
                act.wait_ge(shifted_ready, n + 1)
                nc.scalar.activation(expd[:], shifted[:], ACT.Exp).then_inc(exp_ready, 1)

            def copy_combT(n, b):
                act.wait_ge(misc_ready, 4 * n + 4)
                nc.scalar.copy(combT[:, b], misc[:].bitcast(BF16)[0:CR, 0:TOK]).then_inc(misc_copied, 1)

            act.wait_ge(weights_loaded, weights_value)
            for held, whole in zip(high, raw):
                nc.scalar.copy(held[:], whole).then_inc(high_ready, 1)
            copy_hT(0, 0, 0)
            copy_hT(0, 0, 1)
            exps(0)
            copy_combT(0, 0)
            with act.Fori(0, STEPS // 2) as i:
                for u in range(2):
                    t, nb = 2 * i + u, 1 - u
                    for j in range(NCH):
                        f, r = t * NCH + j, (u * NCH + j) % 2
                        m = min(P, hidden - j * P)
                        act.wait_ge(gate_ready, f + 1)
                        act.wait_ge(gated_ready, f + 1)
                        nc.scalar.activation(silu[0:m, r], gate_banks[r][0:m], ACT.Silu).then_inc(silu_ready, 1)
                        if j == COPY0:
                            copy_hT(t + 1, nb, 0)
                        if j == COPY1:
                            copy_hT(t + 1, nb, 1)
                        if j == EXPS:
                            exps(t + 1)
                        if j == COPY_COMB:
                            copy_combT(t + 1, nb)

        @block.vector
        def _(dve):
            chain = Chain(dve, look, 4 * T + 8 + (18 if keep == 8 else 1))

            def statistics(n, b, before):
                dve.wait_ge(loaded[b], 16 * (before + 1))
                chain.start(n)
                for k in range(T):
                    chain.add(nc.vector.bn_stats(stats[:, k], xin[:, b, k]))
                chain.wait()
                dve.sem_inc(apart, 1)
                for k in range(T - 1):
                    chain.add(nc.vector.bn_aggr(mv[:, k], stats[:, k]))
                nc.vector.bn_aggr(mv[:, T - 1], stats[:, T - 1]).then_inc(var_ready, 1)

            def normalise(n, b):
                dve.wait_ge(rstd_ready, n + 1)
                for k in range(T):
                    nc.vector.tensor_scalar(hn[:, k], xin[:, b, k], mv[:, k, 0:1], rstd[:, k:k + 1],
                                            ALU.subtract, ALU.mult).then_inc(hn_ready, 1)

            def per_token(a, width):
                return a.unsqueeze(2).to_broadcast([P, T, width])

            def low_hT(n, b, half):
                dve.wait_ge(misc_copied, 3 * n + half + 1)
                at = slice(half * 2 * P, (half + 1) * 2 * P)
                nc.vector.tensor_tensor(hT[1][:, b, :, at], misc[:].rearrange("p (k t) -> p k t", k=KT),
                                        hT[0][:, b, :, at], ALU.subtract).then_inc(hT_ready, 1)

            def shift(n):
                logits = misc[:, 0:T * experts].rearrange("p (t e) -> p t e", t=T)
                dve.wait_ge(misc_ready, 4 * n + 3)
                chain.add(nc.vector.reduce_max(mx[:], logits, AX.X))
                chain.wait()
                nc.vector.tensor_tensor(shifted[:], logits, per_token(mx[:], experts), ALU.subtract).then_inc(shifted_ready, 1)

            def probabilities(n):
                dve.wait_ge(exp_ready, n + 1)
                chain.add(nc.vector.reduce_sum(rsum[:], expd[:], AX.X))
                chain.wait()
                chain.add(nc.vector.reciprocal(tsum[:], rsum[:]))
                chain.wait()
                chain.add(nc.vector.tensor_tensor(probs[:, :, 0:experts], expd[:], per_token(tsum[:], experts), ALU.mult))
                chain.wait()
                dve.sem_inc(apart, 1)
                for k in range(T):
                    chain.add(nc.vector.max(top[:, k], probs[:, k, 0:experts]))
                chain.wait()

            def keep_by_share():
                chain.add(nc.vector.reduce_sum(tsum[:], top[:], AX.X))
                chain.wait()
                chain.add(nc.vector.tensor_scalar(tsum[:], tsum[:], 1e-12, None, ALU.max))
                chain.wait()
                chain.add(nc.vector.reciprocal(rsum[:], tsum[:]))
                chain.wait()
                chain.add(nc.vector.tensor_tensor(cum[:, 0], top[:], per_token(rsum[:], 8), ALU.mult))
                chain.wait()
                a = 0
                for d in (1, 2, 4):
                    chain.add(nc.vector.tensor_copy(cum[:, 1 - a, :, 0:d], cum[:, a, :, 0:d]))
                    chain.add(nc.vector.tensor_tensor(cum[:, 1 - a, :, d:8], cum[:, a, :, d:8], cum[:, a, :, 0:8 - d], ALU.add))
                    chain.wait()
                    a = 1 - a
                chain.add(nc.vector.tensor_scalar(active[:, :, 1:8], cum[:, a, :, 0:7], THRESHOLD, None, ALU.is_lt))
                chain.wait()
                chain.add(nc.vector.tensor_tensor(kept[:], top[:], active[:], ALU.mult))
                chain.add(nc.vector.tensor_scalar(found[:], active[:], -NOT_KEPT, NOT_KEPT, ALU.mult, ALU.add))
                chain.wait()
                chain.add(nc.vector.tensor_tensor(found[:], found[:], kept[:], ALU.add))
                chain.add(nc.vector.reduce_sum(tsum[:], kept[:], AX.X))
                chain.wait()
                chain.add(nc.vector.tensor_scalar(tsum[:], tsum[:], 1e-12, None, ALU.max))
                chain.wait()
                chain.add(nc.vector.reciprocal(rsum[:], tsum[:]))

            def combine(n):
                if keep == 8:
                    keep_by_share()
                else:
                    chain.add(nc.vector.tensor_copy(found[:, :, 0:keep], top[:, :, 0:keep]))
                chain.wait()
                dve.sem_inc(apart, 1)
                for k in range(T):
                    chain.add(nc.vector.match_replace(replaced[:, k], found[:, k], probs[:, k], -9.0))
                chain.wait()
                chain.add(nc.vector.tensor_tensor(chosen[:], replaced[:, :, 0:experts], probs[:, :, 0:experts], ALU.not_equal))
                chain.wait()
                chain.add(nc.vector.tensor_tensor(comb[:], chosen[:], probs[:, :, 0:experts], ALU.mult))
                chain.wait()
                if keep == 8:
                    chain.add(nc.vector.tensor_tensor(comb[:], comb[:], per_token(rsum[:], experts), ALU.mult))
                    chain.wait()
                chain.add(nc.vector.tensor_copy(parts[:, :, 0:experts], comb[:]))
                chain.wait()
                chain.add(nc.vector.tensor_tensor(rest[:], comb[:], parts[:, :, 0:experts], ALU.subtract))
                chain.wait()
                chain.add(nc.vector.tensor_copy(parts[:, :, experts:2 * experts], rest[:]))
                chain.wait()
                nc.vector.tensor_tensor(parts[:, :, 2 * experts:3 * experts], rest[:], parts[:, :, experts:2 * experts],
                                        ALU.subtract).then_inc(parts_ready, 1)
                chain.done()

            nc.vector.memset(probs[:, :, experts:], NOT_KEPT).then_inc(const_ready, 1)
            nc.vector.memset(active[:], 1.0).then_inc(const_ready, 1)
            nc.vector.memset(found[:], NOT_KEPT).then_inc(const_ready, 1)
            nc.vector.memset(parts[:], 1.0).then_inc(const_ready, 1)
            dve.wait_ge(const_ready, 4)
            statistics(0, 0, 0)
            normalise(0, 0)
            for i, whole in enumerate(raw):
                dve.wait_ge(high_ready, i + 1)
                nc.vector.tensor_tensor(low[i], whole, high[i][:], ALU.subtract).then_inc(split_ready, 1)
            low_hT(0, 0, 0)
            low_hT(0, 0, 1)
            shift(0)
            probabilities(0)
            combine(0)
            with dve.Fori(0, STEPS // 2) as i:
                for u in range(2):
                    t, nb = 2 * i + u, 1 - u
                    for j in range(NCH):
                        f, r = t * NCH + j, (u * NCH + j) % 2
                        m = min(P, hidden - j * P)
                        dve.wait_ge(silu_ready, f + 3)
                        dve.wait_ge(up_ready, f + 1)
                        nc.vector.tensor_tensor(gated[0:m, r], silu[0:m, r], up_banks[r][0:m], ALU.mult).then_inc(gated_ready, 1)
                        dve.wait_ge(gated_ready, f + 3)
                        dve.wait_ge(comb_ready, f + 1)
                        dve.wait_ge(h_used, f + 1)
                        nc.vector.tensor_tensor(h[0:m, r], gated[0:m, r], comb_bank[0:m], ALU.mult).then_inc(h_ready, 1)
                        if j == STATS:
                            statistics(t + 1, nb, i + u)
                        if j == NORM:
                            normalise(t + 1, nb)
                        if j == COPY0:
                            low_hT(t + 1, nb, 0)
                        if j == COPY1:
                            low_hT(t + 1, nb, 1)
                        if j == SHIFT:
                            shift(t + 1)
                        if j == PROBS:
                            probabilities(t + 1)
                        if j == COMB:
                            combine(t + 1)
                    dve.wait_ge(h_used, (t + 1) * NCH + 2)
                    dve.wait_ge(stored, 16 * t + 16)
                    for half in range(2):
                        s = slice(2 * half, 2 * half + 2)
                        nc.vector.tensor_tensor(xout[:, u, s], y_banks[half][:].rearrange("p (t c) -> p t c", t=2),
                                                xin[:, u, s], ALU.add).then_inc(result_ready, 1)


def lightning_phase(nc, banks, w, weights_loaded, weights_value, src, dst):
    T = 2
    TOK = T * P
    STEPS = NT // T
    QC = C // P
    HPC = LA_HEADS // QC
    TRI = 3 * P
    RING = 4
    F_T, F_Q, F_K, F_OUT, F_V, FILLS = 0, 1, 2, 4, 5, 6
    PROLOGUE = 5
    STATS, NORM, TR = 0, 4, 8

    with ExitStack() as ctx:
        def sb(name, shape, dt=F32):
            return ctx.enter_context(nc.sbuf_tensor(f"la_{name}", shape, dt))

        def sem(name):
            return ctx.enter_context(nc.semaphore(f"la_{name}"))

        decay = sb("decay", [P, LA_HEADS, TRI])
        neg_slopes = sb("neg_slopes", [P, LA_HEADS])
        xin = sb("xin", [P, 2, T, C])
        xout = sb("xout", [P, 2, T, C])
        xb = sb("xb", [P, 2, T, C])
        stats = sb("stats", [P, T, 6])
        mv = sb("mv", [P, T, 2])
        veps = sb("veps", [P, T])
        rstd = sb("rstd", [P, T])
        hn = sb("hn", [P, T, C])
        hT = sb("hT", [P, KT, TOK])
        q = sb("q", [P, QC, TOK])
        kz = sb("kz", [P, LA_HEADS, TOK])
        vz = sb("vz", [P, T, QC, HPC * (P + LA_HD)])
        weighted = sb("weighted", [P, RING, TRI])
        oT = sb("oT", [P, KT, TOK])

        proj_banks, score_banks, o_banks = banks[0:2], banks[2:6], banks[6:8]

        loaded = [sem("x_loaded_0"), sem("x_loaded_1")]
        stored = sem("x_stored")
        slopes_ready = sem("slopes_ready")
        exp_ready = sem("exp_ready")
        decay_ready = sem("decay_ready")
        stats_chain = sem("stats_chain")
        var_ready = sem("var_ready")
        pool_chain = sem("pool_chain")
        rstd_ready = sem("rstd_ready")
        xb_ready = sem("xb_ready")
        hn_ready = sem("hn_ready")
        hT_ready = sem("hT_ready")
        proj_ready = sem("proj_ready")
        q_ready = sem("q_ready")
        k_ready = [sem("k_ready_0"), sem("k_ready_1")]
        v_ready = sem("v_ready")
        zeros_ready = sem("zeros_ready")
        scores_ready = sem("scores_ready")
        weighted_ready = sem("weighted_ready")
        head_done = sem("head_done")
        o_copied = sem("o_copied")
        result_ready = sem("result_ready")

        apart = sem("apart")

        block = ctx.enter_context(nc.Block())

        @block.sync
        def _(sp):
            move_x(sp, STEPS, T, src, dst, xin, xout, loaded, result_ready, 1, stored)

        @block.gpsimd
        def _(pool):
            def inverse_deviation(n):
                pool.wait_ge(var_ready, n + 1)
                pool.sem_inc(apart, 1)
                nc.gpsimd.tensor_scalar(veps[:], mv[:, :, 1], LN_EPS, None, ALU.add).then_inc(pool_chain, 1)
                pool.wait_ge(pool_chain, n + 1)
                nc.gpsimd.tensor_tensor(rstd[:], veps[:], w["minus_half"][:, 0:T], ALU.pow).then_inc(rstd_ready, 1)

            def add_bias(b, before):
                pool.wait_ge(loaded[b], 16 * (before + 1))
                nc.gpsimd.tensor_tensor(xb[:, b], xin[:, b], w["bout"][:].unsqueeze(1).to_broadcast([P, T, C]),
                                        ALU.add).then_inc(xb_ready, 1)

            pool.wait_ge(weights_loaded, weights_value)
            inverse_deviation(0)
            add_bias(0, 0)
            for hd in range(LA_HEADS):
                pool.wait_ge(exp_ready, hd + 1)
                nc.gpsimd.tensor_tensor(decay[:, hd], decay[:, hd], w["causal"][:], ALU.mult).then_inc(decay_ready, 1)
            with pool.Fori(0, STEPS // 2) as i:
                for u in range(2):
                    inverse_deviation(2 * i + u + 1)
                    pool.wait_ge(result_ready, 2 * i + u + 1)
                    add_bias(1 - u, i + u)

        @block.tensor
        def _(pe):
            def bank_free(loops, k):
                n = 0 if loops is None else loops + 1
                if k == F_T and loops is not None:
                    pe.wait_ge(result_ready, n)
                elif k == F_Q and loops is not None:
                    pe.wait_ge(v_ready, n)
                elif k == F_K:
                    pe.wait_ge(hT_ready, n + 1)
                elif k == F_K + 1:
                    pe.wait_ge(q_ready, n + 1)
                elif k > F_K + 1:
                    pe.wait_ge(k_ready[k - F_K - 2], HPC * (n + 1))

            def bank_of(loops, k):
                return proj_banks[((k if k < F_OUT else F_OUT) if loops is None else PROLOGUE + k) % 2]

            def transpose_hn(loops, n):
                pe.wait_ge(hn_ready, T * (n + 1))
                bank_free(loops, F_T)
                out = bank_of(loops, F_T)[:].rearrange("p (k t) -> p k t", k=KT)
                for k in range(KT):
                    for j in range(T):
                        last = nc.tensor.transpose(out[:, k, j * P:(j + 1) * P], hn[:, j, k * P:(k + 1) * P], w["ident"][:])
                last.then_inc(proj_ready, 1)

            def project_chunk(out, ch):
                for k in range(KT):
                    last = nc.tensor.matmul(out, w["wqk"][:, k, ch * P:(ch + 1) * P], hT[:, k, :],
                                            start=(k == 0), stop=(k == KT - 1))
                return last

            def project_qk(loops, n):
                pe.wait_ge(hT_ready, n + 1)
                bank_free(loops, F_Q)
                for ch in range(QC):
                    last = project_chunk(bank_of(loops, F_Q)[:, ch * TOK:(ch + 1) * TOK], ch)
                last.then_inc(proj_ready, 1)
                for ch in range(QC):
                    bank_free(loops, F_K + ch)
                    project_chunk(bank_of(loops, F_K + ch)[:, 0:TOK], QC + ch).then_inc(proj_ready, 1)

            def project_tokens(loops, fill, a, wt):
                bank_free(loops, fill if loops is not None else F_OUT)
                for j in range(T):
                    for k in range(KT):
                        last = nc.tensor.matmul(bank_of(loops, fill)[:, j * C:(j + 1) * C], a[:, k, j * P:(j + 1) * P],
                                                wt[:, k, :], start=(k == 0), stop=(k == KT - 1))
                last.then_inc(proj_ready, 1)

            def scores(g, hd):
                s, k, qc = score_banks[hd % RING], kz[:, hd], q[:, hd // HPC]
                pe.wait_ge(weighted_ready, g + 1)
                nc.tensor.matmul(s[:, 0:TOK], k[:, 0:P], qc[:, 0:TOK], start=True, stop=True)
                nc.tensor.matmul(s[:, TOK:TRI], k[:, P:TOK], qc[:, P:TOK], start=True, stop=True).then_inc(scores_ready, 1)

            def outputs(g, u, hd):
                a, ch, n = weighted[:, hd % RING], hd // HPC, hd % HPC
                out = o_banks[u][:, ch * TOK:(ch + 1) * TOK]
                pe.wait_ge(weighted_ready, g + 1 + RING)
                nc.tensor.matmul(out, vz[:, 0, ch, n * P:(n + 1) * P], a[:, 0:TOK], start=(n == 0), stop=False)
                nc.tensor.matmul(out[:, P:TOK], vz[:, 1, ch, n * P:(n + 1) * P], a[:, TOK:TRI], start=False,
                                 stop=(n == HPC - 1)).then_inc(head_done, 1)

            pe.sem_inc(weighted_ready, RING)
            pe.sem_inc(head_done, RING)
            pe.sem_inc(o_copied, 1)
            pe.wait_ge(weights_loaded, weights_value)
            transpose_hn(None, 0)
            project_qk(None, 0)
            project_tokens(None, F_V, hT, w["wv"])
            with pe.Fori(0, STEPS // 2) as i:
                for u in range(2):
                    t = 2 * i + u
                    pe.wait_ge(q_ready, t + 1)
                    pe.wait_ge(k_ready[0], HPC * (t + 1))
                    pe.wait_ge(o_copied, t + 1)
                    for s in range(LA_HEADS + 3):
                        if s == HPC:
                            pe.wait_ge(k_ready[1], HPC * (t + 1))
                        if s < LA_HEADS:
                            scores(t * LA_HEADS + s, s)
                        if s == TR:
                            transpose_hn(t, t + 1)
                        if s == 3:
                            pe.wait_ge(v_ready, t + 1)
                        if s >= 3:
                            outputs(t * LA_HEADS + s - 3, u, s - 3)
                    project_qk(t, t + 1)
                    pe.wait_ge(o_copied, t + 2)
                    project_tokens(t, F_OUT, oT, w["wo"])
                    project_tokens(t, F_V, hT, w["wv"])

        @block.scalar
        def _(act):
            def copy_hT(loops, first):
                act.wait_ge(proj_ready, loops * FILLS + first + 1)
                nc.scalar.copy(hT[:], proj_banks[first % 2][:].rearrange("p (k t) -> p k t", k=KT)).then_inc(hT_ready, 1)

            def copy_q(loops, first):
                f = first + F_Q
                act.wait_ge(proj_ready, loops * FILLS + f + 1)
                for ch in range(QC):
                    last = nc.scalar.activation(q[:, ch], proj_banks[f % 2][:, ch * TOK:(ch + 1) * TOK],
                                                ACT.Identity, bias=w["bq0"][:, ch:ch + 1])
                last.then_inc(q_ready, 1)

            def copy_k(loops, first):
                f = first + F_K
                act.wait_ge(proj_ready, loops * FILLS + f + 1)
                for n in range(HPC):
                    nc.scalar.activation(kz[:, n], proj_banks[f % 2][:, 0:TOK], ACT.Identity, bias=w["bkz"][:, n:n + 1],
                                         scale=w["own"][:, n:n + 1]).then_inc(k_ready[0], 1)

            act.wait_ge(weights_loaded, weights_value)
            nc.scalar.mul(neg_slopes[:], w["slopes"][:], -1.0).then_inc(slopes_ready, 1)
            act.wait_ge(slopes_ready, 1)
            for hd in range(LA_HEADS):
                nc.scalar.activation(decay[:, hd], w["distance"][:], ACT.Exp, scale=neg_slopes[:, hd:hd + 1]).then_inc(exp_ready, 1)
            copy_hT(0, 0)
            copy_q(0, 0)
            copy_k(0, 0)
            with act.Fori(0, STEPS // 2) as i:
                for u in range(2):
                    t = 2 * i + u
                    copy_hT(t, PROLOGUE)
                    act.wait_ge(head_done, (t + 1) * LA_HEADS + RING)
                    nc.scalar.copy(oT[:], o_banks[u][:].rearrange("p (k t) -> p k t", k=KT)).then_inc(o_copied, 1)
                    copy_q(t, PROLOGUE)
                    copy_k(t, PROLOGUE)

        @block.vector
        def _(dve):
            chain = Chain(dve, stats_chain, 2 * T - 1)

            def statistics(n, b, before):
                dve.wait_ge(loaded[b], 16 * (before + 1))
                chain.start(n)
                for k in range(T):
                    chain.add(nc.vector.bn_stats(stats[:, k], xin[:, b, k]))
                chain.wait()
                dve.sem_inc(apart, 1)
                for k in range(T - 1):
                    chain.add(nc.vector.bn_aggr(mv[:, k], stats[:, k]))
                nc.vector.bn_aggr(mv[:, T - 1], stats[:, T - 1]).then_inc(var_ready, 1)
                chain.done()

            def normalise(n, b):
                dve.wait_ge(rstd_ready, n + 1)
                for k in range(T):
                    nc.vector.tensor_scalar(hn[:, k], xin[:, b, k], mv[:, k, 0:1], rstd[:, k:k + 1],
                                            ALU.subtract, ALU.mult).then_inc(hn_ready, 1)

            def copy_k(loops, first):
                f = first + F_K + 1
                dve.wait_ge(proj_ready, loops * FILLS + f + 1)
                for n in range(HPC):
                    nc.vector.tensor_scalar(kz[:, HPC + n], proj_banks[f % 2][:, 0:TOK], w["own"][:, n:n + 1],
                                            w["bkz"][:, HPC + n:HPC + n + 1], ALU.mult, ALU.add).then_inc(k_ready[1], 1)

            def copy_v(loops, f):
                dve.wait_ge(proj_ready, loops * FILLS + f + 1)
                for j in range(T):
                    last = nc.vector.tensor_tensor(
                        vz[:, j].rearrange("p c (n s) -> p c n s", s=P + LA_HD)[:, :, :, 0:LA_HD],
                        proj_banks[f % 2][:, j * C:(j + 1) * C].rearrange("p (c n d) -> p c n d", c=QC, d=LA_HD),
                        w["bv"][:].rearrange("p (c n d) -> p c n d", c=QC, d=LA_HD), ALU.add)
                last.then_inc(v_ready, 1)

            nc.vector.memset(vz[:], 0.0).then_inc(zeros_ready, 1)
            dve.wait_ge(weights_loaded, weights_value)
            statistics(0, 0, 0)
            normalise(0, 0)
            dve.wait_ge(zeros_ready, 1)
            copy_k(0, 0)
            copy_v(0, PROLOGUE - 1)
            with dve.Fori(0, STEPS // 2) as i:
                for u in range(2):
                    t = 2 * i + u
                    for s in range(LA_HEADS):
                        g = t * LA_HEADS + s
                        if u == 0:
                            dve.wait_ge(decay_ready, s + 1)
                        dve.wait_ge(scores_ready, g + 1)
                        dve.wait_ge(head_done, g + 1)
                        nc.vector.tensor_tensor(weighted[:, s % RING], score_banks[s % RING][:, 0:TRI], decay[:, s],
                                                ALU.mult).then_inc(weighted_ready, 1)
                        if s == STATS:
                            statistics(t + 1, 1 - u, i + u)
                        if s == NORM:
                            normalise(t + 1, 1 - u)
                    copy_k(t, PROLOGUE)
                    f = PROLOGUE + F_OUT
                    dve.wait_ge(proj_ready, t * FILLS + f + 1)
                    dve.wait_ge(stored, 16 * t + 16)
                    dve.wait_ge(xb_ready, t + 1)
                    nc.vector.tensor_tensor(xout[:, u], proj_banks[f % 2][:].rearrange("p (j c) -> p j c", j=T),
                                            xb[:, u], ALU.add).then_inc(result_ready, 1)
                    copy_v(t, PROLOGUE + F_V)


def grouped_phase(nc, banks, w, weights_loaded, weights_value, next_weights, src, dst):
    T = 2
    TOK = T * P
    STEPS = NT // T
    GROUP = HQ // HKV
    PAIRS = HQ // 2
    TRI = 3 * P
    RING = 4
    SCALE = HD ** -0.5
    PROLOGUE = 3 + 2 + 2
    F_T, F_K, F_Q, F_V, F_OUT = 6, 7, 9, 11, 13
    FILLS = 14
    ROPE_PROLOGUE, ROPES = 4, 10
    STATS, NORM = 5, 9

    with ExitStack() as ctx:
        def sb(name, shape, dt=F32):
            return ctx.enter_context(nc.sbuf_tensor(f"ga_{name}", shape, dt))

        def sem(name):
            return ctx.enter_context(nc.semaphore(f"ga_{name}"))

        xin = sb("xin", [P, 2, T, C])
        xout = sb("xout", [P, 2, T, C])
        stats = sb("stats", [P, T, 6])
        mv = sb("mv", [P, T, 2])
        small = sb("small", [P, 6, T])
        rstd = sb("rstd", [P, T])
        hn = sb("hn", [P, T, C])
        hT = sb("hT", [P, KT, TOK])
        raw = sb("raw", [P, 2, 2, TOK])
        by_cos = sb("by_cos", [P, 2, 2, TOK])
        by_sin = sb("by_sin", [P, 2, TOK])
        q = sb("q", [P, 4, 2, TOK])
        kr = sb("kr", [P, HKV, TOK])
        v = sb("v", [P, T, HKV * HD])
        top = sb("top", [P, RING, 2])
        bias = sb("bias", [P, RING, 2])
        rsum = sb("rsum", [P, RING, 2])
        rinv = sb("rinv", [P, RING, 2])
        probs = sb("probs", [P, RING, TRI])
        probsT = sb("probsT", [P, 2, TRI])
        attn = sb("attn", [P, HQ, TOK])

        proj_banks, score_banks, pt_banks, attn_banks = banks[0:2], banks[2:4], banks[4:6], banks[6:8]

        loaded = [sem("x_loaded_0"), sem("x_loaded_1")]
        stored = sem("x_stored")
        stats_chain = sem("stats_chain")
        var_ready = sem("var_ready")
        pool_chain = sem("pool_chain")
        rstd_ready = sem("rstd_ready")
        hn_ready = sem("hn_ready")
        proj_ready = sem("proj_ready")
        hT_ready = sem("hT_ready")
        raw_ready = sem("raw_ready")
        v_ready = sem("v_ready")
        cos_ready = sem("cos_ready")
        sin_ready = sem("sin_ready")
        roped = sem("roped")
        scores_ready = sem("scores_ready")
        max_chain = sem("max_chain")
        bias_ready = sem("bias_ready")
        exp_ready = sem("exp_ready")
        rinv_ready = sem("rinv_ready")
        probs_ready = sem("probs_ready")
        pt_ready = sem("pt_ready")
        pt_copied = sem("pt_copied")
        attn_ready = sem("attn_ready")
        attn_copied = sem("attn_copied")
        result_ready = sem("result_ready")

        apart = sem("apart")

        block = ctx.enter_context(nc.Block())

        @block.sync
        def _(sp):
            move_x(sp, STEPS, T, src, dst, xin, xout, loaded, result_ready, 1, stored, next_weights)

        @block.gpsimd
        def _(pool):
            steps = Chain(pool, pool_chain, 6)

            def inverse_deviation(n):
                pool.wait_ge(var_ready, n + 1)
                pool.sem_inc(apart, 1)
                var = mv[:, :, 1]
                steps.start(n)
                steps.add(nc.gpsimd.tensor_scalar(small[:, 0], var, LN_EPS, None, ALU.add))
                steps.wait()
                steps.add(nc.gpsimd.tensor_tensor(small[:, 1], small[:, 0], w["minus_half"][:, 0:T], ALU.pow))
                steps.wait()
                steps.add(nc.gpsimd.tensor_tensor(small[:, 2], small[:, 1], small[:, 1], ALU.mult))
                steps.wait()
                steps.add(nc.gpsimd.tensor_tensor(small[:, 3], small[:, 2], var, ALU.mult))
                steps.wait()
                pool.sem_inc(apart, 1)
                steps.add(nc.gpsimd.tensor_scalar(small[:, 4], small[:, 3], RMS_EPS, None, ALU.add))
                steps.wait()
                steps.add(nc.gpsimd.tensor_tensor(small[:, 5], small[:, 4], w["minus_half"][:, 0:T], ALU.pow))
                steps.wait()
                nc.gpsimd.tensor_tensor(rstd[:], small[:, 5], small[:, 1], ALU.mult).then_inc(rstd_ready, 1)
                steps.done()

            def cosine(loops, k):
                r = k % 2
                pool.wait_ge(raw_ready, loops * ROPES + k + 1)
                if isinstance(loops, int) and k < 2:
                    pass
                else:
                    pool.wait_ge(roped, loops * ROPES + k - 1)
                nc.gpsimd.tensor_tensor(by_cos[:, r], raw[:, r], w["cos"][:].unsqueeze(1).to_broadcast([P, 2, TOK]),
                                        ALU.mult).then_inc(cos_ready, 1)

            pool.wait_ge(weights_loaded, weights_value)
            inverse_deviation(0)
            for k in range(ROPE_PROLOGUE):
                cosine(0, k)
            with pool.Fori(0, STEPS // 2) as i:
                for u in range(2):
                    t = 2 * i + u
                    for s in range(HQ):
                        if s % 2 == 0 and s // 2 < PAIRS - 2:
                            cosine(t, ROPE_PROLOGUE + s // 2)
                        if s == STATS:
                            inverse_deviation(t + 1)
                    for k in range(4):
                        cosine(t, ROPE_PROLOGUE + PAIRS - 2 + k)

        @block.tensor
        def _(pe):
            def bank_free(loops, f):
                if loops is None:
                    if f >= 2:
                        pe.wait_ge(*((hT_ready, 1), (raw_ready, 1), (raw_ready, 2), (raw_ready, 3), (raw_ready, 4))[f - 2])
                    return
                k = f - PROLOGUE - 2
                if k == -2:
                    pe.wait_ge(v_ready, 2 * (loops + 1))
                elif k == -1:
                    pe.wait_ge(result_ready, loops + 1)
                elif k < F_T:
                    pe.wait_ge(raw_ready, loops * ROPES + ROPE_PROLOGUE + k + 1)
                elif k == F_T:
                    pe.wait_ge(hT_ready, loops + 2)
                elif k < F_V:
                    pe.wait_ge(raw_ready, loops * ROPES + ROPE_PROLOGUE + k)
                else:
                    pe.wait_ge(v_ready, 2 * loops + 3 + k - F_V)

            def transpose_hn(loops, f, n):
                pe.wait_ge(hn_ready, T * (n + 1))
                bank_free(loops, f)
                out = proj_banks[f % 2][:].rearrange("p (k t) -> p k t", k=KT)
                for k in range(KT):
                    for j in range(T):
                        last = nc.tensor.transpose(out[:, k, j * P:(j + 1) * P], hn[:, j, k * P:(k + 1) * P], w["ident"][:])
                last.then_inc(proj_ready, 1)

            def project(loops, f, wt, pair):
                bank_free(loops, f)
                for c in range(2):
                    ch = 2 * pair + c
                    for k in range(KT):
                        last = nc.tensor.matmul(proj_banks[f % 2][:, c * TOK:(c + 1) * TOK], wt[:, k, ch * HD:(ch + 1) * HD],
                                                hT[:, k, :], start=(k == 0), stop=(k == KT - 1))
                last.then_inc(proj_ready, 1)

            def project_v(loops, f, j):
                bank_free(loops, f)
                for k in range(KT):
                    last = nc.tensor.matmul(proj_banks[f % 2][:], hT[:, k, j * P:(j + 1) * P], w["wv1"][:, k, :],
                                            start=(k == 0), stop=(k == KT - 1))
                last.then_inc(proj_ready, 1)

            def scores(g, hd):
                s, kv = score_banks[hd % 2], kr[:, hd // GROUP]
                qh = q[:, (hd // 2) % 4, hd % 2]
                pe.wait_ge(exp_ready, g + 1)
                for tile, c0, keys in ((0, 0, P), (1, P, TOK)):
                    nc.tensor.matmul(s[:, c0:c0 + keys], qh[:, tile * P:(tile + 1) * P], kv[:, 0:keys], start=True, stop=False)
                    last = nc.tensor.matmul(s[:, c0 + keys - P:c0 + keys], w["ident_bf"][:], w["masked"][:],
                                            start=False, stop=True)
                last.then_inc(scores_ready, 1)

            def transpose_probs(g, hd):
                pe.wait_ge(probs_ready, g + 1)
                pe.wait_ge(pt_copied, g + 1)
                for blk in range(3):
                    last = nc.tensor.transpose(pt_banks[hd % 2][:, blk * P:(blk + 1) * P],
                                               probs[:, hd % RING, blk * P:(blk + 1) * P], w["ident"][:])
                last.then_inc(pt_ready, 1)

            def attend(g, t, hd):
                out = attn_banks[(hd // 2) % 2][:, (hd % 2) * TOK:(hd % 2 + 1) * TOK]
                cols = slice((hd // GROUP) * HD, (hd // GROUP + 1) * HD)
                pe.wait_ge(pt_copied, g + 3)
                if hd == 0:
                    pe.wait_ge(v_ready, 2 * (t + 1))
                if hd % 2 == 0:
                    pe.wait_ge(attn_copied, t * PAIRS + hd // 2 + 1)
                nc.tensor.matmul(out, v[:, 0, cols], probsT[:, hd % 2, 0:TOK], start=True, stop=False)
                nc.tensor.matmul(out[:, P:TOK], v[:, 1, cols], probsT[:, hd % 2, TOK:TRI], start=False,
                                 stop=True).then_inc(attn_ready, 1)

            def project_out(t):
                f = PROLOGUE + F_OUT
                pe.wait_ge(attn_copied, (t + 1) * PAIRS + 2)
                bank_free(t, f)
                for j in range(T):
                    for hd in range(HQ):
                        last = nc.tensor.matmul(proj_banks[f % 2][:, j * C:(j + 1) * C], attn[:, hd, j * P:(j + 1) * P],
                                                w["wo1"][:, hd, :], start=(hd == 0), stop=(hd == HQ - 1))
                last.then_inc(proj_ready, 1)

            pe.sem_inc(exp_ready, 2)
            pe.sem_inc(pt_copied, 2)
            pe.sem_inc(attn_ready, 2)
            pe.sem_inc(attn_copied, 2)
            pe.wait_ge(weights_loaded, weights_value)
            transpose_hn(None, 0, 0)
            pe.wait_ge(hT_ready, 1)
            project(None, 1, w["wk"], 0)
            project(None, 2, w["wk"], 1)
            project(None, 3, w["wq"], 0)
            project(None, 4, w["wq"], 1)
            project_v(None, 5, 0)
            project_v(None, 6, 1)
            with pe.Fori(0, STEPS // 2) as i:
                for u in range(2):
                    t = 2 * i + u
                    for s in range(HQ + 4):
                        if 3 <= s < HQ + 3:
                            transpose_probs(t * HQ + s - 3, s - 3)
                        if s < HQ:
                            if s == 0:
                                pe.wait_ge(roped, t * ROPES + ROPE_PROLOGUE - 1)
                            elif s == 2:
                                pe.wait_ge(roped, t * ROPES + ROPE_PROLOGUE)
                            elif s % 2 == 0:
                                pe.wait_ge(roped, t * ROPES + ROPE_PROLOGUE + s // 2 - 1)
                            scores(t * HQ + s, s)
                        if s % 2 == 0 and s // 2 < PAIRS - 2:
                            project(t, PROLOGUE + s // 2, w["wq"], 2 + s // 2)
                        if s == HQ - 4:
                            transpose_hn(t, PROLOGUE + F_T, t + 1)
                        if s == HQ:
                            pe.wait_ge(hT_ready, t + 2)
                            project(t, PROLOGUE + F_K, w["wk"], 0)
                        if s == HQ + 1:
                            project(t, PROLOGUE + F_K + 1, w["wk"], 1)
                        if s == HQ + 2:
                            project(t, PROLOGUE + F_Q, w["wq"], 0)
                        if s == HQ + 3:
                            project(t, PROLOGUE + F_Q + 1, w["wq"], 1)
                        if s >= 4:
                            attend(t * HQ + s - 4, t, s - 4)
                    project_v(t, PROLOGUE + F_V, 0)
                    project_v(t, PROLOGUE + F_V + 1, 1)
                    project_out(t)

        @block.scalar
        def _(act):
            def copy_hT(loops, f):
                act.wait_ge(proj_ready, loops * FILLS + f + 1)
                for k in range(KT):
                    last = nc.scalar.activation(hT[:, k], proj_banks[f % 2][:, k * TOK:(k + 1) * TOK], ACT.Identity,
                                                scale=w["ln_weight"][:, k:k + 1])
                last.then_inc(hT_ready, 1)

            def copy_raw(loops, f, rope, biases, pair):
                act.wait_ge(proj_ready, loops * FILLS + f + 1)
                if not (isinstance(loops, int) and rope < 2):
                    act.wait_ge(roped, loops * ROPES + rope - 1)
                for c in range(2):
                    ch = 2 * pair + c
                    last = nc.scalar.activation(raw[:, rope % 2, c], proj_banks[f % 2][:, c * TOK:(c + 1) * TOK],
                                                ACT.Identity, bias=biases[:, ch:ch + 1])
                last.then_inc(raw_ready, 1)

            def exps(g, hd):
                r, s = hd % RING, score_banks[hd % 2]
                act.wait_ge(bias_ready, g + 1)
                for tile, c in ((0, slice(0, P)), (1, slice(P, TRI))):
                    last = nc.scalar.activation(probs[:, r, c], s[:, c], ACT.Exp, bias=bias[:, r, tile:tile + 1],
                                                scale=SCALE, accum_out=rsum[:, r, tile:tile + 1])
                last.then_inc(exp_ready, 1)

            def copy_probsT(g, hd):
                act.wait_ge(pt_ready, g + 1)
                act.wait_ge(attn_ready, g + 1)
                nc.scalar.copy(probsT[:, hd % 2], pt_banks[hd % 2][:, 0:TRI]).then_inc(pt_copied, 1)

            def copy_attn(t, pair):
                act.wait_ge(attn_ready, t * HQ + 2 * pair + 4)
                nc.scalar.copy(attn[:, 2 * pair:2 * pair + 2], attn_banks[pair % 2][:].rearrange("p (h t) -> p h t", h=2)).then_inc(attn_copied, 1)

            act.wait_ge(weights_loaded, weights_value)
            copy_hT(0, 0)
            copy_raw(0, 1, 0, w["bk"], 0)
            copy_raw(0, 2, 1, w["bk"], 1)
            copy_raw(0, 3, 2, w["bq"], 0)
            copy_raw(0, 4, 3, w["bq"], 1)
            with act.Fori(0, STEPS // 2) as i:
                for u in range(2):
                    t = 2 * i + u
                    for s in range(HQ + 5):
                        if 3 <= s < HQ + 3:
                            copy_probsT(t * HQ + s - 3, s - 3)
                        if s >= 6 and s % 2 == 0:
                            copy_attn(t, (s - 6) // 2)
                        if s < HQ:
                            exps(t * HQ + s, s)
                        if s % 2 == 0 and s // 2 < PAIRS - 2:
                            copy_raw(t, PROLOGUE + s // 2, ROPE_PROLOGUE + s // 2, w["bq"], 2 + s // 2)
                        if s == HQ - 4:
                            copy_hT(t, PROLOGUE + F_T)
                        if s == HQ:
                            copy_raw(t, PROLOGUE + F_K, ROPE_PROLOGUE + PAIRS - 2, w["bk"], 0)
                        if s == HQ + 1:
                            copy_raw(t, PROLOGUE + F_K + 1, ROPE_PROLOGUE + PAIRS - 1, w["bk"], 1)
                        if s == HQ + 2:
                            copy_raw(t, PROLOGUE + F_Q, ROPE_PROLOGUE + PAIRS, w["bq"], 0)
                        if s == HQ + 3:
                            copy_raw(t, PROLOGUE + F_Q + 1, ROPE_PROLOGUE + PAIRS + 1, w["bq"], 1)

        @block.vector
        def _(dve):
            chain = Chain(dve, stats_chain, 2 * T - 1)

            def statistics(n, b, before):
                dve.wait_ge(loaded[b], 16 * (before + 1))
                chain.start(n)
                for k in range(T):
                    chain.add(nc.vector.bn_stats(stats[:, k], xin[:, b, k]))
                chain.wait()
                dve.sem_inc(apart, 1)
                for k in range(T - 1):
                    chain.add(nc.vector.bn_aggr(mv[:, k], stats[:, k]))
                nc.vector.bn_aggr(mv[:, T - 1], stats[:, T - 1]).then_inc(var_ready, 1)
                chain.done()

            def normalise(n, b):
                dve.wait_ge(rstd_ready, n + 1)
                for k in range(T):
                    nc.vector.tensor_scalar(hn[:, k], xin[:, b, k], mv[:, k, 0:1], rstd[:, k:k + 1],
                                            ALU.subtract, ALU.mult).then_inc(hn_ready, 1)

            def rope(loops, k, out):
                r, half = k % 2, HD // 2
                dve.wait_ge(raw_ready, loops * ROPES + k + 1)
                if not (isinstance(loops, int) and k == 0):
                    dve.wait_ge(roped, loops * ROPES + k)
                for d in range(2):
                    frm, to = slice((1 - d) * half, (2 - d) * half), slice(d * half, (d + 1) * half)
                    last = nc.vector.tensor_tensor(by_sin[to], raw[frm, r], w["sin"][frm].unsqueeze(1).to_broadcast([half, 2, TOK]),
                                                   ALU.mult)
                last.then_inc(sin_ready, 1)
                dve.wait_ge(sin_ready, loops * ROPES + k + 1)
                dve.wait_ge(cos_ready, loops * ROPES + k + 1)
                nc.vector.tensor_tensor(out, by_cos[:, r], by_sin[:], ALU.add).then_inc(roped, 1)

            def copy_v(loops, f, j):
                dve.wait_ge(proj_ready, loops * FILLS + f + 1)
                nc.vector.tensor_tensor(v[:, j], proj_banks[f % 2][:], w["bv1"][:], ALU.add).then_inc(v_ready, 1)

            def maximum(g, hd):
                r, s = hd % RING, score_banks[hd % 2]
                dve.wait_ge(scores_ready, g + 1)
                nc.vector.reduce_max(top[:, r, 0:1], s[:, 0:P], AX.X)
                nc.vector.reduce_max(top[:, r, 1:2], s[:, P:TRI], AX.X).then_inc(max_chain, 1)
                dve.wait_ge(max_chain, g + 1)
                nc.vector.tensor_scalar(bias[:, r], top[:, r], -SCALE, None, ALU.mult).then_inc(bias_ready, 1)

            def divide_by_sum(g, hd):
                r = hd % RING
                dve.wait_ge(exp_ready, g + 3)
                nc.vector.reciprocal(rinv[:, r], rsum[:, r]).then_inc(rinv_ready, 1)
                dve.wait_ge(rinv_ready, g + 1)
                for tile, cols in ((0, slice(0, P)), (1, slice(P, TRI))):
                    last = nc.vector.tensor_scalar(probs[:, r, cols], probs[:, r, cols], rinv[:, r, tile:tile + 1], None, ALU.mult)
                last.then_inc(probs_ready, 1)

            dve.wait_ge(weights_loaded, weights_value)
            statistics(0, 0, 0)
            normalise(0, 0)
            rope(0, 0, kr[:, 0:2])
            rope(0, 1, kr[:, 2:4])
            rope(0, 2, q[:, 0])
            rope(0, 3, q[:, 1])
            copy_v(0, 5, 0)
            copy_v(0, 6, 1)
            with dve.Fori(0, STEPS // 2) as i:
                for u in range(2):
                    t = 2 * i + u
                    for s in range(HQ + 1):
                        if s < HQ:
                            maximum(t * HQ + s, s)
                        if s >= 1:
                            divide_by_sum(t * HQ + s - 1, s - 1)
                        if s % 2 == 0 and s // 2 < PAIRS - 2:
                            rope(t, ROPE_PROLOGUE + s // 2, q[:, (2 + s // 2) % 4])
                        if s == STATS:
                            statistics(t + 1, 1 - u, i + u)
                        if s == NORM:
                            normalise(t + 1, 1 - u)
                    rope(t, ROPE_PROLOGUE + PAIRS - 2, kr[:, 0:2])
                    rope(t, ROPE_PROLOGUE + PAIRS - 1, kr[:, 2:4])
                    rope(t, ROPE_PROLOGUE + PAIRS, q[:, 0])
                    rope(t, ROPE_PROLOGUE + PAIRS + 1, q[:, 1])
                    copy_v(t, PROLOGUE + F_V, 0)
                    copy_v(t, PROLOGUE + F_V + 1, 1)
                    f = PROLOGUE + F_OUT
                    dve.wait_ge(proj_ready, t * FILLS + f + 1)
                    dve.wait_ge(stored, 16 * t + 16)
                    nc.vector.tensor_tensor(xout[:, u], proj_banks[f % 2][:].rearrange("p (j c) -> p j c", j=T),
                                            xin[:, u], ALU.add).then_inc(result_ready, 1)


def program(nc, a, out):
    with ExitStack() as ctx:
        def sb(name, shape, dt=F32):
            return ctx.enter_context(nc.sbuf_tensor(name, shape, dt))

        banks = [ctx.enter_context(nc.psum_tensor(f"bank{i}", [P, BANK], F32)) for i in range(8)]
        between = [nc.dram_tensor(f"x_after_{i}", (P, NT, C), F32, kind="Internal").ap() for i in range(3)]
        H0, H1 = E0 * I0, E1 * I1 + S1
        CH0, CH1 = -(-H0 // P), -(-H1 // P)
        wa = {"wqk": [P, KT, 2 * C], "wv": [P, KT, C], "wo": [P, KT, C], "bq0": [P, KT], "bkz": [P, LA_HEADS], "own": [P, P // LA_HD], "bv": [P, C], "bout": [P, C],
              "slopes": [P, LA_HEADS], "distance": [P, 3 * P], "causal": [P, 3 * P]}
        wc = {"wq": [P, KT, HQ * HD], "wk": [P, KT, HKV * HD], "wv1": [P, KT, HKV * HD], "wo1": [P, HQ, C],
              "bq": [P, HQ], "bk": [P, HKV], "bv1": [P, HKV * HD], "ln_weight": [P, KT]}
        ca = {"ident": [P, P], "minus_half": [P, 8]}
        cc = {"cos": [P, 2 * P], "sin": [P, 2 * P]}
        w = {name: sb(name, shape) for name, shape in ca.items()}
        w["ident_bf"] = sb("ident_bf", [P, P], BF16)
        whole_shapes = {"gate": [P, KT, H1], "up": [P, KT, H1], "router": [P, KT, E0 + E1]}
        with ExitStack() as place:
            gate, up, router = (place.enter_context(nc.sbuf_tensor(name, shape, F32))
                                for name, shape in whole_shapes.items())
        gate_low, up_low, router_low = (sb(f"{name}_low", shape, F32R) for name, shape in whole_shapes.items())
        down = sb("down", [P, CH1, C])
        spread = sb("spread", [3 * E0 + 1, H1], BF16)
        w0 = dict(w, gate=gate[:, :, 0:H0], up=up[:, :, 0:H0], router=router[:, :, 0:E0],
                  gate_low=gate_low[:, :, 0:H0], up_low=up_low[:, :, 0:H0], router_low=router_low[:, :, 0:E0],
                  down=down[:, 0:CH0], spread=spread)
        w1 = dict(w, gate=gate[:], up=up[:], router=router[:, :, E0:E0 + E1],
                  gate_low=gate_low[:], up_low=up_low[:], router_low=router_low[:, :, E0:E0 + E1],
                  down=down, spread=spread)

        loads_a = ctx.enter_context(nc.semaphore("weights_a"))
        loads_b = ctx.enter_context(nc.semaphore("weights_b"))
        loads_c = ctx.enter_context(nc.semaphore("weights_c"))
        loads_d = ctx.enter_context(nc.semaphore("weights_d"))

        def load_ffn(q, sem, n, h, chunks, rows):
            q.dma_start(gate[:, :, 0:h], a[f"gate{n}"]).then_inc(sem, 16)
            q.dma_start(up[:, :, 0:h], a[f"up{n}"]).then_inc(sem, 16)
            q.dma_start(down[:, 0:chunks], a[f"down{n}"]).then_inc(sem, 16)
            q.dma_start(router[:, :, n * E0:n * E0 + (E0, E1)[n]], a[f"router{n}"]).then_inc(sem, 16)
            q.dma_start(spread[0:rows, 0:h], a[f"spread{n}"]).then_inc(sem, 16)

        with ExitStack() as first:
            wl = {name: first.enter_context(nc.sbuf_tensor(name, shape, F32)) for name, shape in wa.items()}
            with nc.Block() as block:
                @block.sync
                def _(sp):
                    for name in (*ca, *wa):
                        sp.dma_start((wl | w)[name][:], a[name]).then_inc(loads_a, 16)

                @block.scalar
                def _(act):
                    act.wait_ge(loads_a, 16 * len((*ca, *wa)))
                    act.dma_start(w["ident_bf"][:], a["ident_bf"]).then_inc(loads_b, 16)
                    load_ffn(act, loads_b, 0, H0, CH0, 3 * E0 + 1)

            lightning_phase(nc, banks, wl | w, loads_a, 16 * len((*ca, *wa)), a["x"], between[0])

        ffn_phase(nc, "f0", banks, w0, loads_b, 16 * 6, between[0], between[1], E0, H0, K0)

        with ExitStack() as third:
            wg = {name: third.enter_context(nc.sbuf_tensor(name, shape, F32))
                  for group in (wc, cc) for name, shape in group.items()}
            wg["masked"] = third.enter_context(nc.sbuf_tensor("masked", [P, P], BF16))

            def loads(sp):
                for name, held in wg.items():
                    sp.dma_start(held[:], a[name]).then_inc(loads_c, 16)
                load_ffn(sp, loads_d, 1, H1, CH1, 3 * E1 + 1)

            grouped_phase(nc, banks, w | wg, loads_c, 16 * len(wg), loads, between[1], between[2])
        ffn_phase(nc, "f1", banks, w1, loads_d, 16 * 5, between[2], out, E1, H1, K1)


def kernel(**inputs):
    import ml_dtypes
    import numpy as np
    import concourse.bacc as bacc
    from concourse.bass_utils import run_bass_kernel_spmd

    x = {k: np.asarray(v) for k, v in inputs.items()}
    f32, bf16 = np.float32, ml_dtypes.bfloat16

    def by_partition(m):
        return m.reshape(m.shape[0] // P, P, -1).transpose(1, 0, 2)

    def to_all(v):
        return np.broadcast_to(v, (P, v.shape[0]))

    def spread(experts, unit, hidden):
        s = np.zeros((3 * experts + 1, hidden), bf16)
        for e in range(experts):
            for part in range(3):
                s[part * experts + e, e * unit:(e + 1) * unit] = 1
        s[3 * experts, experts * unit:] = 1
        return s

    w, b = x["L0_attn_Wqkv"], x["L0_attn_bqkv"]
    a = {"x": x["L0_attn_x"].reshape(NT, P, C).transpose(1, 0, 2)}
    a["wqk"] = by_partition(w[:, 0:2 * C])
    a["bq0"] = b[0:C].reshape(KT, P).T
    bkz = np.zeros((P // LA_HD, LA_HD, LA_HEADS), f32)
    for hd in range(LA_HEADS):
        bkz[hd % (P // LA_HD), :, hd] = b[C + hd * LA_HD:C + (hd + 1) * LA_HD]
    a["bkz"] = bkz.reshape(P, LA_HEADS)
    a["own"] = np.repeat(np.eye(P // LA_HD, dtype=f32), LA_HD, axis=0)
    a["wv"], a["bv"] = by_partition(w[:, 2 * C:]), to_all(b[2 * C:])
    a["wo"], a["bout"] = by_partition(x["L0_attn_Wout"]), to_all(x["L0_attn_bout"])
    a["slopes"] = to_all(x["L0_attn_slopes"])

    gu, down = x["L0_ffn_gate_up_proj"], x["L0_ffn_down_proj"]
    a["gate0"] = by_partition(gu[:, 0:I0].reshape(E0 * I0, C).T)
    a["up0"] = by_partition(gu[:, I0:].reshape(E0 * I0, C).T)
    a["down0"] = by_partition(down.transpose(0, 2, 1).reshape(E0 * I0, C))
    a["router0"] = by_partition(x["L0_ffn_gate_weight"].T)

    a["wq"], a["bq"] = by_partition(x["L1_attn_q_project"].T), x["L1_attn_q_bias"].reshape(HQ, HD).T
    a["wk"], a["bk"] = by_partition(x["L1_attn_k_project"].T), x["L1_attn_k_bias"].reshape(HKV, HD).T
    a["wv1"], a["bv1"] = by_partition(x["L1_attn_v_project"].T), to_all(x["L1_attn_v_bias"])
    a["wo1"] = by_partition(x["L1_attn_o_project"].T)
    a["ln_weight"] = x["L1_attn_ln_weight"].reshape(KT, P).T

    gu, shared = x["L1_ffn_w_gate_up"], x["L1_ffn_shared_gate_up"]
    a["gate1"] = by_partition(np.concatenate([gu[:, :, 0:I1].transpose(1, 0, 2).reshape(C, -1), shared[:, 0:S1]], 1))
    a["up1"] = by_partition(np.concatenate([gu[:, :, I1:].transpose(1, 0, 2).reshape(C, -1), shared[:, S1:]], 1))
    rows = E1 * I1 + S1
    down = np.zeros((-(-rows // P) * P, C), f32)
    down[0:E1 * I1] = x["L1_ffn_w_down"].reshape(-1, C)
    down[E1 * I1:rows] = x["L1_ffn_shared_down"]
    a["down1"] = by_partition(down)
    a["router1"] = by_partition(x["L1_ffn_gate_w"].T)

    key, query = np.arange(P)[:, None], np.arange(2 * P)[None, :]
    distance = np.maximum(query - key, 0).astype(f32)
    causal = (query >= key).astype(f32)
    a["distance"] = np.concatenate([distance, distance[:, 0:P]], 1)
    a["causal"] = np.concatenate([causal, causal[:, 0:P]], 1)
    a["minus_half"] = np.full((P, 8), -0.5, f32)
    a["ident"], a["ident_bf"] = np.eye(P, dtype=f32), np.eye(P, dtype=f32).astype(bf16)
    a["masked"] = np.where(np.arange(P)[:, None] >= np.arange(P)[None, :], 0.0, MASKED).astype(bf16)
    inv_freq = (f32(1.0) / f32(10000.0) ** (np.arange(0, HD, 2, dtype=f32) / f32(HD))).astype(f32)
    angle = (np.arange(2 * P, dtype=f32)[:, None] * inv_freq).astype(f32).T
    a["cos"] = np.concatenate([np.cos(angle), np.cos(angle)], 0)
    a["sin"] = np.concatenate([np.sin(angle), -np.sin(angle)], 0)
    a["spread0"], a["spread1"] = spread(E0, I0, E0 * I0), spread(E1, I1, E1 * I1 + S1)

    nc = bacc.Bacc("TRN2", target_bir_lowering=False, num_devices=1)
    arrays = {f"in_{k}": np.ascontiguousarray(v) for k, v in a.items()}
    aps = {k: nc.dram_tensor(f"in_{k}", v.shape, mybir.dt.from_np(v.dtype), kind="ExternalInput").ap()
           for k, v in ((k, arrays[f"in_{k}"]) for k in a)}
    out = nc.dram_tensor("out_x", (P, NT, C), F32, kind="ExternalOutput").ap()
    program(nc, aps, out)
    r = run_bass_kernel_spmd(nc, [arrays], core_ids=[0])
    y = r.results[0]["out_x"]
    return y.transpose(1, 0, 2).reshape(x["L0_attn_x"].shape)
```

```python
import concourse.bass as bass
from concourse import mybir
from contextlib import ExitStack

F32 = mybir.dt.float32
F32R = mybir.dt.float32r
BF16 = mybir.dt.bfloat16
ALU = mybir.AluOpType
ACT = mybir.ActivationFunctionType
AX = mybir.AxisListType

P = 128
C = 256
KT = C // P
NT = 32
LN_EPS = 1e-5
RMS_EPS = 1e-6
BANK = 512

LA_HEADS, LA_HD = 16, 16
HQ, HKV, HD = 16, 4, 128
E0, I0, K0 = 32, 96, 8
E1, I1, K1, S1 = 16, 176, 2, 352
THRESHOLD = 0.8
NOT_KEPT = -5.0
MASKED = -1e30


HALVES = ((0, 1), (1, 0), (0, 0))


class Chain:

    def __init__(self, eng, sem, per):
        self.eng, self.sem, self.per = eng, sem, per

    def start(self, step):
        self.base, self.n = step * self.per, 0

    def add(self, instruction):
        instruction.then_inc(self.sem, 1)
        self.n += 1

    def wait(self):
        self.eng.wait_ge(self.sem, self.base + self.n)

    def done(self):
        assert self.n == self.per, (self.n, self.per)


def move_x(sp, steps, tiles, src, dst, xin, results_at, loaded, result_ready, results, stored, behind=None):

    def load(step, buf):
        sp.dma_start(xin[:, buf], src[:, bass.ds(step * tiles, tiles), :]).then_inc(loaded[buf], 16)

    def store(step, buf):
        sp.wait_ge(result_ready, results * (step + 1) + 1)
        sp.dma_start(dst[:, bass.ds(step * tiles, tiles), :], results_at[buf]).then_inc(stored, 16)

    sp.sem_inc(result_ready, 1)
    sp.sem_inc(stored, 16)
    load(0, 0)
    load(1, 1)
    if behind is not None:
        behind(sp)
    with sp.Fori(0, steps // 2 - 1) as i:
        for u in range(2):
            store(2 * i + u, u)
            load(2 * i + u + 2, u)
    store(steps - 2, 0)
    load(0, 0)
    store(steps - 1, 1)
    sp.wait_ge(stored, 16 * (steps + 1))
    sp.wait_ge(loaded[0], 16 * (steps // 2 + 1))


def ffn_phase(nc, tag, banks, w, weights_loaded, weights_value, down_loaded, src, dst,
              experts, hidden, keep, behind=None):
    T = 4
    TOK = T * P
    STEPS = NT // T
    NCH = -(-hidden // P)
    CR = 3 * experts + 1
    STATS, NORM, TR0, TR1, LOGITS = 2, 5, 7, 9, 11
    SHIFT, EXPS, PROBS, SHARES, CHOOSE, COMB, SPLIT, COMB_T = 12, 13, 14, 15, 16, 17, 18, 20
    COPY0, COPY1, COPY_COMB = 8, 10, 21

    with ExitStack() as ctx:
        def sb(name, shape, dt=F32):
            return ctx.enter_context(nc.sbuf_tensor(f"{tag}_{name}", shape, dt))

        def sem(name):
            return ctx.enter_context(nc.semaphore(f"{tag}_{name}"))

        xin = sb("xin", [P, 2, T, C])
        rows = sb("rows", [P, T, C])
        stats = sb("stats", [P, T, 6])
        mv = sb("mv", [P, T, 2])
        veps = sb("veps", [P, T])
        rstd = sb("rstd", [P, T])
        hT = [sb("hT_high", [P, 2, KT, TOK], F32R), sb("hT_low", [P, 2, KT, TOK], F32R)]
        names = "router", "gate", "up", "down"
        raw, low = [w[name] for name in names], [w[f"{name}_low"] for name in names]
        high = [sb("router_high", [P, KT, experts], F32R), sb("gate_high", [P, KT, hidden], F32R),
                sb("up_high", [P, KT, hidden], F32R), sb("down_high", [P, NCH, C], F32R)]
        router, gate, up, down = zip(high, low)

        def piece(i, at):
            return high[i][:, at], raw[i][:, at], low[i][:, at]

        cut = NCH // 2
        pieces = [piece(0, slice(0, KT)), piece(1, 0), piece(1, 1), piece(2, 0), piece(2, 1),
                  piece(3, slice(0, cut)), piece(3, slice(cut, NCH))]
        BY_POOL = 4, 6
        combT = sb("combT", [CR, 2, TOK], BF16)
        silu = sb("silu", [P, 2, TOK])
        gated = sb("gated", [P, 2, TOK])
        h = [sb("h_high", [P, 2, TOK], F32R), sb("h_low", [P, 2, TOK], F32R)]
        mx = sb("mx", [P, T])
        shifted = sb("shifted", [P, T, experts])
        expd = sb("expd", [P, T, experts])
        rsum = sb("rsum", [P, T])
        probs = sb("probs", [P, T, experts + 8])
        top = sb("top", [P, T, 8])
        cum = sb("cum", [P, 2, T, 8])
        active = sb("active", [P, T, 8])
        kept = sb("kept", [P, T, 8])
        found = sb("found", [P, T, 8])
        tsum = sb("tsum", [P, T])
        replaced = sb("replaced", [P, T, experts + 8])
        chosen = sb("chosen", [P, T, experts])
        comb = sb("comb", [P, T, experts])
        rest = sb("rest", [P, T, experts])
        parts = sb("parts", [P, T, CR], BF16)

        gate_banks, up_banks, comb_bank, y_banks, misc = banks[0:2], banks[2:4], banks[4], banks[5:7], banks[7]

        loaded = [sem("x_loaded_0"), sem("x_loaded_1")]
        stored = sem("x_stored")
        var_ready = sem("var_ready")
        pool_chain = sem("pool_chain")
        rstd_ready = sem("rstd_ready")
        look = sem("lookahead_chain")
        hn_ready = sem("hn_ready")
        misc_ready = sem("misc_ready")
        misc_copied = sem("misc_copied")
        shifted_ready = sem("shifted_ready")
        exp_ready = sem("exp_ready")
        parts_ready = sem("parts_ready")
        gate_ready = sem("gate_ready")
        silu_ready = sem("silu_ready")
        up_ready = sem("up_ready")
        gated_ready = sem("gated_ready")
        comb_ready = sem("comb_ready")
        whole_ready = sem("whole_h_ready")
        high_h_ready = sem("high_h_ready")
        h_ready = sem("h_ready")
        h_used = sem("h_used")
        result_ready = sem("result_ready")
        const_ready = sem("const_ready")
        high_ready = sem("high_ready")
        split_ready = sem("split_ready")
        pool_split_ready = sem("pool_split_ready")
        hT_ready = sem("hT_ready")

        apart = sem("apart")

        block = ctx.enter_context(nc.Block())

        @block.sync
        def _(sp):
            move_x(sp, STEPS, T, src, dst, xin, [rows[:], rows[:]], loaded, result_ready, 2, stored, behind)

        @block.gpsimd
        def _(pool):
            def inverse_deviation(n):
                pool.wait_ge(var_ready, n + 1)
                pool.sem_inc(apart, 1)
                nc.gpsimd.tensor_scalar(veps[:], mv[:, :, 1], LN_EPS, None, ALU.add).then_inc(pool_chain, 1)
                pool.wait_ge(pool_chain, n + 1)
                nc.gpsimd.tensor_tensor(rstd[:], veps[:], w["minus_half"][:, 0:T], ALU.pow).then_inc(rstd_ready, 1)

            inverse_deviation(0)
            for i in BY_POOL:
                held, whole, rest_of = pieces[i]
                pool.wait_ge(high_ready, i + 1)
                nc.gpsimd.tensor_tensor(rest_of, whole, held, ALU.subtract).then_inc(pool_split_ready, 1)
            with pool.Fori(0, STEPS // 2) as i:
                for u in range(2):
                    inverse_deviation(2 * i + u + 1)

        @block.tensor
        def _(pe):
            def transposes(n, half):
                pe.wait_ge(hn_ready, T * n + 2 * half + 2)
                if half:
                    pe.wait_ge(hT_ready, 2 * n + 1)
                elif not (isinstance(n, int) and n == 0):
                    pe.wait_ge(misc_copied, 3 * n)
                out = misc[:].rearrange("p (k t) -> p k t", k=KT)
                for k in range(KT):
                    for j in range(2):
                        last = nc.tensor.transpose(out[:, k, j * P:(j + 1) * P], rows[:, 2 * half + j, k * P:(k + 1) * P],
                                                   w["ident"][:])
                last.then_inc(misc_ready, 1)

            def logits(n, b):
                pe.wait_ge(hT_ready, 2 * n + 2)
                for j in range(T):
                    products = [(k, a, c) for k in range(KT) for a, c in HALVES]
                    for k, a, c in products:
                        last = nc.tensor.matmul(misc[:, j * experts:(j + 1) * experts], hT[a][:, b, k, j * P:(j + 1) * P],
                                                router[c][:, k, :], start=((k, a, c) == products[0]),
                                                stop=((k, a, c) == products[-1]))
                last.then_inc(misc_ready, 1)

            def transpose_parts(n):
                pe.wait_ge(shifted_ready, n + 1)
                pe.wait_ge(parts_ready, n + 1)
                pe.sem_inc(apart, 1)
                for j in range(T):
                    last = nc.tensor.transpose(misc[:].bitcast(BF16)[0:CR, j * P:(j + 1) * P], parts[:, j, :],
                                               w["ident_bf"][:])
                last.then_inc(misc_ready, 1)

            def gate_up(f, b, r, j):
                m = min(P, hidden - j * P)
                for banks_of, free, ready, wt in ((gate_banks, silu_ready, gate_ready, gate),
                                                  (up_banks, gated_ready, up_ready, up)):
                    pe.wait_ge(free, f + 1)
                    products = [(k, a, c) for k in range(KT) for a, c in HALVES]
                    for k, a, c in products:
                        last = nc.tensor.matmul(banks_of[r][0:m], wt[a][:, k, j * P:j * P + m], hT[c][:, b, k, :],
                                                start=((k, a, c) == products[0]), stop=((k, a, c) == products[-1]))
                    last.then_inc(ready, 1)

            pe.sem_inc(silu_ready, 2)
            pe.sem_inc(gated_ready, 2)
            pe.sem_inc(h_used, 2)
            pe.sem_inc(whole_ready, 2)
            transposes(0, 0)
            transposes(0, 1)
            pe.wait_ge(split_ready, 1)
            logits(0, 0)
            pe.wait_ge(split_ready, 4)
            pe.wait_ge(pool_split_ready, 1)
            gate_up(0, 0, 0, 0)
            transpose_parts(0)
            pe.wait_ge(split_ready, 5)
            pe.wait_ge(pool_split_ready, 2)
            with pe.Fori(0, STEPS // 2) as i:
                for u in range(2):
                    t = 2 * i + u
                    for j in range(NCH):
                        f, r = t * NCH + j, (u * NCH + j) % 2
                        m = min(P, hidden - j * P)
                        if j == 0:
                            pe.wait_ge(misc_copied, 3 * t + 3)
                        pe.wait_ge(whole_ready, 2 * f + 2)
                        nc.tensor.matmul(comb_bank[0:m], w["spread"][0:CR, j * P:j * P + m], combT[:, u, :],
                                         start=True, stop=True).then_inc(comb_ready, 1)
                        if j < NCH - 1:
                            gate_up(f + 1, u, (r + 1) % 2, j + 1)
                        else:
                            gate_up(f + 1, 1 - u, (r + 1) % 2, 0)
                        if j == TR0:
                            transposes(t + 1, 0)
                        if j == TR1:
                            transposes(t + 1, 1)
                        if j == LOGITS:
                            logits(t + 1, 1 - u)
                        if j == COMB_T:
                            transpose_parts(t + 1)
                        if j == 0:
                            pe.wait_ge(result_ready, 2 * t + 1)
                        for k in range(T):
                            if k % 2 == 0:
                                pe.wait_ge(h_ready, 2 * f + k // 2 + 1)
                            for n, (a, c) in enumerate(HALVES):
                                last = nc.tensor.matmul(y_banks[k // 2][:, (k % 2) * C:(k % 2 + 1) * C],
                                                        h[a][0:m, r, k * P:(k + 1) * P], down[c][0:m, j, :],
                                                        start=(j == 0 and k % 2 == 0 and n == 0), stop=(j == NCH - 1),
                                                        skip_group_check=True)
                        last.then_inc(h_used, 1)

        @block.scalar
        def _(act):
            def copy_hT(n, b, half):
                act.wait_ge(misc_ready, 4 * n + half + 1)
                nc.scalar.copy(hT[0][:, b, :, half * 2 * P:(half + 1) * 2 * P],
                               misc[:].rearrange("p (k t) -> p k t", k=KT)).then_inc(misc_copied, 1)

            def exps(n):
                act.wait_ge(shifted_ready, n + 1)
                nc.scalar.activation(expd[:], shifted[:], ACT.Exp).then_inc(exp_ready, 1)

            def copy_combT(n, b):
                act.wait_ge(misc_ready, 4 * n + 4)
                nc.scalar.copy(combT[:, b], misc[:].bitcast(BF16)[0:CR, 0:TOK]).then_inc(misc_copied, 1)

            def take_high(i):
                nc.scalar.copy(pieces[i][0], pieces[i][1]).then_inc(high_ready, 1)

            act.wait_ge(weights_loaded, weights_value)
            for i in range(4):
                take_high(i)
            copy_hT(0, 0, 0)
            copy_hT(0, 0, 1)
            take_high(4)
            exps(0)
            act.wait_ge(down_loaded, 16)
            take_high(5)
            take_high(6)
            copy_combT(0, 0)
            def take_silu(f, r, m):
                act.wait_ge(gate_ready, f + 1)
                act.wait_ge(gated_ready, f + 1)
                nc.scalar.activation(silu[0:m, r], gate_banks[r][0:m], ACT.Silu).then_inc(silu_ready, 1)

            with act.Fori(0, STEPS // 2) as i:
                for u in range(2):
                    t, nb = 2 * i + u, 1 - u
                    for j in range(NCH):
                        f, r = t * NCH + j, (u * NCH + j) % 2
                        m = min(P, hidden - j * P)
                        take_silu(f, r, m)
                        act.wait_ge(h_used, f + 1)
                        for half in range(2):
                            at = slice(half * 2 * P, (half + 1) * 2 * P)
                            act.wait_ge(whole_ready, 2 * f + half + 3)
                            nc.scalar.copy(h[0][0:m, r, at], gated[0:m, r, at]).then_inc(high_h_ready, 1)
                        if j == COPY0:
                            copy_hT(t + 1, nb, 0)
                        if j == COPY1:
                            copy_hT(t + 1, nb, 1)
                        if j == EXPS:
                            exps(t + 1)
                        if j == COPY_COMB:
                            copy_combT(t + 1, nb)
            take_silu(STEPS * NCH, 0, P)

        @block.vector
        def _(dve):
            chain = Chain(dve, look, 4 * T + 8 + (18 if keep == 8 else 1))

            def statistics(n, b, before):
                dve.wait_ge(loaded[b], 16 * (before + 1))
                chain.start(n)
                for k in range(T):
                    chain.add(nc.vector.bn_stats(stats[:, k], xin[:, b, k]))
                chain.wait()
                dve.sem_inc(apart, 1)
                for k in range(T - 1):
                    chain.add(nc.vector.bn_aggr(mv[:, k], stats[:, k]))
                nc.vector.bn_aggr(mv[:, T - 1], stats[:, T - 1]).then_inc(var_ready, 1)

            def normalise(n, b):
                dve.wait_ge(rstd_ready, n + 1)
                if not (isinstance(n, int) and n == 0):
                    dve.wait_ge(stored, 16 * n)
                for k in range(T):
                    nc.vector.tensor_scalar(rows[:, k], xin[:, b, k], mv[:, k, 0:1], rstd[:, k:k + 1],
                                            ALU.subtract, ALU.mult).then_inc(hn_ready, 1)

            def per_token(a, width):
                return a.unsqueeze(2).to_broadcast([P, T, width])

            def low_hT(n, b, half):
                dve.wait_ge(misc_copied, 3 * n + half + 1)
                at = slice(half * 2 * P, (half + 1) * 2 * P)
                nc.vector.tensor_tensor(hT[1][:, b, :, at], misc[:].rearrange("p (k t) -> p k t", k=KT),
                                        hT[0][:, b, :, at], ALU.subtract).then_inc(hT_ready, 1)

            def shift(n):
                logits = misc[:, 0:T * experts].rearrange("p (t e) -> p t e", t=T)
                dve.wait_ge(misc_ready, 4 * n + 3)
                chain.add(nc.vector.reduce_max(mx[:], logits, AX.X))
                chain.wait()
                nc.vector.tensor_tensor(shifted[:], logits, per_token(mx[:], experts), ALU.subtract).then_inc(shifted_ready, 1)

            def probabilities(n):
                dve.wait_ge(exp_ready, n + 1)
                chain.add(nc.vector.reduce_sum(rsum[:], expd[:], AX.X))
                chain.wait()
                chain.add(nc.vector.reciprocal(tsum[:], rsum[:]))
                chain.wait()
                chain.add(nc.vector.tensor_tensor(probs[:, :, 0:experts], expd[:], per_token(tsum[:], experts), ALU.mult))
                chain.wait()
                dve.sem_inc(apart, 1)
                for k in range(T):
                    chain.add(nc.vector.max(top[:, k], probs[:, k, 0:experts]))
                chain.wait()

            def running_shares():
                chain.add(nc.vector.reduce_sum(tsum[:], top[:], AX.X))
                chain.wait()
                chain.add(nc.vector.tensor_scalar(tsum[:], tsum[:], 1e-12, None, ALU.max))
                chain.wait()
                chain.add(nc.vector.reciprocal(rsum[:], tsum[:]))
                chain.wait()
                chain.add(nc.vector.tensor_tensor(cum[:, 0], top[:], per_token(rsum[:], 8), ALU.mult))
                chain.wait()
                a = 0
                for d in (1, 2, 4):
                    chain.add(nc.vector.tensor_copy(cum[:, 1 - a, :, 0:d], cum[:, a, :, 0:d]))
                    chain.add(nc.vector.tensor_tensor(cum[:, 1 - a, :, d:8], cum[:, a, :, d:8], cum[:, a, :, 0:8 - d], ALU.add))
                    chain.wait()
                    a = 1 - a

            def keep_by_share():
                shares = cum[:, 1]
                chain.add(nc.vector.tensor_scalar(active[:, :, 1:8], shares[:, :, 0:7], THRESHOLD, None, ALU.is_lt))
                chain.wait()
                chain.add(nc.vector.tensor_tensor(kept[:], top[:], active[:], ALU.mult))
                chain.add(nc.vector.tensor_scalar(found[:], active[:], -NOT_KEPT, NOT_KEPT, ALU.mult, ALU.add))
                chain.wait()
                chain.add(nc.vector.tensor_tensor(found[:], found[:], kept[:], ALU.add))
                chain.add(nc.vector.reduce_sum(tsum[:], kept[:], AX.X))
                chain.wait()
                chain.add(nc.vector.tensor_scalar(tsum[:], tsum[:], 1e-12, None, ALU.max))
                chain.wait()
                chain.add(nc.vector.reciprocal(rsum[:], tsum[:]))

            def sum_shares():
                if keep == 8:
                    running_shares()

            def choose():
                if keep == 8:
                    keep_by_share()
                else:
                    chain.add(nc.vector.tensor_copy(found[:, :, 0:keep], top[:, :, 0:keep]))
                chain.wait()

            def combine():
                dve.sem_inc(apart, 1)
                for k in range(T):
                    chain.add(nc.vector.match_replace(replaced[:, k], found[:, k], probs[:, k], -9.0))
                chain.wait()
                chain.add(nc.vector.tensor_tensor(chosen[:], replaced[:, :, 0:experts], probs[:, :, 0:experts], ALU.not_equal))
                chain.wait()
                chain.add(nc.vector.tensor_tensor(comb[:], chosen[:], probs[:, :, 0:experts], ALU.mult))
                chain.wait()
                if keep == 8:
                    chain.add(nc.vector.tensor_tensor(comb[:], comb[:], per_token(rsum[:], experts), ALU.mult))
                    chain.wait()

            def split_weights():
                chain.add(nc.vector.tensor_copy(parts[:, :, 0:experts], comb[:]))
                chain.wait()
                chain.add(nc.vector.tensor_tensor(rest[:], comb[:], parts[:, :, 0:experts], ALU.subtract))
                chain.wait()
                chain.add(nc.vector.tensor_copy(parts[:, :, experts:2 * experts], rest[:]))
                chain.wait()
                nc.vector.tensor_tensor(parts[:, :, 2 * experts:3 * experts], rest[:], parts[:, :, experts:2 * experts],
                                        ALU.subtract).then_inc(parts_ready, 1)
                chain.done()

            def take_low(i):
                dve.wait_ge(high_ready, i + 1)
                held, whole, rest_of = pieces[i]
                nc.vector.tensor_tensor(rest_of, whole, held, ALU.subtract).then_inc(split_ready, 1)

            nc.vector.memset(probs[:, :, experts:], NOT_KEPT).then_inc(const_ready, 1)
            nc.vector.memset(active[:], 1.0).then_inc(const_ready, 1)
            nc.vector.memset(found[:], NOT_KEPT).then_inc(const_ready, 1)
            nc.vector.memset(parts[:], 1.0).then_inc(const_ready, 1)
            dve.wait_ge(const_ready, 4)
            take_low(0)
            take_low(1)
            statistics(0, 0, 0)
            normalise(0, 0)
            take_low(2)
            low_hT(0, 0, 0)
            low_hT(0, 0, 1)
            take_low(3)
            shift(0)
            probabilities(0)
            sum_shares()
            choose()
            combine()
            split_weights()
            take_low(5)

            def gate(f, r, m):
                dve.wait_ge(silu_ready, f + 3)
                dve.wait_ge(up_ready, f + 1)
                nc.vector.tensor_tensor(gated[0:m, r], silu[0:m, r], up_banks[r][0:m], ALU.mult).then_inc(gated_ready, 1)

            gate(0, 0, P)
            with dve.Fori(0, STEPS // 2) as i:
                for u in range(2):
                    t, nb = 2 * i + u, 1 - u
                    for j in range(NCH):
                        f, r = t * NCH + j, (u * NCH + j) % 2
                        m = min(P, hidden - j * P)
                        if j > 0:
                            gate(f, r, m)
                        dve.wait_ge(gated_ready, f + 3)
                        dve.wait_ge(comb_ready, f + 1)
                        halves = [slice(half * 2 * P, (half + 1) * 2 * P) for half in range(2)]
                        for at in halves:
                            nc.vector.tensor_tensor(gated[0:m, r, at], gated[0:m, r, at], comb_bank[0:m, at],
                                                    ALU.mult).then_inc(whole_ready, 1)
                        for half, at in enumerate(halves):
                            dve.wait_ge(high_h_ready, 2 * f + half + 1)
                            nc.vector.tensor_tensor(h[1][0:m, r, at], gated[0:m, r, at], h[0][0:m, r, at],
                                                    ALU.subtract).then_inc(h_ready, 1)
                        if j == STATS:
                            statistics(t + 1, nb, i + u)
                        if j == NORM:
                            normalise(t + 1, nb)
                        if j == COPY0:
                            low_hT(t + 1, nb, 0)
                        if j == COPY1:
                            low_hT(t + 1, nb, 1)
                        if j == SHIFT:
                            shift(t + 1)
                        if j == PROBS:
                            probabilities(t + 1)
                        if j == SHARES:
                            sum_shares()
                        if j == CHOOSE:
                            choose()
                        if j == COMB:
                            combine()
                        if j == SPLIT:
                            split_weights()
                    gate((t + 1) * NCH, ((u + 1) * NCH) % 2, P)
                    dve.wait_ge(h_used, (t + 1) * NCH + 2)
                    for half in range(2):
                        s = slice(2 * half, 2 * half + 2)
                        nc.vector.tensor_tensor(rows[:, s], y_banks[half][:].rearrange("p (t c) -> p t c", t=2),
                                                xin[:, u, s], ALU.add).then_inc(result_ready, 1)


def lightning_phase(nc, banks, w, weights_loaded, weights_value, next_weights, src, dst):
    T = 2
    TOK = T * P
    STEPS = NT // T
    QC = C // P
    HPC = LA_HEADS // QC
    TRI = 3 * P
    RING = 4
    F_T, F_Q, F_K, F_OUT, F_V, FILLS = 0, 1, 2, 4, 5, 6
    PROLOGUE = 5
    STATS, NORM, TR = 3, 7, 10

    with ExitStack() as ctx:
        def sb(name, shape, dt=F32):
            return ctx.enter_context(nc.sbuf_tensor(f"la_{name}", shape, dt))

        def sem(name):
            return ctx.enter_context(nc.semaphore(f"la_{name}"))

        decay = sb("decay", [P, LA_HEADS, TRI])
        neg_slopes = sb("neg_slopes", [P, LA_HEADS])
        xin = sb("xin", [P, 2, T, C])
        xout = sb("xout", [P, 2, T, C])
        xb = sb("xb", [P, 2, T, C])
        stats = sb("stats", [P, T, 6])
        mv = sb("mv", [P, T, 2])
        veps = sb("veps", [P, T])
        rstd = sb("rstd", [P, T])
        hn = sb("hn", [P, T, C])
        hT = [sb("hT_high", [P, KT, TOK], F32R), sb("hT_low", [P, KT, TOK], F32R)]
        oT = [sb("oT_high", [P, KT, TOK], F32R), sb("oT_low", [P, KT, TOK], F32R)]
        names = "wqk", "wv", "wo"
        raw, low = [w[name] for name in names], [w[f"{name}_low"] for name in names]
        high = [sb(f"{name}_high", whole.shape, F32R) for name, whole in zip(names, raw)]
        wqk, wv, wo = zip(high, low)
        q = sb("q", [P, QC, TOK])
        kz = sb("kz", [P, LA_HEADS, TOK])
        vz = sb("vz", [P, T, QC, HPC * (P + LA_HD)])
        weighted = sb("weighted", [P, RING, TRI])

        proj_banks, score_banks, o_banks = banks[0:2], banks[2:6], banks[6:8]

        loaded = [sem("x_loaded_0"), sem("x_loaded_1")]
        stored = sem("x_stored")
        slopes_ready = sem("slopes_ready")
        exp_ready = sem("exp_ready")
        decay_ready = sem("decay_ready")
        stats_chain = sem("stats_chain")
        var_ready = sem("var_ready")
        pool_chain = sem("pool_chain")
        rstd_ready = sem("rstd_ready")
        xb_ready = sem("xb_ready")
        hn_ready = sem("hn_ready")
        high_ready = sem("high_ready")
        split_ready = sem("split_ready")
        high_hT_ready = sem("high_hT_ready")
        hT_ready = sem("hT_ready")
        high_o_ready = sem("high_o_ready")
        proj_ready = sem("proj_ready")
        q_ready = sem("q_ready")
        k_ready = [sem("k_ready_0"), sem("k_ready_1")]
        v_ready = sem("v_ready")
        zeros_ready = sem("zeros_ready")
        scores_ready = sem("scores_ready")
        weighted_ready = sem("weighted_ready")
        head_done = sem("head_done")
        o_copied = sem("o_copied")
        result_ready = sem("result_ready")

        apart = sem("apart")

        block = ctx.enter_context(nc.Block())

        @block.sync
        def _(sp):
            move_x(sp, STEPS, T, src, dst, xin, [xout[:, 0], xout[:, 1]], loaded, result_ready, 1, stored, next_weights)

        @block.gpsimd
        def _(pool):
            def inverse_deviation(n):
                pool.wait_ge(var_ready, n + 1)
                pool.sem_inc(apart, 1)
                nc.gpsimd.tensor_scalar(veps[:], mv[:, :, 1], LN_EPS, None, ALU.add).then_inc(pool_chain, 1)
                pool.wait_ge(pool_chain, n + 1)
                nc.gpsimd.tensor_tensor(rstd[:], veps[:], w["minus_half"][:, 0:T], ALU.pow).then_inc(rstd_ready, 1)

            def add_bias(b, before):
                pool.wait_ge(loaded[b], 16 * (before + 1))
                nc.gpsimd.tensor_tensor(xb[:, b], xin[:, b], w["bout"][:].unsqueeze(1).to_broadcast([P, T, C]),
                                        ALU.add).then_inc(xb_ready, 1)

            pool.wait_ge(weights_loaded, weights_value)
            inverse_deviation(0)
            add_bias(0, 0)
            for hd in range(LA_HEADS):
                pool.wait_ge(exp_ready, hd + 1)
                nc.gpsimd.tensor_tensor(decay[:, hd], decay[:, hd], w["causal"][:], ALU.mult).then_inc(decay_ready, 1)
            with pool.Fori(0, STEPS // 2) as i:
                for u in range(2):
                    inverse_deviation(2 * i + u + 1)
                    pool.wait_ge(result_ready, 2 * i + u + 1)
                    add_bias(1 - u, i + u)

        @block.tensor
        def _(pe):
            def bank_free(loops, k):
                n = 0 if loops is None else loops + 1
                if k in (F_T, F_Q) and loops is not None:
                    pe.wait_ge(k_ready[k - F_T], HPC * n)
                elif k == F_K:
                    pe.wait_ge(hT_ready, n + 1)
                elif k == F_K + 1:
                    pe.wait_ge(q_ready, n + 1)
                elif k == F_OUT:
                    pe.wait_ge(o_copied, n + 1)
                elif k == F_V and loops is not None:
                    pe.wait_ge(result_ready, n)

            def transpose_hn(loops, n):
                pe.wait_ge(hn_ready, T * (n + 1))
                bank_free(loops, F_T)
                out = proj_banks[0][:].rearrange("p (k t) -> p k t", k=KT)
                for k in range(KT):
                    for j in range(T):
                        last = nc.tensor.transpose(out[:, k, j * P:(j + 1) * P], hn[:, j, k * P:(k + 1) * P], w["ident"][:])
                last.then_inc(proj_ready, 1)

            products = [(k, a, b) for k in range(KT) for a, b in HALVES]

            def project_chunk(out, ch):
                for k, a, b in products:
                    last = nc.tensor.matmul(out, wqk[a][:, k, ch * P:(ch + 1) * P], hT[b][:, k, :],
                                            start=((k, a, b) == products[0]), stop=((k, a, b) == products[-1]))
                return last

            def project_qk(loops, n):
                pe.wait_ge(hT_ready, n + 1)
                bank_free(loops, F_Q)
                for ch in range(QC):
                    last = project_chunk(proj_banks[1][:, ch * TOK:(ch + 1) * TOK], ch)
                last.then_inc(proj_ready, 1)
                for ch in range(QC):
                    bank_free(loops, F_K + ch)
                    project_chunk(proj_banks[ch][:, 0:TOK], QC + ch).then_inc(proj_ready, 1)

            def project_tokens(loops, fill, bank, tokens, wt):
                bank_free(loops, fill)
                for j in range(T):
                    for k, a, b in products:
                        last = nc.tensor.matmul(bank[:, j * C:(j + 1) * C], tokens[a][:, k, j * P:(j + 1) * P],
                                                wt[b][:, k, :], start=((k, a, b) == products[0]),
                                                stop=((k, a, b) == products[-1]))
                last.then_inc(proj_ready, 1)

            def scores(g, hd):
                s, k, qc = score_banks[hd % RING], kz[:, hd], q[:, hd // HPC]
                pe.wait_ge(weighted_ready, g + 1)
                nc.tensor.matmul(s[:, 0:TOK], k[:, 0:P], qc[:, 0:TOK], start=True, stop=True)
                nc.tensor.matmul(s[:, TOK:TRI], k[:, P:TOK], qc[:, P:TOK], start=True, stop=True).then_inc(scores_ready, 1)

            def outputs(g, u, hd):
                a, ch, n = weighted[:, hd % RING], hd // HPC, hd % HPC
                out = o_banks[u][:, ch * TOK:(ch + 1) * TOK]
                pe.wait_ge(weighted_ready, g + 1 + RING)
                nc.tensor.matmul(out, vz[:, 0, ch, n * P:(n + 1) * P], a[:, 0:TOK], start=(n == 0), stop=False)
                nc.tensor.matmul(out[:, P:TOK], vz[:, 1, ch, n * P:(n + 1) * P], a[:, TOK:TRI], start=False,
                                 stop=(n == HPC - 1)).then_inc(head_done, 1)

            pe.sem_inc(weighted_ready, RING)
            pe.sem_inc(head_done, RING)
            pe.sem_inc(o_copied, 1)
            pe.wait_ge(weights_loaded, weights_value)
            transpose_hn(None, 0)
            pe.wait_ge(split_ready, len(raw))
            project_qk(None, 0)
            project_tokens(None, F_V, o_banks[0], hT, wv)
            with pe.Fori(0, STEPS // 2) as i:
                for u in range(2):
                    t = 2 * i + u
                    pe.wait_ge(q_ready, t + 1)
                    for s in range(LA_HEADS + 3):
                        if s < LA_HEADS:
                            pe.wait_ge(k_ready[s // HPC], HPC * t + s % HPC + 1)
                            scores(t * LA_HEADS + s, s)
                        if s == TR:
                            transpose_hn(t, t + 1)
                        if s == 3:
                            pe.wait_ge(v_ready, t + 1)
                        if s >= 3:
                            outputs(t * LA_HEADS + s - 3, u, s - 3)
                    project_qk(t, t + 1)
                    project_tokens(t, F_OUT, o_banks[u], oT, wo)
                    project_tokens(t, F_V, o_banks[1 - u], hT, wv)

        @block.scalar
        def _(act):
            def copy_hT(loops, first):
                act.wait_ge(proj_ready, loops * FILLS + first + 1)
                nc.scalar.copy(hT[0][:], proj_banks[0][:].rearrange("p (k t) -> p k t", k=KT)).then_inc(high_hT_ready, 1)

            def copy_q(loops, first):
                f = first + F_Q
                act.wait_ge(proj_ready, loops * FILLS + f + 1)
                for ch in range(QC):
                    last = nc.scalar.activation(q[:, ch], proj_banks[1][:, ch * TOK:(ch + 1) * TOK],
                                                ACT.Identity, bias=w["bq0"][:, ch:ch + 1])
                last.then_inc(q_ready, 1)

            def copy_k(loops, first):
                f = first + F_K
                act.wait_ge(proj_ready, loops * FILLS + f + 1)
                for n in range(HPC):
                    nc.scalar.activation(kz[:, n], proj_banks[0][:, 0:TOK], ACT.Identity, bias=w["bkz"][:, n:n + 1],
                                         scale=w["own"][:, n:n + 1]).then_inc(k_ready[0], 1)

            act.wait_ge(weights_loaded, weights_value)
            for whole, held in zip(raw, high):
                nc.scalar.copy(held[:], whole[:]).then_inc(high_ready, 1)
            nc.scalar.mul(neg_slopes[:], w["slopes"][:], -1.0).then_inc(slopes_ready, 1)
            act.wait_ge(slopes_ready, 1)
            for hd in range(LA_HEADS):
                nc.scalar.activation(decay[:, hd], w["distance"][:], ACT.Exp, scale=neg_slopes[:, hd:hd + 1]).then_inc(exp_ready, 1)
            copy_hT(0, 0)
            copy_q(0, 0)
            copy_k(0, 0)
            with act.Fori(0, STEPS // 2) as i:
                for u in range(2):
                    t = 2 * i + u
                    copy_hT(t, PROLOGUE)
                    act.wait_ge(head_done, (t + 1) * LA_HEADS + RING)
                    nc.scalar.copy(oT[0][:], o_banks[u][:].rearrange("p (k t) -> p k t", k=KT)).then_inc(high_o_ready, 1)
                    copy_q(t, PROLOGUE)
                    copy_k(t, PROLOGUE)

        @block.vector
        def _(dve):
            chain = Chain(dve, stats_chain, 2 * T - 1)

            def statistics(n, b, before):
                dve.wait_ge(loaded[b], 16 * (before + 1))
                chain.start(n)
                for k in range(T):
                    chain.add(nc.vector.bn_stats(stats[:, k], xin[:, b, k]))
                chain.wait()
                dve.sem_inc(apart, 1)
                for k in range(T - 1):
                    chain.add(nc.vector.bn_aggr(mv[:, k], stats[:, k]))
                nc.vector.bn_aggr(mv[:, T - 1], stats[:, T - 1]).then_inc(var_ready, 1)
                chain.done()

            def normalise(n, b):
                dve.wait_ge(rstd_ready, n + 1)
                for k in range(T):
                    nc.vector.tensor_scalar(hn[:, k], xin[:, b, k], mv[:, k, 0:1], rstd[:, k:k + 1],
                                            ALU.subtract, ALU.mult).then_inc(hn_ready, 1)

            def copy_k(t, n):
                if n == 0:
                    dve.wait_ge(proj_ready, t * FILLS + F_K + 2)
                nc.vector.tensor_scalar(kz[:, HPC + n], proj_banks[1][:, 0:TOK], w["own"][:, n:n + 1],
                                        w["bkz"][:, HPC + n:HPC + n + 1], ALU.mult, ALU.add).then_inc(k_ready[1], 1)

            def copy_v(loops, f, bank):
                dve.wait_ge(proj_ready, loops * FILLS + f + 1)
                for j in range(T):
                    last = nc.vector.tensor_tensor(
                        vz[:, j].rearrange("p c (n s) -> p c n s", s=P + LA_HD)[:, :, :, 0:LA_HD],
                        bank[:, j * C:(j + 1) * C].rearrange("p (c n d) -> p c n d", c=QC, d=LA_HD),
                        w["bv"][:].rearrange("p (c n d) -> p c n d", c=QC, d=LA_HD), ALU.add)
                last.then_inc(v_ready, 1)

            def low_of(out, bank, held):
                return nc.vector.tensor_tensor(out[:], bank[:].rearrange("p (k t) -> p k t", k=KT), held[:], ALU.subtract)

            def low_hT(n):
                dve.wait_ge(high_hT_ready, n + 1)
                low_of(hT[1], proj_banks[0], hT[0]).then_inc(hT_ready, 1)

            nc.vector.memset(vz[:], 0.0).then_inc(zeros_ready, 1)
            dve.wait_ge(weights_loaded, weights_value)
            statistics(0, 0, 0)
            normalise(0, 0)
            for i, (whole, held, rest_of) in enumerate(zip(raw, high, low)):
                dve.wait_ge(high_ready, i + 1)
                nc.vector.tensor_tensor(rest_of[:], whole[:], held[:], ALU.subtract).then_inc(split_ready, 1)
            low_hT(0)
            dve.wait_ge(zeros_ready, 1)
            copy_v(0, PROLOGUE - 1, o_banks[0])
            with dve.Fori(0, STEPS // 2) as i:
                for u in range(2):
                    t = 2 * i + u
                    for s in range(LA_HEADS):
                        g = t * LA_HEADS + s
                        if u == 0:
                            dve.wait_ge(decay_ready, s + 1)
                        dve.wait_ge(scores_ready, g + 1)
                        dve.wait_ge(head_done, g + 1)
                        nc.vector.tensor_tensor(weighted[:, s % RING], score_banks[s % RING][:, 0:TRI], decay[:, s],
                                                ALU.mult).then_inc(weighted_ready, 1)
                        if s < HPC:
                            copy_k(t, s)
                        if s == STATS:
                            statistics(t + 1, 1 - u, i + u)
                        if s == NORM:
                            normalise(t + 1, 1 - u)
                        if s == TR + 2:
                            low_hT(t + 1)
                    dve.wait_ge(high_o_ready, t + 1)
                    low_of(oT[1], o_banks[u], oT[0]).then_inc(o_copied, 1)
                    f = PROLOGUE + F_OUT
                    dve.wait_ge(proj_ready, t * FILLS + f + 1)
                    dve.wait_ge(stored, 16 * t + 16)
                    dve.wait_ge(xb_ready, t + 1)
                    nc.vector.tensor_tensor(xout[:, u], o_banks[u][:].rearrange("p (j c) -> p j c", j=T),
                                            xb[:, u], ALU.add).then_inc(result_ready, 1)
                    copy_v(t, PROLOGUE + F_V, o_banks[1 - u])


def grouped_phase(nc, banks, w, weights_loaded, weights_value, split_loaded, next_weights, src, dst):
    T = 2
    TOK = T * P
    STEPS = NT // T
    GROUP = HQ // HKV
    PAIRS = HQ // 2
    TRI = 3 * P
    RING = 4
    SCALE = HD ** -0.5
    PROLOGUE = 3 + 2 + 2
    F_T, F_K, F_Q, F_V, F_OUT = 7, 8, 10, 13, (6, 12, 15)
    FILLS = 16
    PARTS = (0, 3), (3, 6), (6, 8)
    HELD = 4
    ROPE_PROLOGUE, ROPES = 4, 10
    STATS, NORM = 5, 9

    with ExitStack() as ctx:
        def sb(name, shape, dt=F32):
            return ctx.enter_context(nc.sbuf_tensor(f"ga_{name}", shape, dt))

        def sem(name):
            return ctx.enter_context(nc.semaphore(f"ga_{name}"))

        xin = sb("xin", [P, 2, T, C])
        xout = sb("xout", [P, T, C])
        stats = sb("stats", [P, T, 6])
        mv = sb("mv", [P, T, 2])
        small = sb("small", [P, 6, T])
        rstd = sb("rstd", [P, T])
        hn = sb("hn", [P, T, C])
        hT = [sb("hT_high", [P, KT, TOK], F32R), sb("hT_low", [P, KT, TOK], F32R)]
        raw = sb("raw", [P, 2, 2, TOK])
        by_cos = sb("by_cos", [P, 2, 2, TOK])
        by_sin = sb("by_sin", [P, 2, 2, TOK])
        q = sb("q", [P, 4, 2, TOK])
        kr = sb("kr", [P, HKV, TOK])
        v = sb("v", [P, T, HKV * HD])
        top = sb("top", [P, RING, 2])
        bias = sb("bias", [P, RING, 2])
        rsum = sb("rsum", [P, RING, 2])
        rinv = sb("rinv", [P, RING, 2])
        probs = sb("probs", [P, RING, TRI])
        probsT = sb("probsT", [P, 2, TRI])
        attn = [sb("attn_high", [P, HELD, 2 * TOK], F32R), sb("attn_low", [P, HELD, 2 * TOK], F32R)]
        names = "wk", "wq", "wv1", "wo1"
        raw_weights, low = [w[name] for name in names], [w[f"{name}_low"] for name in names]
        high = [sb(f"{name}_high", whole.shape, F32R) for name, whole in zip(names, raw_weights)]
        wk, wq, wv, wo = zip(high, low)

        proj_banks, score_banks, pt_banks, attn_banks = banks[0:2], banks[2:4], banks[4:6], banks[6:8]

        loaded = [sem("x_loaded_0"), sem("x_loaded_1")]
        stored = sem("x_stored")
        stats_chain = sem("stats_chain")
        var_ready = sem("var_ready")
        pool_chain = sem("pool_chain")
        rstd_ready = sem("rstd_ready")
        hn_ready = sem("hn_ready")
        proj_ready = sem("proj_ready")
        high_hT_ready = sem("high_hT_ready")
        hT_ready = sem("hT_ready")
        high_ready = sem("high_ready")
        split_ready = sem("split_ready")
        raw_ready = sem("raw_ready")
        v_ready = sem("v_ready")
        cos_ready = sem("cos_ready")
        sin_ready = sem("sin_ready")
        pool_sin_ready = sem("pool_sin_ready")
        roped = sem("roped")
        scores_ready = sem("scores_ready")
        max_chain = sem("max_chain")
        bias_ready = sem("bias_ready")
        exp_ready = sem("exp_ready")
        rinv_ready = sem("rinv_ready")
        probs_ready = sem("probs_ready")
        pt_ready = sem("pt_ready")
        pt_copied = sem("pt_copied")
        attn_ready = sem("attn_ready")
        high_attn_ready = sem("high_attn_ready")
        attn_copied = sem("attn_copied")
        part_added = sem("part_added")
        result_ready = sem("result_ready")

        apart = sem("apart")

        def rotate(eng, r, d):
            half = HD // 2
            frm, to = slice((1 - d) * half, (2 - d) * half), slice(d * half, (d + 1) * half)
            return eng.tensor_tensor(by_sin[to, r], raw[frm, r], w["sin"][frm].unsqueeze(1).to_broadcast([half, 2, TOK]),
                                     ALU.mult)

        block = ctx.enter_context(nc.Block())

        @block.sync
        def _(sp):
            move_x(sp, STEPS, T, src, dst, xin, [xout[:], xout[:]], loaded, result_ready, 1, stored, next_weights)

        @block.gpsimd
        def _(pool):
            steps = Chain(pool, pool_chain, 6)

            def inverse_deviation(n):
                pool.wait_ge(var_ready, n + 1)
                pool.sem_inc(apart, 1)
                var = mv[:, :, 1]
                steps.start(n)
                steps.add(nc.gpsimd.tensor_scalar(small[:, 0], var, LN_EPS, None, ALU.add))
                steps.wait()
                steps.add(nc.gpsimd.tensor_tensor(small[:, 1], small[:, 0], w["minus_half"][:, 0:T], ALU.pow))
                steps.wait()
                steps.add(nc.gpsimd.tensor_tensor(small[:, 2], small[:, 1], small[:, 1], ALU.mult))
                steps.wait()
                steps.add(nc.gpsimd.tensor_tensor(small[:, 3], small[:, 2], var, ALU.mult))
                steps.wait()
                pool.sem_inc(apart, 1)
                steps.add(nc.gpsimd.tensor_scalar(small[:, 4], small[:, 3], RMS_EPS, None, ALU.add))
                steps.wait()
                steps.add(nc.gpsimd.tensor_tensor(small[:, 5], small[:, 4], w["minus_half"][:, 0:T], ALU.pow))
                steps.wait()
                nc.gpsimd.tensor_tensor(rstd[:], small[:, 5], small[:, 1], ALU.mult).then_inc(rstd_ready, 1)
                steps.done()

            def products_of_rope(loops, k):
                r = k % 2
                pool.wait_ge(raw_ready, loops * ROPES + k + 1)
                if isinstance(loops, int) and k < 2:
                    pass
                else:
                    pool.wait_ge(roped, loops * ROPES + k - 1)
                nc.gpsimd.tensor_tensor(by_cos[:, r], raw[:, r], w["cos"][:].unsqueeze(1).to_broadcast([P, 2, TOK]),
                                        ALU.mult).then_inc(cos_ready, 1)
                pool.wait_ge(cos_ready, loops * ROPES + k + 1)
                rotate(nc.gpsimd, r, 1).then_inc(pool_sin_ready, 1)
                pool.wait_ge(pool_sin_ready, loops * ROPES + k + 1)

            pool.wait_ge(weights_loaded, weights_value)
            inverse_deviation(0)
            for k in range(ROPE_PROLOGUE):
                products_of_rope(0, k)
            with pool.Fori(0, STEPS // 2) as i:
                for u in range(2):
                    t = 2 * i + u
                    for s in range(HQ):
                        if s % 2 == 0 and s // 2 < PAIRS - 2:
                            products_of_rope(t, ROPE_PROLOGUE + s // 2)
                        if s == STATS:
                            inverse_deviation(t + 1)
                    for k in range(4):
                        products_of_rope(t, ROPE_PROLOGUE + PAIRS - 2 + k)

        @block.tensor
        def _(pe):
            def bank_free(loops, f):
                if loops is None:
                    if f >= 2:
                        pe.wait_ge(*((hT_ready, 1), (raw_ready, 1), (raw_ready, 2), (raw_ready, 3), (raw_ready, 4))[f - 2])
                    return
                k = f - PROLOGUE - 2
                if k == -2:
                    pe.wait_ge(v_ready, 2 * (loops + 1))
                elif k == -1:
                    pe.wait_ge(result_ready, loops + 1)
                elif k in F_OUT:
                    pe.wait_ge(part_added, 2 * loops + F_OUT.index(k) + 1)
                elif k < F_T:
                    pe.wait_ge(raw_ready, loops * ROPES + ROPE_PROLOGUE + k + 1)
                elif k == F_T:
                    pe.wait_ge(hT_ready, loops + 2)
                elif k < F_V:
                    pe.wait_ge(raw_ready, loops * ROPES + ROPE_PROLOGUE + k - 1)
                else:
                    pe.wait_ge(v_ready, 2 * loops + 3 + k - F_V)

            def transpose_hn(loops, f, n):
                pe.wait_ge(hn_ready, T * (n + 1))
                bank_free(loops, f)
                out = proj_banks[f % 2][:].rearrange("p (k t) -> p k t", k=KT)
                for k in range(KT):
                    for j in range(T):
                        last = nc.tensor.transpose(out[:, k, j * P:(j + 1) * P], hn[:, j, k * P:(k + 1) * P], w["ident"][:])
                last.then_inc(proj_ready, 1)

            products = [(k, a, b) for k in range(KT) for a, b in HALVES]

            def project(loops, f, wt, pair):
                bank_free(loops, f)
                for c in range(2):
                    ch = 2 * pair + c
                    for k, a, b in products:
                        last = nc.tensor.matmul(proj_banks[f % 2][:, c * TOK:(c + 1) * TOK], wt[a][:, k, ch * HD:(ch + 1) * HD],
                                                hT[b][:, k, :], start=((k, a, b) == products[0]),
                                                stop=((k, a, b) == products[-1]))
                last.then_inc(proj_ready, 1)

            def project_v(loops, f, j):
                bank_free(loops, f)
                for k, a, b in products:
                    last = nc.tensor.matmul(proj_banks[f % 2][:], hT[a][:, k, j * P:(j + 1) * P], wv[b][:, k, :],
                                            start=((k, a, b) == products[0]), stop=((k, a, b) == products[-1]))
                last.then_inc(proj_ready, 1)

            def scores(g, hd):
                s, kv = score_banks[hd % 2], kr[:, hd // GROUP]
                qh = q[:, (hd // 2) % 4, hd % 2]
                pe.wait_ge(exp_ready, g + 1)
                for tile, c0, keys in ((0, 0, P), (1, P, TOK)):
                    nc.tensor.matmul(s[:, c0:c0 + keys], qh[:, tile * P:(tile + 1) * P], kv[:, 0:keys], start=True, stop=False)
                    last = nc.tensor.matmul(s[:, c0 + keys - P:c0 + keys], w["ident_bf"][:], w["masked"][:],
                                            start=False, stop=True)
                last.then_inc(scores_ready, 1)

            def transpose_probs(g, hd):
                pe.wait_ge(probs_ready, g + 1)
                pe.wait_ge(pt_copied, g + 1)
                for blk in range(3):
                    last = nc.tensor.transpose(pt_banks[hd % 2][:, blk * P:(blk + 1) * P],
                                               probs[:, hd % RING, blk * P:(blk + 1) * P], w["ident"][:])
                last.then_inc(pt_ready, 1)

            def attend(g, t, hd):
                out = attn_banks[(hd // 2) % 2][:, (hd % 2) * TOK:(hd % 2 + 1) * TOK]
                cols = slice((hd // GROUP) * HD, (hd // GROUP + 1) * HD)
                pe.wait_ge(pt_copied, g + 3)
                if hd == 0:
                    pe.wait_ge(v_ready, 2 * (t + 1))
                if hd % 2 == 0:
                    pe.wait_ge(attn_copied, t * PAIRS + hd // 2 + 1)
                nc.tensor.matmul(out, v[:, 0, cols], probsT[:, hd % 2, 0:TOK], start=True, stop=False)
                nc.tensor.matmul(out[:, P:TOK], v[:, 1, cols], probsT[:, hd % 2, TOK:TRI], start=False,
                                 stop=True).then_inc(attn_ready, 1)

            def project_out(t, part):
                f, (first, end) = PROLOGUE + F_OUT[part], PARTS[part]
                pe.wait_ge(attn_copied, t * PAIRS + end + 2)
                bank_free(t, f)
                sums = [(hd, a, b) for hd in range(2 * first, 2 * end) for a, b in HALVES]
                for j in range(T):
                    for hd, a, b in sums:
                        at = (hd % 2) * TOK + j * P
                        last = nc.tensor.matmul(proj_banks[f % 2][:, j * C:(j + 1) * C], attn[a][:, hd // 2 % HELD, at:at + P],
                                                wo[b][:, hd, :], start=((hd, a, b) == sums[0]), stop=((hd, a, b) == sums[-1]))
                last.then_inc(proj_ready, 1)

            pe.sem_inc(exp_ready, 2)
            pe.sem_inc(pt_copied, 2)
            pe.sem_inc(attn_ready, 2)
            pe.sem_inc(attn_copied, 2)
            pe.wait_ge(weights_loaded, weights_value)
            transpose_hn(None, 0, 0)
            pe.wait_ge(hT_ready, 1)
            pe.wait_ge(split_ready, 1)
            project(None, 1, wk, 0)
            project(None, 2, wk, 1)
            pe.wait_ge(split_ready, 2)
            project(None, 3, wq, 0)
            project(None, 4, wq, 1)
            pe.wait_ge(split_ready, 3)
            project_v(None, 5, 0)
            project_v(None, 6, 1)
            pe.wait_ge(split_ready, 4)
            with pe.Fori(0, STEPS // 2) as i:
                for u in range(2):
                    t = 2 * i + u
                    for s in range(HQ + 4):
                        if 3 <= s < HQ + 3:
                            transpose_probs(t * HQ + s - 3, s - 3)
                        if s < HQ:
                            if s == 0:
                                pe.wait_ge(roped, t * ROPES + ROPE_PROLOGUE - 1)
                            elif s == 2:
                                pe.wait_ge(roped, t * ROPES + ROPE_PROLOGUE)
                            elif s % 2 == 0:
                                pe.wait_ge(roped, t * ROPES + ROPE_PROLOGUE + s // 2 - 1)
                            scores(t * HQ + s, s)
                        if s % 2 == 0 and s // 2 < PAIRS - 2:
                            project(t, PROLOGUE + s // 2, wq, 2 + s // 2)
                        if s == HQ - 4:
                            transpose_hn(t, PROLOGUE + F_T, t + 1)
                        if s == HQ:
                            pe.wait_ge(hT_ready, t + 2)
                            project(t, PROLOGUE + F_K, wk, 0)
                        if s == HQ + 1:
                            project(t, PROLOGUE + F_K + 1, wk, 1)
                        if s == HQ + 2:
                            project(t, PROLOGUE + F_Q, wq, 0)
                        if s == HQ + 3:
                            project(t, PROLOGUE + F_Q + 1, wq, 1)
                        if s >= 4:
                            attend(t * HQ + s - 4, t, s - 4)
                        if s == 11:
                            project_out(t, 0)
                    project_out(t, 1)
                    project_v(t, PROLOGUE + F_V, 0)
                    project_v(t, PROLOGUE + F_V + 1, 1)
                    project_out(t, 2)

        @block.scalar
        def _(act):
            def copy_hT(loops, f):
                act.wait_ge(proj_ready, loops * FILLS + f + 1)
                for k in range(KT):
                    last = nc.scalar.activation(hT[0][:, k], proj_banks[f % 2][:, k * TOK:(k + 1) * TOK], ACT.Identity,
                                                scale=w["ln_weight"][:, k:k + 1])
                last.then_inc(high_hT_ready, 1)

            def copy_raw(loops, f, rope, biases, pair):
                act.wait_ge(proj_ready, loops * FILLS + f + 1)
                if not (isinstance(loops, int) and rope < 2):
                    act.wait_ge(roped, loops * ROPES + rope - 1)
                for c in range(2):
                    ch = 2 * pair + c
                    last = nc.scalar.activation(raw[:, rope % 2, c], proj_banks[f % 2][:, c * TOK:(c + 1) * TOK],
                                                ACT.Identity, bias=biases[:, ch:ch + 1])
                last.then_inc(raw_ready, 1)

            def exps(g, hd):
                r, s = hd % RING, score_banks[hd % 2]
                act.wait_ge(bias_ready, g + 1)
                for tile, c in ((0, slice(0, P)), (1, slice(P, TRI))):
                    last = nc.scalar.activation(probs[:, r, c], s[:, c], ACT.Exp, bias=bias[:, r, tile:tile + 1],
                                                scale=SCALE, accum_out=rsum[:, r, tile:tile + 1])
                last.then_inc(exp_ready, 1)

            def copy_probsT(g, hd):
                act.wait_ge(pt_ready, g + 1)
                act.wait_ge(attn_ready, g + 1)
                nc.scalar.copy(probsT[:, hd % 2], pt_banks[hd % 2][:, 0:TRI]).then_inc(pt_copied, 1)

            def copy_attn(t, pair):
                act.wait_ge(attn_ready, t * HQ + 2 * pair + 4)
                fills = PROLOGUE if pair < HELD else PROLOGUE + F_OUT[(pair - HELD) // 3] + 1
                act.wait_ge(proj_ready, t * FILLS + fills)
                nc.scalar.copy(attn[0][:, pair % HELD], attn_banks[pair % 2][:]).then_inc(high_attn_ready, 1)

            def take_high(i):
                act.wait_ge(split_loaded[i], 16)
                nc.scalar.copy(high[i][:], raw_weights[i][:]).then_inc(high_ready, 1)

            act.wait_ge(weights_loaded, weights_value)
            copy_hT(0, 0)
            take_high(0)
            take_high(1)
            copy_raw(0, 1, 0, w["bk"], 0)
            copy_raw(0, 2, 1, w["bk"], 1)
            copy_raw(0, 3, 2, w["bq"], 0)
            take_high(2)
            copy_raw(0, 4, 3, w["bq"], 1)
            take_high(3)
            with act.Fori(0, STEPS // 2) as i:
                for u in range(2):
                    t = 2 * i + u
                    for s in range(HQ + 5):
                        if 3 <= s < HQ + 3:
                            copy_probsT(t * HQ + s - 3, s - 3)
                        if s >= 6 and s % 2 == 0:
                            copy_attn(t, (s - 6) // 2)
                        if s < HQ:
                            exps(t * HQ + s, s)
                        if s % 2 == 0 and s // 2 < PAIRS - 2:
                            copy_raw(t, PROLOGUE + s // 2, ROPE_PROLOGUE + s // 2, w["bq"], 2 + s // 2)
                        if s == HQ - 4:
                            copy_hT(t, PROLOGUE + F_T)
                        if s == HQ:
                            copy_raw(t, PROLOGUE + F_K, ROPE_PROLOGUE + PAIRS - 2, w["bk"], 0)
                        if s == HQ + 1:
                            copy_raw(t, PROLOGUE + F_K + 1, ROPE_PROLOGUE + PAIRS - 1, w["bk"], 1)
                        if s == HQ + 2:
                            copy_raw(t, PROLOGUE + F_Q, ROPE_PROLOGUE + PAIRS, w["bq"], 0)
                        if s == HQ + 3:
                            copy_raw(t, PROLOGUE + F_Q + 1, ROPE_PROLOGUE + PAIRS + 1, w["bq"], 1)

        @block.vector
        def _(dve):
            chain = Chain(dve, stats_chain, 2 * T - 1)

            def statistics(n, b, before):
                dve.wait_ge(loaded[b], 16 * (before + 1))
                chain.start(n)
                for k in range(T):
                    chain.add(nc.vector.bn_stats(stats[:, k], xin[:, b, k]))
                chain.wait()
                dve.sem_inc(apart, 1)
                for k in range(T - 1):
                    chain.add(nc.vector.bn_aggr(mv[:, k], stats[:, k]))
                nc.vector.bn_aggr(mv[:, T - 1], stats[:, T - 1]).then_inc(var_ready, 1)
                chain.done()

            def normalise(n, b):
                dve.wait_ge(rstd_ready, n + 1)
                for k in range(T):
                    nc.vector.tensor_scalar(hn[:, k], xin[:, b, k], mv[:, k, 0:1], rstd[:, k:k + 1],
                                            ALU.subtract, ALU.mult).then_inc(hn_ready, 1)

            def low_hT(n, loops, f):
                dve.wait_ge(high_hT_ready, n + 1)
                for k in range(KT):
                    last = nc.vector.scalar_tensor_tensor(hT[1][:, k], proj_banks[f % 2][:, k * TOK:(k + 1) * TOK],
                                                          w["ln_weight"][:, k:k + 1], hT[0][:, k], ALU.mult, ALU.subtract)
                last.then_inc(hT_ready, 1)

            def low_attn(t, pair):
                dve.wait_ge(high_attn_ready, t * PAIRS + pair + 1)
                nc.vector.tensor_tensor(attn[1][:, pair % HELD], attn_banks[pair % 2][:], attn[0][:, pair % HELD],
                                        ALU.subtract).then_inc(attn_copied, 1)

            def take_low(i):
                dve.wait_ge(high_ready, i + 1)
                nc.vector.tensor_tensor(low[i][:], raw_weights[i][:], high[i][:], ALU.subtract).then_inc(split_ready, 1)

            def add_part(t, part, before):
                f = PROLOGUE + F_OUT[part]
                dve.wait_ge(proj_ready, t * FILLS + f + 1)
                return nc.vector.tensor_tensor(xout[:], proj_banks[f % 2][:].rearrange("p (j c) -> p j c", j=T),
                                               before, ALU.add)

            def rotated(loops, k):
                dve.wait_ge(raw_ready, loops * ROPES + k + 1)
                rotate(nc.vector, k % 2, 0).then_inc(sin_ready, 1)

            def rope_sum(loops, k, out):
                dve.wait_ge(sin_ready, loops * ROPES + k + 1)
                dve.wait_ge(pool_sin_ready, loops * ROPES + k + 1)
                nc.vector.tensor_tensor(out, by_cos[:, k % 2], by_sin[:, k % 2], ALU.add).then_inc(roped, 1)

            def rope(loops, k, out):
                rotated(loops, k)
                rope_sum(loops, k, out)

            def copy_v(loops, f, j):
                dve.wait_ge(proj_ready, loops * FILLS + f + 1)
                nc.vector.tensor_tensor(v[:, j], proj_banks[f % 2][:], w["bv1"][:], ALU.add).then_inc(v_ready, 1)

            def maximum(g, hd):
                r, s = hd % RING, score_banks[hd % 2]
                dve.wait_ge(scores_ready, g + 1)
                nc.vector.reduce_max(top[:, r, 0:1], s[:, 0:P], AX.X)
                nc.vector.reduce_max(top[:, r, 1:2], s[:, P:TRI], AX.X).then_inc(max_chain, 1)
                dve.wait_ge(max_chain, g + 1)
                nc.vector.tensor_scalar(bias[:, r], top[:, r], -SCALE, None, ALU.mult).then_inc(bias_ready, 1)

            def divide_by_sum(g, hd):
                r = hd % RING
                dve.wait_ge(exp_ready, g + 3)
                nc.vector.reciprocal(rinv[:, r], rsum[:, r]).then_inc(rinv_ready, 1)
                dve.wait_ge(rinv_ready, g + 1)
                for tile, cols in ((0, slice(0, P)), (1, slice(P, TRI))):
                    last = nc.vector.tensor_scalar(probs[:, r, cols], probs[:, r, cols], rinv[:, r, tile:tile + 1], None, ALU.mult)
                last.then_inc(probs_ready, 1)

            dve.wait_ge(weights_loaded, weights_value)
            statistics(0, 0, 0)
            normalise(0, 0)
            low_hT(0, 0, 0)
            take_low(0)
            take_low(1)
            rope(0, 0, kr[:, 0:2])
            rope(0, 1, kr[:, 2:4])
            rope(0, 2, q[:, 0])
            take_low(2)
            rope(0, 3, q[:, 1])
            copy_v(0, 5, 0)
            copy_v(0, 6, 1)
            take_low(3)
            with dve.Fori(0, STEPS // 2) as i:
                for u in range(2):
                    t = 2 * i + u
                    for s in range(HQ + 1):
                        if s < HQ:
                            maximum(t * HQ + s, s)
                        if s >= 1:
                            divide_by_sum(t * HQ + s - 1, s - 1)
                        if s % 2 == 1 and s // 2 < PAIRS - 2:
                            rotated(t, ROPE_PROLOGUE + s // 2)
                        if s % 2 == 0 and 1 <= s // 2 < PAIRS - 1:
                            rope_sum(t, ROPE_PROLOGUE + s // 2 - 1, q[:, (1 + s // 2) % 4])
                        if s == STATS:
                            statistics(t + 1, 1 - u, i + u)
                        if s >= 6 and s % 2 == 0:
                            low_attn(t, (s - 6) // 2)
                        if s == NORM:
                            normalise(t + 1, 1 - u)
                        if s == 12:
                            dve.wait_ge(stored, 16 * t + 16)
                            add_part(t, 0, xin[:, u]).then_inc(part_added, 1)
                        if s == 14:
                            low_hT(t + 1, t, PROLOGUE + F_T)
                    rotated(t, ROPE_PROLOGUE + PAIRS - 2)
                    rotated(t, ROPE_PROLOGUE + PAIRS - 1)
                    rope_sum(t, ROPE_PROLOGUE + PAIRS - 2, kr[:, 0:2])
                    low_attn(t, PAIRS - 2)
                    rope_sum(t, ROPE_PROLOGUE + PAIRS - 1, kr[:, 2:4])
                    rotated(t, ROPE_PROLOGUE + PAIRS)
                    rotated(t, ROPE_PROLOGUE + PAIRS + 1)
                    rope_sum(t, ROPE_PROLOGUE + PAIRS, q[:, 0])
                    dve.wait_ge(part_added, 2 * t + 1)
                    add_part(t, 1, xout[:]).then_inc(part_added, 1)
                    low_attn(t, PAIRS - 1)
                    copy_v(t, PROLOGUE + F_V, 0)
                    rope_sum(t, ROPE_PROLOGUE + PAIRS + 1, q[:, 1])
                    copy_v(t, PROLOGUE + F_V + 1, 1)
                    dve.wait_ge(part_added, 2 * t + 2)
                    add_part(t, 2, xout[:]).then_inc(result_ready, 1)


def program(nc, a, out):
    with ExitStack() as ctx:
        def sb(name, shape, dt=F32):
            return ctx.enter_context(nc.sbuf_tensor(name, shape, dt))

        banks = [ctx.enter_context(nc.psum_tensor(f"bank{i}", [P, BANK], F32)) for i in range(8)]
        between = [nc.dram_tensor(f"x_after_{i}", (P, NT, C), F32, kind="Internal").ap() for i in range(3)]
        H0, H1 = E0 * I0, E1 * I1 + S1
        CH0, CH1 = -(-H0 // P), -(-H1 // P)
        wa = {"wqk": [P, KT, 2 * C], "wv": [P, KT, C], "wo": [P, KT, C], "bq0": [P, KT], "bkz": [P, LA_HEADS],
              "own": [P, P // LA_HD], "bv": [P, C], "bout": [P, C],
              "slopes": [P, LA_HEADS], "distance": [P, 3 * P], "causal": [P, 3 * P]}
        wc = {"wq": [P, KT, HQ * HD], "wk": [P, KT, HKV * HD], "wv1": [P, KT, HKV * HD], "wo1": [P, HQ, C],
              "bq": [P, HQ], "bk": [P, HKV], "bv1": [P, HKV * HD], "ln_weight": [P, KT]}
        ca = {"ident": [P, P], "minus_half": [P, 8]}
        cc = {"cos": [P, 2 * P], "sin": [P, 2 * P]}
        w = {name: sb(name, shape) for name, shape in ca.items()}
        w["ident_bf"] = sb("ident_bf", [P, P], BF16)

        def place_twice(at, name, shape):
            with ExitStack() as place:
                whole = place.enter_context(nc.sbuf_tensor(name, shape, F32))
            return whole, at.enter_context(nc.sbuf_tensor(f"{name}_low", shape, F32R))

        gate, gate_low = place_twice(ctx, "gate", [P, KT, H1])
        up, up_low = place_twice(ctx, "up", [P, KT, H1])
        router, router_low = place_twice(ctx, "router", [P, KT, E0 + E1])
        spread = sb("spread", [3 * E0 + 1, H1], BF16)

        def ffn_weights(hidden, experts, down, down_low):
            return dict(w, gate=gate[:, :, 0:hidden], up=up[:, :, 0:hidden], router=router[:, :, experts],
                        gate_low=gate_low[:, :, 0:hidden], up_low=up_low[:, :, 0:hidden],
                        router_low=router_low[:, :, experts], down=down[:], down_low=down_low[:], spread=spread)

        loads_a = ctx.enter_context(nc.semaphore("weights_a"))
        loads_b = ctx.enter_context(nc.semaphore("weights_b"))
        loads_c = ctx.enter_context(nc.semaphore("weights_c"))
        loads_d = ctx.enter_context(nc.semaphore("weights_d"))
        down_loaded = [ctx.enter_context(nc.semaphore(f"down_{n}_loaded")) for n in range(2)]

        def load_ffn(q, sem, n, h, rows):
            q.dma_start(gate[:, :, 0:h], a[f"gate{n}"]).then_inc(sem, 16)
            q.dma_start(up[:, :, 0:h], a[f"up{n}"]).then_inc(sem, 16)
            q.dma_start(router[:, :, n * E0:n * E0 + (E0, E1)[n]], a[f"router{n}"]).then_inc(sem, 16)
            q.dma_start(spread[0:rows, 0:h], a[f"spread{n}"]).then_inc(sem, 16)

        with ExitStack() as early:
            down, down_low = place_twice(early, "down0", [P, CH0, C])
            with ExitStack() as first:
                split = "wqk", "wv", "wo"
                wl = {name: first.enter_context(nc.sbuf_tensor(name, shape, F32))
                      for name, shape in wa.items() if name not in split}
                low = {}
                for name in split:
                    wl[name], low[f"{name}_low"] = place_twice(first, name, wa[name])
                with nc.Block() as block:
                    @block.sync
                    def _(sp):
                        for name in (*ca, *wa):
                            sp.dma_start((wl | w)[name][:], a[name]).then_inc(loads_a, 16)

                def loads(sp):
                    sp.dma_start(w["ident_bf"][:], a["ident_bf"]).then_inc(loads_b, 16)
                    load_ffn(sp, loads_b, 0, H0, 3 * E0 + 1)
                    sp.dma_start(down[:], a["down0"]).then_inc(down_loaded[0], 16)

                lightning_phase(nc, banks, wl | low | w, loads_a, 16 * len((*ca, *wa)), loads, a["x"], between[0])
            ffn_phase(nc, "f0", banks, ffn_weights(H0, slice(0, E0), down, down_low), loads_b, 16 * 5,
                      down_loaded[0], between[0], between[1], E0, H0, K0)

        with ExitStack() as third:
            split = "wk", "wq", "wv1", "wo1"
            wg = {name: third.enter_context(nc.sbuf_tensor(name, shape, F32))
                  for name, shape in (wc | cc).items() if name not in split}
            wg["masked"] = third.enter_context(nc.sbuf_tensor("masked", [P, P], BF16))
            split_loaded = [third.enter_context(nc.semaphore(f"{name}_loaded")) for name in split]
            whole, low = {}, {}
            for name in split:
                whole[name], low[f"{name}_low"] = place_twice(third, name, wc[name])

            def loads(sp):
                for name, held in wg.items():
                    sp.dma_start(held[:], a[name]).then_inc(loads_c, 16)
                for name, loaded in zip(split, split_loaded):
                    sp.dma_start(whole[name][:], a[name]).then_inc(loaded, 16)
                load_ffn(sp, loads_d, 1, H1, 3 * E1 + 1)

            grouped_phase(nc, banks, w | wg | whole | low, loads_c, 16 * len(wg), split_loaded, loads, between[1], between[2])

        last_down, last_down_low = place_twice(ctx, "down1", [P, CH1, C])

        def load_down(sp):
            sp.dma_start(last_down[:], a["down1"]).then_inc(down_loaded[1], 16)

        ffn_phase(nc, "f1", banks, ffn_weights(H1, slice(E0, E0 + E1), last_down, last_down_low), loads_d, 16 * 4,
                  down_loaded[1], between[2], out, E1, H1, K1, load_down)


def kernel(**inputs):
    import ml_dtypes
    import numpy as np
    import concourse.bacc as bacc
    from concourse.bass_utils import run_bass_kernel_spmd

    x = {k: np.asarray(v) for k, v in inputs.items()}
    f32, bf16 = np.float32, ml_dtypes.bfloat16

    def by_partition(m):
        return m.reshape(m.shape[0] // P, P, -1).transpose(1, 0, 2)

    def to_all(v):
        return np.broadcast_to(v, (P, v.shape[0]))

    def spread(experts, unit, hidden):
        s = np.zeros((3 * experts + 1, hidden), bf16)
        for e in range(experts):
            for part in range(3):
                s[part * experts + e, e * unit:(e + 1) * unit] = 1
        s[3 * experts, experts * unit:] = 1
        return s

    w, b = x["L0_attn_Wqkv"], x["L0_attn_bqkv"]
    a = {"x": x["L0_attn_x"].reshape(NT, P, C).transpose(1, 0, 2)}
    a["wqk"] = by_partition(w[:, 0:2 * C])
    a["bq0"] = b[0:C].reshape(KT, P).T
    bkz = np.zeros((P // LA_HD, LA_HD, LA_HEADS), f32)
    for hd in range(LA_HEADS):
        bkz[hd % (P // LA_HD), :, hd] = b[C + hd * LA_HD:C + (hd + 1) * LA_HD]
    a["bkz"] = bkz.reshape(P, LA_HEADS)
    a["own"] = np.repeat(np.eye(P // LA_HD, dtype=f32), LA_HD, axis=0)
    a["wv"], a["bv"] = by_partition(w[:, 2 * C:]), to_all(b[2 * C:])
    a["wo"], a["bout"] = by_partition(x["L0_attn_Wout"]), to_all(x["L0_attn_bout"])
    a["slopes"] = to_all(x["L0_attn_slopes"])

    gu, down = x["L0_ffn_gate_up_proj"], x["L0_ffn_down_proj"]
    a["gate0"] = by_partition(gu[:, 0:I0].reshape(E0 * I0, C).T)
    a["up0"] = by_partition(gu[:, I0:].reshape(E0 * I0, C).T)
    a["down0"] = by_partition(down.transpose(0, 2, 1).reshape(E0 * I0, C))
    a["router0"] = by_partition(x["L0_ffn_gate_weight"].T)

    a["wq"], a["bq"] = by_partition(x["L1_attn_q_project"].T), x["L1_attn_q_bias"].reshape(HQ, HD).T
    a["wk"], a["bk"] = by_partition(x["L1_attn_k_project"].T), x["L1_attn_k_bias"].reshape(HKV, HD).T
    a["wv1"], a["bv1"] = by_partition(x["L1_attn_v_project"].T), to_all(x["L1_attn_v_bias"])
    a["wo1"] = by_partition(x["L1_attn_o_project"].T)
    a["ln_weight"] = x["L1_attn_ln_weight"].reshape(KT, P).T

    gu, shared = x["L1_ffn_w_gate_up"], x["L1_ffn_shared_gate_up"]
    a["gate1"] = by_partition(np.concatenate([gu[:, :, 0:I1].transpose(1, 0, 2).reshape(C, -1), shared[:, 0:S1]], 1))
    a["up1"] = by_partition(np.concatenate([gu[:, :, I1:].transpose(1, 0, 2).reshape(C, -1), shared[:, S1:]], 1))
    rows = E1 * I1 + S1
    down = np.zeros((-(-rows // P) * P, C), f32)
    down[0:E1 * I1] = x["L1_ffn_w_down"].reshape(-1, C)
    down[E1 * I1:rows] = x["L1_ffn_shared_down"]
    a["down1"] = by_partition(down)
    a["router1"] = by_partition(x["L1_ffn_gate_w"].T)

    key, query = np.arange(P)[:, None], np.arange(2 * P)[None, :]
    distance = np.maximum(query - key, 0).astype(f32)
    causal = (query >= key).astype(f32)
    a["distance"] = np.concatenate([distance, distance[:, 0:P]], 1)
    a["causal"] = np.concatenate([causal, causal[:, 0:P]], 1)
    a["minus_half"] = np.full((P, 8), -0.5, f32)
    a["ident"], a["ident_bf"] = np.eye(P, dtype=f32), np.eye(P, dtype=f32).astype(bf16)
    a["masked"] = np.where(np.arange(P)[:, None] >= np.arange(P)[None, :], 0.0, MASKED).astype(bf16)
    inv_freq = (f32(1.0) / f32(10000.0) ** (np.arange(0, HD, 2, dtype=f32) / f32(HD))).astype(f32)
    angle = (np.arange(2 * P, dtype=f32)[:, None] * inv_freq).astype(f32).T
    a["cos"] = np.concatenate([np.cos(angle), np.cos(angle)], 0)
    a["sin"] = np.concatenate([np.sin(angle), -np.sin(angle)], 0)
    a["spread0"], a["spread1"] = spread(E0, I0, E0 * I0), spread(E1, I1, E1 * I1 + S1)

    nc = bacc.Bacc("TRN2", target_bir_lowering=False, num_devices=1)
    arrays = {f"in_{k}": np.ascontiguousarray(v) for k, v in a.items()}
    aps = {k: nc.dram_tensor(f"in_{k}", v.shape, mybir.dt.from_np(v.dtype), kind="ExternalInput").ap()
           for k, v in ((k, arrays[f"in_{k}"]) for k in a)}
    out = nc.dram_tensor("out_x", (P, NT, C), F32, kind="ExternalOutput").ap()
    program(nc, aps, out)
    r = run_bass_kernel_spmd(nc, [arrays], core_ids=[0])
    y = r.results[0]["out_x"]
    return y.transpose(1, 0, 2).reshape(x["L0_attn_x"].shape)
```
